# Optimizing a Trainium2 kernel written in Bass

```python
import numpy as np
import jax
import jax.numpy as jnp

def _softmax(x, axis=-1):
    return jax.nn.softmax(x, axis=axis)

def _gelu(x):
    return jax.nn.gelu(x, approximate=True)

def _silu(x):
    return jax.nn.silu(x)

def _sigmoid(x):
    return jax.nn.sigmoid(x)

def _layernorm(x, axis=-1, eps=1e-05):
    m = jnp.mean(x, axis=axis, keepdims=True)
    v = jnp.var(x, axis=axis, keepdims=True)
    return (x - m) / jnp.sqrt(v + eps)

def _scatter_add(tgt, idx, src, axis=0):
    return tgt.at[idx].add(src)

def _segment_sum(src, seg, n):
    return jax.ops.segment_sum(src, seg, n)
kernel_name = 'mk_lm_tower_d1_tok_ids2048_r4_417db0'

def setup_inputs(seed: int=0):
    np.random.seed(seed)
    _w = jnp.asarray

    def _rec_inputs():
        import jax
        import jax.numpy as jnp
        _rk = jax.random.key(seed)
        x = jax.random.randint(jax.random.fold_in(_rk, 1), (32, 128), 0, 127999, jnp.int32)
        return x
    x = _rec_inputs()

    def _L0_tok_setup():
        import jax, jax.numpy as jnp
        import numpy as np
        VOCAB = 32000
        DIM = 512
        R = 16
        SCALING = 32.0 / 16.0
        BATCH, SEQ = (4, 2048)
        key = jax.random.key(seed)
        k1, k2, k3, k4 = jax.random.split(key, 4)
        x = jax.random.randint(k1, (BATCH, SEQ), 0, VOCAB, dtype=jnp.int32)
        weight = jax.random.normal(k2, (VOCAB, DIM), dtype=jnp.float32) * 0.02
        lora_A = jax.random.normal(k3, (R, VOCAB), dtype=jnp.float32)
        lora_B = jax.random.normal(k4, (DIM, R), dtype=jnp.float32) * 0.01
        magnitude = jnp.sqrt(jnp.sum(weight * weight, axis=0))
        return {'x': x, 'weight': weight, 'lora_A': lora_A, 'lora_B': lora_B, 'magnitude': magnitude}
    _L0_tok_all = _L0_tok_setup()
    _L0_tok_in = {k: v for k, v in _L0_tok_all.items() if k in ('weight', 'lora_A', 'lora_B', 'magnitude')}
    del _L0_tok_all

    def _L0_attn_setup():
        import jax, jax.numpy as jnp
        import numpy as np
        D_MODEL = 512
        N_HEADS = 16
        D_HEAD = D_MODEL // N_HEADS

        def _act_quant(x):
            scale = 127.0 / jnp.clip(jnp.max(jnp.abs(x), axis=-1, keepdims=True), 1e-05, None)
            q = jnp.clip(jnp.round(x * scale), -128.0, 127.0) / scale
            return x + jax.lax.stop_gradient(q - x)

        def _weight_quant(w):
            scale = 1.0 / jnp.clip(jnp.mean(jnp.abs(w)), 1e-05, None)
            q = jnp.clip(jnp.round(w * scale), -1.0, 1.0) / scale
            return w + jax.lax.stop_gradient(q - w)

        def _bitlinear(x, w):
            return _act_quant(x) @ _weight_quant(w).T
        key = jax.random.key(seed)
        ks = jax.random.split(key, 5)
        B, T = (2, 512)
        x = jax.random.normal(ks[0], (B, T, D_MODEL), dtype=jnp.float32)
        init = 0.02
        w_q = jax.random.normal(ks[1], (D_MODEL, D_MODEL), dtype=jnp.float32) * init
        w_k = jax.random.normal(ks[2], (D_MODEL, D_MODEL), dtype=jnp.float32) * init
        w_v = jax.random.normal(ks[3], (D_MODEL, D_MODEL), dtype=jnp.float32) * init
        w_o = jax.random.normal(ks[4], (D_MODEL, D_MODEL), dtype=jnp.float32) * init
        return {'x': x, 'w_q': w_q, 'w_k': w_k, 'w_v': w_v, 'w_o': w_o}
    _L0_attn_all = _L0_attn_setup()
    _L0_attn_in = {k: v for k, v in _L0_attn_all.items() if k in ('w_q', 'w_k', 'w_v', 'w_o')}
    del _L0_attn_all

    def _L0_ffn_setup():
        import jax, jax.numpy as jnp
        import numpy as np
        D = 512
        F = 352
        E = 8
        K = 2
        FS = 704
        B, S = (2, 256)
        key = jax.random.key(seed)
        ks = jax.random.split(key, 9)
        sc = 0.02
        return {'x': jax.random.normal(ks[0], (B, S, D), dtype=jnp.float32), 'Wr': jax.random.normal(ks[1], (E, D), dtype=jnp.float32) * sc, 'Wg': jax.random.normal(ks[2], (E, F, D), dtype=jnp.float32) * sc, 'Wu': jax.random.normal(ks[3], (E, F, D), dtype=jnp.float32) * sc, 'Wd': jax.random.normal(ks[4], (E, D, F), dtype=jnp.float32) * sc, 'Wsg': jax.random.normal(ks[5], (FS, D), dtype=jnp.float32) * sc, 'Wsu': jax.random.normal(ks[6], (FS, D), dtype=jnp.float32) * sc, 'Wsd': jax.random.normal(ks[7], (D, FS), dtype=jnp.float32) * sc}
    _L0_ffn_all = _L0_ffn_setup()
    _L0_ffn_in = {k: v for k, v in _L0_ffn_all.items() if k in ('Wr', 'Wg', 'Wu', 'Wd', 'Wsg', 'Wsu', 'Wsd')}
    del _L0_ffn_all
    return {'x': x, 'L0_tok_weight': _L0_tok_in['weight'], 'L0_tok_lora_A': _L0_tok_in['lora_A'], 'L0_tok_lora_B': _L0_tok_in['lora_B'], 'L0_tok_magnitude': _L0_tok_in['magnitude'], 'L0_attn_w_q': _L0_attn_in['w_q'], 'L0_attn_w_k': _L0_attn_in['w_k'], 'L0_attn_w_v': _L0_attn_in['w_v'], 'L0_attn_w_o': _L0_attn_in['w_o'], 'L0_ffn_Wr': _L0_ffn_in['Wr'], 'L0_ffn_Wg': _L0_ffn_in['Wg'], 'L0_ffn_Wu': _L0_ffn_in['Wu'], 'L0_ffn_Wd': _L0_ffn_in['Wd'], 'L0_ffn_Wsg': _L0_ffn_in['Wsg'], 'L0_ffn_Wsu': _L0_ffn_in['Wsu'], 'L0_ffn_Wsd': _L0_ffn_in['Wsd']}

def reference(x, L0_tok_weight, L0_tok_lora_A, L0_tok_lora_B, L0_tok_magnitude, L0_attn_w_q, L0_attn_w_k, L0_attn_w_v, L0_attn_w_o, L0_ffn_Wr, L0_ffn_Wg, L0_ffn_Wu, L0_ffn_Wd, L0_ffn_Wsg, L0_ffn_Wsu, L0_ffn_Wsd):
    import jax
    import jax.numpy as jnp

    def _L0_tok_ref(x, weight, lora_A, lora_B, magnitude):
        import jax, jax.numpy as jnp
        import numpy as np
        VOCAB = 32000
        DIM = 512
        R = 16
        SCALING = 32.0 / 16.0
        BATCH, SEQ = (4, 2048)
        base = weight[x]
        emb_A = lora_A.T
        emb_B = lora_B.T
        after_A = emb_A[x]
        result = base + jnp.einsum('bsr,rd->bsd', after_A, emb_B) * SCALING
        direction = weight + emb_A @ emb_B * SCALING
        direction_norm = jax.lax.stop_gradient(jnp.sqrt(jnp.sum(direction * direction, axis=0, keepdims=True)))
        return result * magnitude * direction_norm[0]

    def _L0_attn_ref(x, w_q, w_k, w_v, w_o):
        import jax, jax.numpy as jnp
        import numpy as np
        D_MODEL = 512
        N_HEADS = 16
        D_HEAD = D_MODEL // N_HEADS

        def _act_quant(x):
            scale = 127.0 / jnp.clip(jnp.max(jnp.abs(x), axis=-1, keepdims=True), 1e-05, None)
            q = jnp.clip(jnp.round(x * scale), -128.0, 127.0) / scale
            return x + jax.lax.stop_gradient(q - x)

        def _weight_quant(w):
            scale = 1.0 / jnp.clip(jnp.mean(jnp.abs(w)), 1e-05, None)
            q = jnp.clip(jnp.round(w * scale), -1.0, 1.0) / scale
            return w + jax.lax.stop_gradient(q - w)

        def _bitlinear(x, w):
            return _act_quant(x) @ _weight_quant(w).T
        B, T, C = x.shape
        q = _bitlinear(x, w_q).reshape(B, T, N_HEADS, D_HEAD)
        k = _bitlinear(x, w_k).reshape(B, T, N_HEADS, D_HEAD)
        v = _bitlinear(x, w_v).reshape(B, T, N_HEADS, D_HEAD)
        attn = jnp.einsum('bqhd,bkhd->bhqk', q, k) * D_HEAD ** (-0.5)
        attn = jax.nn.softmax(attn, axis=-1)
        out = jnp.einsum('bhqk,bkhd->bqhd', attn, v).reshape(B, T, C)
        return _bitlinear(out, w_o)

    def _L0_ffn_ref(x, Wr, Wg, Wu, Wd, Wsg, Wsu, Wsd):
        import jax, jax.numpy as jnp
        import numpy as np
        D = 512
        F = 352
        E = 8
        K = 2
        FS = 704
        B, S = (2, 256)
        silu = jax.nn.silu
        sg = silu(jnp.einsum('bsd,fd->bsf', x, Wsg))
        su = jnp.einsum('bsd,fd->bsf', x, Wsu)
        shared_out = jnp.einsum('bsf,df->bsd', sg * su, Wsd)
        logits = jnp.einsum('bsd,ed->bse', x, Wr)
        scores = jax.nn.softmax(logits, axis=-1)
        topk_scores, topk_idx = jax.lax.top_k(scores, K)
        w_full = jnp.sum(jax.nn.one_hot(topk_idx, E, dtype=x.dtype) * topk_scores[..., None], axis=-2)
        g = silu(jnp.einsum('bsd,efd->bsef', x, Wg))
        u = jnp.einsum('bsd,efd->bsef', x, Wu)
        out_e = jnp.einsum('bsef,edf->bsed', g * u, Wd)
        routed_out = jnp.einsum('bsed,bse->bsd', out_e, w_full)
        return routed_out + shared_out
    h = _L0_tok_ref(x, L0_tok_weight, L0_tok_lora_A, L0_tok_lora_B, L0_tok_magnitude)
    h = h + _L0_attn_ref(_layernorm(h, axis=-1), L0_attn_w_q, L0_attn_w_k, L0_attn_w_v, L0_attn_w_o)
    h = h + _L0_ffn_ref(_layernorm(h, axis=-1), L0_ffn_Wr, L0_ffn_Wg, L0_ffn_Wu, L0_ffn_Wd, L0_ffn_Wsg, L0_ffn_Wsu, L0_ffn_Wsd)
    return h

_drawn_inputs = setup_inputs


def setup_inputs(seed=0):
    import zlib

    import numpy as np

    out = dict(_drawn_inputs(seed))
    spreads = {}
    factors = {'L0_tok_magnitude': 8.0,
     'L0_attn_w_q': 8.0,
     'L0_attn_w_k': 8.0,
     'L0_attn_w_v': 4.282,
     'L0_attn_w_o': 4.522,
     'L0_ffn_Wr': 8.0,
     'L0_ffn_Wg': 8.0,
     'L0_ffn_Wu': 8.0,
     'L0_ffn_Wd': 8.0,
     'L0_ffn_Wsg': 5.303,
     'L0_ffn_Wsu': 4.705,
     'L0_ffn_Wsd': 5.053}
    for name, (base, spread) in spreads.items():
        noise = np.random.default_rng([zlib.crc32(name.encode()), seed]).standard_normal(out[name].shape)
        drawn = base * np.exp(spread * noise) if base else spread * noise
        out[name] = jnp.asarray(drawn.astype(out[name].dtype))
    for name, factor in factors.items():
        out[name] = (out[name] * factor).astype(out[name].dtype)
    return out
```

```python
from contextlib import ExitStack

import concourse.bass as bass
from concourse import mybir

F32 = mybir.dt.float32
F32R = mybir.dt.float32r
BF16 = mybir.dt.bfloat16
I32 = mybir.dt.int32
U32 = mybir.dt.uint32
ALU = mybir.AluOpType
ACT = mybir.ActivationFunctionType
X_AXIS = mybir.AxisListType.X

P = 128
SEQS, T = 32, 128
D = 512
KT = D // P
HEADS, DH = 16, 32
GROUPS = P // DH
PER_GROUP = HEADS // GROUPS
VOCAB, RANK = 32000, 16
LORA_SCALE = 2.0
EXPERTS, TOP = 8, 2
LN_EPS = 1e-5
QUANT_MIN = 1e-5
QMAX = 127.0
ROUNDER = 1.5 * 2.0**23

CHUNK = 1000
CHUNKS = VOCAB // CHUNK
HALF = CHUNK // 2
SEQ_GROUP = 4


def after(eng, semaphore, value):
    if not isinstance(value, int) or value > 0:
        eng.wait_ge(semaphore, value)


def row(tile, i):
    return tile[:, bass.ds(i, 1), :].rearrange("p a d -> p (a d)")


def embed(nc, ids, table, table_t, lora_a, lora_a_t, lora_b_t, magnitude_t, attn_ws, H, wT, w_scale, S_bc, ident, ones):
    with ExitStack() as ctx:
        def sb(name, shape, dt=F32):
            return ctx.enter_context(nc.sbuf_tensor(name, shape, dt))

        def ps(name, shape):
            return ctx.enter_context(nc.psum_tensor(name, shape, F32))

        def sem(name):
            return ctx.enter_context(nc.semaphore(name))

        ids_i = sb("ids_i", [P, SEQS], I32)
        ids_f = sb("ids_f", [P, SEQS])
        wrap = sb("wrap", [P, SEQS])
        rows_i = sb("rows_i", [P, SEQS], I32)
        a_rows = sb("a_rows", [P, SEQS, DH])
        a_group = sb("a_group", [P, P])
        a_group_t = sb("a_group_t", [P, P])
        b_rep = sb("b_rep", [P, D])
        b_f = sb("b_f", [96, D])
        b_split = sb("b_split", [96, D], F32R)
        a_f = sb("a_f", [96, 4, CHUNK])
        a_split = [sb(f"a_split{i}", [96, CHUNK], F32R) for i in range(2)]
        W = sb("W", [P, 4, KT, CHUNK])
        part = sb("part", [P, 2, KT])
        total = sb("total", [P, KT])
        root = sb("root", [P, KT])
        half = sb("half", [P, KT])
        mag = sb("mag", [P, KT])
        col_scale = sb("col_scale", [P, KT])
        diag = sb("diag", [P, KT, P])
        w_sum = sb("w_sum", [P, 4])
        w_inv = sb("w_inv", [P, 4])
        norm_ps = [ps(f"norm_ps{i}", [P, 2, 512]) for i in range(2)]
        lora_ps = [ps(f"lora_ps{i}", [P, 512]) for i in range(2)]
        turn_ps = ps("turn_ps", [P, 512])
        misc_ps = ps("misc_ps", [P, 512])

        ids_in, ids_step = sem("ids_in"), sem("ids_step")
        rows_zeroed, operands_zeroed, const_ready, id_zero = sem("rows_zeroed"), sem("operands_zeroed"), sem("const_ready"), sem("id_zero")
        b_in = sem("b_in")
        gathered, rows_ready = sem("gathered"), sem("rows_ready")
        a_in = [sem(f"a_in{i}") for i in range(4)]
        w_in = [sem(f"w_in{i}") for i in range(4)]
        attn_in = sem("attn_in")
        b_hi, b_lo, a_hi, a_lo = sem("b_hi"), sem("b_lo"), sem("a_hi"), sem("a_lo")
        normed, added, squared, part_added, lora_free = sem("normed"), sem("added"), sem("squared"), sem("part_added"), sem("lora_free")
        grouped, group_turned, group_copied, lora_done = sem("grouped"), sem("group_turned"), sem("group_copied"), sem("lora_done")
        w_abs, w_tot, w_scaled, w_step = sem("w_abs"), sem("w_tot"), sem("w_scaled"), sem("w_step")
        rooted, scaled, diagonal, spread, norm_out = sem("rooted"), sem("scaled"), sem("diagonal"), sem("spread"), sem("norm_out")

        block = ctx.enter_context(nc.Block())
        trips = CHUNKS // 4
        w_f = [H[:, SEQS - (4 - n) * KT:SEQS - (3 - n) * KT, :] for n in range(4)]
        table_t_v = table_t.rearrange("(k p) v -> p k v", p=P)

        @block.sync
        def _(sp):
            sp.dma_start(ids_i[:, :], ids).then_inc(ids_in, 16)
            sp.wait_ge(operands_zeroed, 3)
            for r in range(3):
                sp.dma_start(b_f[32 * r:32 * r + RANK, :], lora_b_t).then_inc(b_in, 16)
            for j in range(GROUPS):
                sp.dma_start(b_rep[DH * j:DH * j + RANK, :], lora_b_t).then_inc(b_in, 16)
            sp.dma_start(mag[:, :], magnitude_t).then_inc(b_in, 16)
            sp.sem_inc(squared, 4 * KT)
            sp.sem_inc(a_lo, 4)
            with sp.Fori(0, trips) as g:
                for q in range(4):
                    c = g * 4 + q
                    sp.wait_ge(a_lo, c + 1)
                    for r in range(3):
                        sp.dma_start(a_f[32 * r:32 * r + RANK, q, :], lora_a[:, bass.ds(c * CHUNK, CHUNK)]).then_inc(a_in[q], 16)
                    sp.wait_ge(squared, (c + 1) * KT)
                    sp.dma_start(W[:, q, :, :], table_t_v[:, :, bass.ds(c * CHUNK, CHUNK)]).then_inc(w_in[q], 16)

        @block.gpsimd
        def _(pool):
            pool.memset(ident[:, :], 0.0).then_inc(id_zero, 1)
            pool.memset(ones[:, :], 1.0).then_inc(const_ready, 1)
            pool.memset(a_rows[:, :, :], 0.0).then_inc(rows_zeroed, 1)
            pool.memset(half[:, :], 0.5).then_inc(const_ready, 1)
            pool.wait_ge(id_zero, 1)
            pool.affine_select(out=ident[:, :], in_=ident[:, :], compare_op=ALU.not_equal, fill=1.0, base=0,
                               pattern=[[-1, P]], channel_multiplier=1).then_inc(const_ready, 1)
            pool.wait_ge(ids_step, 5)
            pool.wait_ge(rows_zeroed, 1)
            for i in range(SEQS):
                if i == SEQS - 4 * KT:
                    pool.wait_ge(w_step, 12)
                at = bass.IndirectOffsetOnAxis(ap=rows_i[:, i:i + 1], axis=0)
                pool.indirect_dma_start(out=H[:, i, :], out_offset=None, in_=table, in_offset=at).then_inc(gathered, 16)
                pool.indirect_dma_start(out=a_rows[:, i, 0:RANK], out_offset=None, in_=lora_a_t, in_offset=at).then_inc(gathered, 16)
                if i % SEQ_GROUP == SEQ_GROUP - 1:
                    pool.wait_ge(gathered, 32 * (i + 1))
                    pool.sem_inc(rows_ready, 1)
            pool.wait_ge(part_added, 2 + CHUNKS)
            pool.tensor_tensor(root[:, :], total[:, :], half[:, :], ALU.pow).then_inc(rooted, 1)

        @block.scalar
        def _(act):
            for n in range(4):
                act.dma_start(w_f[n], attn_ws[n].rearrange("(k p) c -> p k c", p=P)).then_inc(attn_in, 16)
            act.sem_inc(added, 2)
            act.wait_ge(attn_in, 16 * 4)
            for n in range(4):
                act.activation(wT[n][:, :, :], w_f[n], ACT.Abs, accum_out=w_sum[:, n:n + 1]).then_inc(w_abs, 1)
            act.wait_ge(b_in, 16 * 8)
            act.activation(b_split[:, :], b_f[:, :], ACT.Copy, scale=LORA_SCALE).then_inc(b_hi, 1)

            def high_part(c, g, q):
                act.wait_ge(a_in[q], (g + 1) * 48)
                act.wait_ge(normed, (c + 1) * KT)
                act.activation(a_split[q % 2][:, :], a_f[:, q, :], ACT.Copy).then_inc(a_hi, 1)

            def squares(c, q):
                for k in range(KT):
                    if k == 0:
                        act.wait_ge(part_added, c + 1)
                    act.wait_ge(added, c * KT + k + 3)
                    act.activation(W[:, q, k, :], W[:, q, k, :], ACT.Square, accum_out=part[:, q % 2, k:k + 1]).then_inc(squared, 1)

            def copy_group(g):
                act.wait_ge(group_turned, g + 1)
                act.activation(a_group_t[:, :], turn_ps[:, 0:P], ACT.Copy).then_inc(group_copied, 1)

            high_part(0, 0, 0)
            with act.Fori(0, trips - 1) as g:
                for q in range(4):
                    high_part(g * 4 + q + 1, g + (q + 1) // 4, (q + 1) % 4)
                    squares(g * 4 + q, q)
                    if q == 2:
                        copy_group(g)
            g = trips - 1
            for q in range(4):
                if q < 3:
                    high_part(g * 4 + q + 1, g, q + 1)
                squares(g * 4 + q, q)
                if q == 2:
                    copy_group(g)

        @block.vector
        def _(dve):
            dve.memset(b_f[:, :], 0.0).then_inc(operands_zeroed, 1)
            dve.memset(b_rep[:, :], 0.0).then_inc(operands_zeroed, 1)
            dve.memset(a_f[:, :, :], 0.0).then_inc(operands_zeroed, 1)
            dve.memset(total[:, :], 0.0).then_inc(const_ready, 1)
            dve.sem_inc(part_added, 2)
            dve.wait_ge(ids_in, 16)
            dve.tensor_copy(ids_f[:, :], ids_i[:, :]).then_inc(ids_step, 1)
            dve.wait_ge(ids_step, 1)
            dve.tensor_scalar(wrap[:, :], ids_f[:, :], 0.0, float(VOCAB), ALU.is_lt, ALU.mult).then_inc(ids_step, 1)
            dve.wait_ge(ids_step, 2)
            dve.tensor_tensor(ids_f[:, :], ids_f[:, :], wrap[:, :], ALU.add).then_inc(ids_step, 1)
            dve.wait_ge(ids_step, 3)
            dve.tensor_scalar(ids_f[:, :], ids_f[:, :], 0.0, float(VOCAB - 1), ALU.max, ALU.min).then_inc(ids_step, 1)
            dve.wait_ge(ids_step, 4)
            dve.tensor_copy(rows_i[:, :], ids_f[:, :]).then_inc(ids_step, 1)
            dve.wait_ge(b_hi, 1)
            dve.scalar_tensor_tensor(out=b_split[32:64, :], in0=b_f[32:64, :], scalar=LORA_SCALE, in1=b_split[32:64, :].bitcast(F32),
                                     op0=ALU.mult, op1=ALU.subtract).then_inc(b_lo, 1)

            def low_part(c, q):
                dve.wait_ge(a_hi, c + 1)
                dve.tensor_tensor(a_split[q % 2][64:96, :], a_f[64:96, q, :], a_split[q % 2][64:96, :].bitcast(F32),
                                  ALU.subtract).then_inc(a_lo, 1)

            def add_products(c, g, q):
                for k in range(KT):
                    if k == 0:
                        dve.wait_ge(w_in[q], (g + 1) * 16)
                    dve.wait_ge(normed, 2 * KT + c * KT + k + 1)
                    w = W[:, q, k, :].rearrange("p (h n) -> p h n", h=2)
                    dve.tensor_tensor(w, w, norm_ps[k % 2][:, :, 0:HALF], ALU.add).then_inc(added, 1)

            def add_part(c, q):
                dve.wait_ge(squared, 4 * KT + (c + 1) * KT)
                dve.wait_ge(part_added, c + 2)
                dve.tensor_tensor(total[:, :], total[:, :], part[:, q % 2, :], ALU.add).then_inc(part_added, 1)

            def add_group(g):
                dve.wait_ge(rows_ready, g + 1)
                dve.tensor_scalar(a_group[:, :].rearrange("p (s r) -> p s r", s=SEQ_GROUP), a_rows[:, bass.ds(g * SEQ_GROUP, SEQ_GROUP), :],
                                  LORA_SCALE, None, ALU.mult).then_inc(grouped, 1)
                for j in range(SEQ_GROUP):
                    i = g * SEQ_GROUP + j
                    dve.wait_ge(lora_done, i + 1)
                    dve.tensor_tensor(row(H, i), row(H, i), lora_ps[j % 2][:, :], ALU.add).then_inc(lora_free, 1)

            dve.wait_ge(const_ready, 4)
            low_part(0, 0)
            dve.wait_ge(w_tot, 1)
            dve.tensor_scalar(w_scale[:, :], misc_ps[:, 0:4], 1.0 / (D * D), QUANT_MIN, ALU.mult, ALU.max).then_inc(w_scaled, 1)
            dve.wait_ge(w_scaled, 1)
            dve.reciprocal(w_inv[:, :], w_scale[:, :]).then_inc(w_scaled, 1)
            dve.wait_ge(w_scaled, 2)
            for n in range(4):
                dve.tensor_scalar(w_f[n], w_f[n], w_inv[:, n:n + 1], ROUNDER, ALU.mult, ALU.add).then_inc(w_step, 1)
            for n in range(4):
                dve.wait_ge(w_step, n + 1)
                dve.tensor_scalar(w_f[n], w_f[n], -ROUNDER, 1.0, ALU.add, ALU.min).then_inc(w_step, 1)
            for n in range(4):
                dve.wait_ge(w_step, 4 + n + 1)
                dve.tensor_scalar(wT[n][:, :, :], w_f[n], -1.0, None, ALU.max).then_inc(w_step, 1)
            with dve.Fori(0, trips - 1) as g:
                for q in range(4):
                    c = g * 4 + q
                    low_part(c + 1, (q + 1) % 4)
                    add_products(c, g, q)
                    if q:
                        add_part(c - 1, q - 1)
                    if q == 2:
                        add_group(g)
                add_part(g * 4 + 3, 3)
            g = trips - 1
            for q in range(4):
                c = g * 4 + q
                if q < 3:
                    low_part(c + 1, q + 1)
                add_products(c, g, q)
                if q:
                    add_part(c - 1, q - 1)
                if q == 2:
                    add_group(g)
            add_part(CHUNKS - 1, 3)
            dve.wait_ge(rooted, 1)
            dve.tensor_tensor(col_scale[:, :], root[:, :], mag[:, :], ALU.mult).then_inc(scaled, 1)
            dve.wait_ge(scaled, 1)
            for k in range(KT):
                dve.tensor_scalar(diag[:, k, :], ident[:, :], col_scale[:, k:k + 1], None, ALU.mult).then_inc(diagonal, 1)
            dve.wait_ge(spread, 1)
            dve.tensor_copy(S_bc[:, :], misc_ps[:, :]).then_inc(norm_out, 1)
            dve.wait_ge(norm_out, 1)

        @block.tensor
        def _(pe):
            pe.sem_inc(normed, 2 * KT)
            pe.sem_inc(lora_free, 2)
            pe.wait_ge(const_ready, 4)
            pe.wait_ge(b_lo, 1)

            def products(c, q):
                pe.wait_ge(a_lo, 4 + c + 1)
                for k in range(KT):
                    pe.wait_ge(added, c * KT + k + 1)
                    for h in range(2):
                        mm = pe.matmul(norm_ps[k % 2][:, h, 0:HALF], b_split[:, k * P:(k + 1) * P],
                                       a_split[q % 2][:, h * HALF:(h + 1) * HALF], start=True, stop=True)
                    mm.then_inc(normed, 1)

            def group_rows(g):
                pe.wait_ge(grouped, g + 1)
                pe.transpose(turn_ps[:, 0:P], a_group[:, :], ident[:, :]).then_inc(group_turned, 1)
                pe.wait_ge(group_copied, g + 1)
                for j in range(SEQ_GROUP):
                    pe.wait_ge(lora_free, g * SEQ_GROUP + j + 1)
                    pe.matmul(lora_ps[j % 2][:, :], a_group_t[DH * j:DH * (j + 1), :], b_rep[DH * j:DH * (j + 1), :],
                              start=True, stop=True).then_inc(lora_done, 1)

            pe.wait_ge(w_abs, 4)
            pe.matmul(misc_ps[:, 0:4], ones[:, :], w_sum[:, :], start=True, stop=True).then_inc(w_tot, 1)
            with pe.Fori(0, trips) as g:
                for q in range(4):
                    products(g * 4 + q, q)
                    if q == 2:
                        group_rows(g)
            for k in range(KT):
                pe.wait_ge(diagonal, k + 1)
                mm = pe.matmul(misc_ps[:, k * P:(k + 1) * P], ones[:, :], diag[:, k, :], start=(k == 0), stop=(k == KT - 1),
                               skip_group_check=True)
            mm.then_inc(spread, 1)


class Live:

    def __init__(self, step, odd, back):
        self.i = step - back
        self.b = (odd + back) % 2
        self.yes = not isinstance(self.i, int) or 0 <= self.i < SEQS
        self.next = self.i + 1


def attend(nc, router_t, x2_dram, H, wT, w_scale, S_bc, ident, ones, gate_values, gate_experts):
    with ExitStack() as ctx:
        def sb(name, shape, dt=F32):
            return ctx.enter_context(nc.sbuf_tensor(name, shape, dt))

        def pair(name, shape, dt=F32):
            return [sb(f"{name}{i}", shape, dt) for i in range(2)]

        def ps(name, shape, dt=F32):
            return ctx.enter_context(nc.psum_tensor(name, shape, dt))

        def sem(name):
            return ctx.enter_context(nc.semaphore(name))

        wr = sb("wr", [P, KT, EXPERTS])
        ident_b = sb("ident_b", [P, P], BF16)
        head_ones = sb("head_ones", [2 * HEADS, GROUPS, PER_GROUP * T], F32R)
        head_ones_f = sb("head_ones_f", [2 * HEADS, GROUPS * PER_GROUP, T])
        eps = sb("eps", [P, 1])
        minus_half = sb("minus_half", [P, 1])
        qk_scale = sb("qk_scale", [P, 1])
        carried = sb("carried", [P, 1])
        carried_b = sb("carried_b", [P, 1])
        stats = sb("stats", [P, 6])
        moments = pair("moments", [P, 2])
        rstd = pair("rstd", [P, 2])
        y = pair("y", [P, D])
        absmax = sb("absmax", [P, 1])
        dequant = pair("dequant", [P, 1])
        quant = pair("quant", [P, 1])
        v_scale = pair("v_scale", [P, 1])
        z = pair("z", [P, D])
        xq = pair("xq", [P, D], BF16)
        xqT = pair("xqT", [P, KT, T], BF16)
        diag = pair("diag_t", [P, P])
        scale_bc = sb("scale_bc", [P, T])
        QT = pair("QT", [P, KT, T])
        KTr = pair("KTr", [P, KT, T])
        VX = pair("VX", [P, HEADS, DH + 1])
        rowmax = sb("rowmax", [P, HEADS])
        negmax = sb("negmax", [P, 2 * HEADS], F32R)
        negmax_t = sb("negmax_t", [2 * HEADS, P], F32R)
        prob = sb("prob", [P, GROUPS, PER_GROUP * T])
        probT = sb("probT", [P, GROUPS, PER_GROUP * T])
        inv_sum = sb("inv_sum", [P, GROUPS, PER_GROUP])
        attn = sb("attn", [P, D])
        absmax2 = sb("absmax2", [P, 1])
        dequant2 = sb("dequant2", [P, 1])
        quant2 = sb("quant2", [P, 1])
        o_scale = sb("o_scale", [P, 1])
        z2 = sb("z2", [P, D])
        aq = sb("aq", [P, D], BF16)
        aqT = sb("aqT", [P, KT, T], BF16)
        stats2 = sb("stats2", [P, 6])
        moments2 = sb("moments2", [P, 2])
        rstd2 = sb("rstd2", [P, 2])
        x2 = pair("x2", [P, D])
        x2T = sb("x2T", [P, KT, T])
        neg_logit = sb("neg_logit", [P, 1])
        e_logit = sb("e_logit", [P, EXPERTS])
        e_sum = sb("e_sum", [P, 1])
        e_inv = sb("e_inv", [P, 1])
        gate = sb("gate", [P, EXPERTS])
        top_v = sb("top_v", [P, 8])
        top_i = sb("top_i", [P, 8], U32)

        S = ps("S", [P, GROUPS, 512])
        bank = [ps(f"bank{i}", [P, 512]) for i in range(4)]

        w_in, const, const_step = sem("wr_in"), sem("const2"), sem("const2_step")
        names = ("rows_scaled stats_done moments_done eps_added rstd_done y_done absmax_done dequant_done quant_done v_scaled z_done xq_done"
                 " diag_done xq_turned xqT_done spread_done scale_bc_done q_done QT_done k_done KT_done v_done V_done"
                 " scores_done max_done neg_hi neg_lo neg_turned neg_t_done shifted exp_done prob_turned even_probT odd_probT heads_done"
                 " inv_done attn_done absmax2_done dequant2_done quant2_done o_scaled z2_done aq_done aq_turned aqT_done projected residual_done"
                 " stats2_done moments2_done eps2_added rstd2_done x2_done x2_turned x2T_done logits_done neg_logit_done e_done e_inv_done"
                 " gate_done top_v_done top_i_done gates_kept").split()
        s = {n: sem(n) for n in names}
        x2_out = [sem(f"x2_out{i}") for i in range(2)]
        (rows_scaled, stats_done, moments_done, eps_added, rstd_done, y_done, absmax_done, dequant_done, quant_done, v_scaled, z_done, xq_done,
         diag_done, xq_turned, xqT_done, spread_done, scale_bc_done, q_done, QT_done, k_done, KT_done, v_done, V_done,
         scores_done, max_done, neg_hi, neg_lo, neg_turned, neg_t_done, shifted, exp_done, prob_turned, even_probT, odd_probT, heads_done,
         inv_done, attn_done, absmax2_done, dequant2_done, quant2_done, o_scaled, z2_done, aq_done, aq_turned, aqT_done, projected, residual_done,
         stats2_done, moments2_done, eps2_added, rstd2_done, x2_done, x2_turned, x2T_done, logits_done, neg_logit_done, e_done, e_inv_done,
         gate_done, top_v_done, top_i_done, gates_kept) = s.values()

        block = ctx.enter_context(nc.Block())

        FIRST, LAST = -1, SEQS + 2
        LOOP_FROM, LOOP_TO = 5, SEQS - 1

        def steps(eng, body):
            def run(k, odd):
                body(Live(k, odd, -1), Live(k, odd, 0), Live(k, odd, 1), Live(k, odd, 2), Live(k, odd, 3))
            for k in range(FIRST, LOOP_FROM):
                run(k, k % 2)
            with eng.Fori(0, (LOOP_TO - LOOP_FROM) // 2) as pair_of_steps:
                for u in range(2):
                    run(pair_of_steps * 2 + (LOOP_FROM + u), (LOOP_FROM + u) % 2)
            for k in range(LOOP_TO, LAST + 1):
                run(k, k % 2)

        @block.sync
        def _(sp):
            sp.dma_start(wr[:, :, :], router_t.rearrange("(k p) e -> p k e", p=P)).then_inc(w_in, 16)

            def body(norm, proj, score, out, route):
                if route.yes:
                    sp.wait_ge(x2_done, route.next)
                    sp.dma_start(x2_dram[bass.ds(route.i * T, T), :], x2[route.b][:, :]).then_inc(x2_out[route.b], 16)

            steps(sp, body)
            for b in range(2):
                sp.wait_ge(x2_out[b], 16 * SEQS // 2)

        @block.gpsimd
        def _(pool):
            pool.memset(eps[:, :], LN_EPS).then_inc(const, 1)
            pool.memset(minus_half[:, :], -0.5).then_inc(const, 1)
            for b in range(2):
                pool.memset(VX[b][:, :, DH:DH + 1], 1.0).then_inc(const, 1)
            pool.memset(head_ones_f[:, :, :], 0.0).then_inc(const_step, 1)
            pool.wait_ge(const_step, 1)
            for n in range(2):
                pool.affine_select(out=head_ones_f[:, :, :], in_=head_ones_f[:, :, :], compare_op=ALU.not_equal, fill=1.0,
                                   base=-n * HEADS, pattern=[[-1, HEADS], [0, T]], channel_multiplier=1).then_inc(const_step, 1)
                pool.wait_ge(const_step, 2 + n)
            pool.tensor_copy(ident_b[:, :], ident[:, :]).then_inc(const, 1)
            pool.tensor_copy(head_ones[:, :, :].rearrange("r a b -> r (a b)"), head_ones_f[:, :, :].rearrange("r a b -> r (a b)")).then_inc(const, 1)
            pool.wait_ge(const, 6)

            def body(norm, proj, score, out, route):
                if route.yes:
                    pool.wait_ge(moments2_done, route.next)
                    pool.tensor_tensor(rstd2[:, 0:1], moments2[:, 1:2], eps[:, :], ALU.add).then_inc(eps2_added, 1)
                    pool.wait_ge(eps2_added, route.next)
                    after(pool, x2_done, route.i)
                    pool.tensor_tensor(rstd2[:, 1:2], rstd2[:, 0:1], minus_half[:, :], ALU.pow).then_inc(rstd2_done, 1)
                if norm.yes:
                    pool.wait_ge(moments_done, norm.next)
                    after(pool, y_done, norm.i)
                    pool.tensor_tensor(rstd[norm.b][:, 0:1], moments[norm.b][:, 1:2], eps[:, :], ALU.add).then_inc(eps_added, 1)
                    pool.wait_ge(eps_added, norm.next)
                    pool.tensor_tensor(rstd[norm.b][:, 1:2], rstd[norm.b][:, 0:1], minus_half[:, :], ALU.pow).then_inc(rstd_done, 1)
                    pool.wait_ge(dequant_done, norm.next)
                    after(pool, spread_done, norm.i - 1)
                    pool.tensor_tensor(diag[norm.b][:, :], ident[:, :], dequant[norm.b][:, 0:1].to_broadcast([P, P]), ALU.mult).then_inc(diag_done, 1)

            steps(pool, body)

        @block.scalar
        def _(act):
            def body(norm, proj, score, out, route):
                if out.yes:
                    act.wait_ge(quant2_done, out.next)
                    after(act, aq_done, out.i)
                    act.activation(z2[:, :], attn[:, :], ACT.Copy, bias=ROUNDER, scale=quant2[:, 0:1]).then_inc(z2_done, 1)
                if proj.yes:
                    act.wait_ge(xq_turned, proj.next)
                    after(act, v_done, proj.i - 1)
                    act.activation(xqT[proj.b][:, :, :], bank[0].bitcast(BF16)[:, 0:D].rearrange("p (k t) -> p k t", k=KT), ACT.Copy).then_inc(xqT_done, 1)
                    act.wait_ge(spread_done, proj.next)
                    after(act, KT_done, proj.i)
                    act.activation(scale_bc[:, :], bank[3][:, 0:T], ACT.Copy).then_inc(scale_bc_done, 1)
                if route.yes:
                    act.wait_ge(x2_turned, route.next)
                    after(act, logits_done, route.i)
                    act.activation(x2T[:, :, :], bank[1][:, :].rearrange("p (k t) -> p k t", k=KT), ACT.Copy).then_inc(x2T_done, 1)
                if score.yes:
                    act.wait_ge(neg_turned, score.next)
                    after(act, shifted, score.i * GROUPS)
                    act.activation(negmax_t[:, :], bank[1][0:2 * HEADS, 0:P], ACT.Copy).then_inc(neg_t_done, 1)
                if proj.yes:
                    act.wait_ge(v_done, proj.next)
                    act.wait_ge(v_scaled, proj.next)
                    after(act, heads_done, (proj.i - 1) * GROUPS)
                    act.activation(VX[proj.b][:, :, 0:DH], bank[3][:, :].rearrange("p (h d) -> p h d", h=HEADS), ACT.Copy,
                                   scale=v_scale[proj.b][:, 0:1]).then_inc(V_done, 1)
                if out.yes:
                    act.wait_ge(aq_turned, out.next)
                    after(act, projected, out.i)
                    act.activation(aqT[:, :, :], bank[2].bitcast(BF16)[:, 0:D].rearrange("p (k t) -> p k t", k=KT), ACT.Copy).then_inc(aqT_done, 1)
                if score.yes:
                    for n in range(2):
                        act.wait_ge(shifted, score.i * GROUPS + 2 * n + 2)
                        after(act, prob_turned, score.i * GROUPS)
                        act.activation(prob[:, 2 * n:2 * n + 2, :], S[:, 2 * n:2 * n + 2, :], ACT.Exp).then_inc(exp_done, 1)
                if route.yes:
                    act.wait_ge(neg_logit_done, route.next)
                    after(act, gate_done, route.i)
                    act.activation(e_logit[:, :], bank[3][:, 0:EXPERTS], ACT.Exp, bias=neg_logit[:, 0:1], accum_out=e_sum[:, 0:1]).then_inc(e_done, 1)
                if score.yes:
                    for j in (0, 2):
                        act.wait_ge(prob_turned, score.i * GROUPS + j + 1)
                        after(act, heads_done, score.i * GROUPS)
                        act.activation(probT[:, j, :], bank[(0, 2, 0, 1)[j]][:, :], ACT.Copy).then_inc(even_probT, 1)
                if norm.yes:
                    act.wait_ge(quant_done, norm.next)
                    after(act, xq_done, norm.i - 1)
                    act.activation(z[norm.b][:, :], y[norm.b][:, :], ACT.Copy, bias=ROUNDER, scale=quant[norm.b][:, 0:1]).then_inc(z_done, 1)

            steps(act, body)

        @block.vector
        def _(dve):
            dve.tensor_scalar(qk_scale[:, :], w_scale[:, 0:1], w_scale[:, 1:2], DH**-0.5, ALU.mult, ALU.mult).then_inc(const, 1)
            dve.memset(carried_b[:, :], 0.0).then_inc(const, 1)
            dve.wait_ge(const, 8)

            def carry(semaphore, value):
                dve.wait_ge(semaphore, value)
                dve.tensor_copy(carried[:, :], carried_b[:, :])

            def body(norm, proj, score, out, route):
                if out.yes:
                    dve.wait_ge(heads_done, out.next * GROUPS)
                    dve.reciprocal(inv_sum[:, :, :], S[:, :, 0:PER_GROUP * (DH + 1)].rearrange("p j (m d) -> p j m d", m=PER_GROUP)[:, :, :, DH]).then_inc(inv_done, 1)
                    dve.wait_ge(inv_done, out.next)
                    after(dve, z2_done, out.i)
                    heads = attn[:, :].rearrange("p (m j d) -> p j m d", m=PER_GROUP, j=GROUPS)
                    found = S[:, :, 0:PER_GROUP * (DH + 1)].rearrange("p j (m d) -> p j m d", m=PER_GROUP)[:, :, :, 0:DH]
                    for j in range(GROUPS):
                        dve.tensor_tensor(heads[:, j], found[:, j], inv_sum[:, j, :].unsqueeze(2).to_broadcast([P, PER_GROUP, DH]), ALU.mult).then_inc(attn_done, 1)
                if route.yes:
                    carry(residual_done, route.next)
                    dve.bn_stats(stats2[:, :], row(H, route.i)).then_inc(stats2_done, 1)
                if out.yes:
                    dve.wait_ge(attn_done, out.next * GROUPS)
                    dve.tensor_reduce(absmax2[:, :], attn[:, :], X_AXIS, ALU.max, apply_absolute_value=True).then_inc(absmax2_done, 1)
                if route.yes:
                    carry(stats2_done, route.next)
                    dve.bn_aggr(moments2[:, :], stats2[:, :]).then_inc(moments2_done, 1)
                if out.yes:
                    dve.wait_ge(absmax2_done, out.next)
                    dve.tensor_scalar(dequant2[:, :], absmax2[:, :], QUANT_MIN, 1.0 / QMAX, ALU.max, ALU.mult).then_inc(dequant2_done, 1)
                    dve.wait_ge(dequant2_done, out.next)
                    dve.reciprocal(quant2[:, :], dequant2[:, :]).then_inc(quant2_done, 1)
                    after(dve, residual_done, out.i)
                    dve.tensor_scalar(o_scale[:, :], dequant2[:, :], w_scale[:, 3:4], None, ALU.mult).then_inc(o_scaled, 1)
                if score.yes:
                    for j in range(GROUPS):
                        dve.wait_ge(scores_done, score.i * GROUPS + j + 1)
                        dve.tensor_reduce(rowmax[:, j * PER_GROUP:(j + 1) * PER_GROUP], S[:, j, :].rearrange("p (m t) -> p m t", m=PER_GROUP),
                                          X_AXIS, ALU.max).then_inc(max_done, 1)
                        if j == 1 and route.yes:
                            dve.wait_ge(rstd2_done, route.next)
                            if route.yes:
                                after(dve, x2_out[route.b], (route.i // 2) * 16 if isinstance(route.i, int) else (route.i - route.b) * 8)
                            dve.tensor_scalar(x2[route.b][:, :], row(H, route.i), moments2[:, 0:1], rstd2[:, 1:2], ALU.subtract, ALU.mult).then_inc(x2_done, 1)
                    dve.wait_ge(max_done, score.next * GROUPS)
                    dve.tensor_scalar(negmax[:, 0:HEADS], rowmax[:, :], -1.0, None, ALU.mult).then_inc(neg_hi, 1)
                    dve.wait_ge(neg_hi, score.next)
                    dve.scalar_tensor_tensor(out=negmax[:, HEADS:2 * HEADS], in0=rowmax[:, :], scalar=-1.0, in1=negmax[:, 0:HEADS].bitcast(F32),
                                             op0=ALU.mult, op1=ALU.subtract).then_inc(neg_lo, 1)
                elif route.yes:
                    dve.wait_ge(rstd2_done, route.next)
                    after(dve, x2_out[route.b], (route.i // 2) * 16)
                    dve.tensor_scalar(x2[route.b][:, :], row(H, route.i), moments2[:, 0:1], rstd2[:, 1:2], ALU.subtract, ALU.mult).then_inc(x2_done, 1)
                if out.yes:
                    dve.wait_ge(z2_done, out.next)
                    dve.tensor_scalar(aq[:, :], z2[:, :], -ROUNDER, None, ALU.add).then_inc(aq_done, 1)
                if proj.yes:
                    bc = scale_bc[:, :].unsqueeze(1).to_broadcast([P, KT, T])
                    dve.wait_ge(scale_bc_done, proj.next)
                    dve.wait_ge(q_done, proj.next)
                    dve.scalar_tensor_tensor(out=QT[proj.b][:, :, :], in0=bank[2][:, :].rearrange("p (k t) -> p k t", k=KT), scalar=qk_scale[:, 0:1],
                                             in1=bc, op0=ALU.mult, op1=ALU.mult).then_inc(QT_done, 1)
                    dve.wait_ge(k_done, proj.next)
                    dve.tensor_tensor(KTr[proj.b][:, :, :], bank[0][:, :].rearrange("p (k t) -> p k t", k=KT), bc, ALU.mult).then_inc(KT_done, 1)
                if norm.yes:
                    dve.tensor_tensor(row(H, norm.i), row(H, norm.i), S_bc[:, :], ALU.mult).then_inc(rows_scaled, 1)
                    carry(rows_scaled, norm.next)
                    dve.bn_stats(stats[:, :], row(H, norm.i)).then_inc(stats_done, 1)
                    carry(stats_done, norm.next)
                    dve.bn_aggr(moments[norm.b][:, :], stats[:, :]).then_inc(moments_done, 1)
                if route.yes:
                    dve.wait_ge(logits_done, route.next)
                    dve.tensor_reduce(neg_logit[:, :], bank[3][:, 0:EXPERTS], X_AXIS, ALU.max, negate=True).then_inc(neg_logit_done, 1)
                if norm.yes:
                    dve.wait_ge(rstd_done, norm.next)
                    after(dve, z_done, norm.i - 1)
                    dve.tensor_scalar(y[norm.b][:, :], row(H, norm.i), moments[norm.b][:, 0:1], rstd[norm.b][:, 1:2], ALU.subtract, ALU.mult).then_inc(y_done, 1)
                    dve.wait_ge(y_done, norm.next)
                    dve.tensor_reduce(absmax[:, :], y[norm.b][:, :], X_AXIS, ALU.max, apply_absolute_value=True).then_inc(absmax_done, 1)
                if score.yes:
                    dve.wait_ge(prob_turned, score.i * GROUPS + 2)
                    dve.tensor_copy(probT[:, 1, :], bank[2][:, :]).then_inc(odd_probT, 1)
                if norm.yes:
                    dve.wait_ge(absmax_done, norm.next)
                    after(dve, diag_done, norm.i - 1)
                    dve.tensor_scalar(dequant[norm.b][:, :], absmax[:, :], QUANT_MIN, 1.0 / QMAX, ALU.max, ALU.mult).then_inc(dequant_done, 1)
                    dve.wait_ge(dequant_done, norm.next)
                    dve.reciprocal(quant[norm.b][:, :], dequant[norm.b][:, :]).then_inc(quant_done, 1)
                    after(dve, V_done, norm.i - 1)
                    dve.tensor_scalar(v_scale[norm.b][:, :], dequant[norm.b][:, :], w_scale[:, 2:3], None, ALU.mult).then_inc(v_scaled, 1)
                if out.yes:
                    dve.wait_ge(projected, out.next)
                    dve.scalar_tensor_tensor(out=row(H, out.i), in0=bank[1][:, :], scalar=o_scale[:, 0:1], in1=row(H, out.i),
                                             op0=ALU.mult, op1=ALU.add).then_inc(residual_done, 1)
                if score.yes:
                    dve.wait_ge(prob_turned, score.i * GROUPS + 4)
                    dve.tensor_copy(probT[:, 3, :], bank[1][:, :]).then_inc(odd_probT, 1)
                if route.yes:
                    dve.wait_ge(e_done, route.next)
                    dve.reciprocal(e_inv[:, :], e_sum[:, :]).then_inc(e_inv_done, 1)
                    dve.wait_ge(e_inv_done, route.next)
                    dve.tensor_scalar(gate[:, :], e_logit[:, :], e_inv[:, 0:1], None, ALU.mult).then_inc(gate_done, 1)
                    carry(gate_done, route.next)
                    dve.max(top_v[:, :], gate[:, :]).then_inc(top_v_done, 1)
                    carry(top_v_done, route.next)
                    dve.max_index(top_i[:, :], top_v[:, :], gate[:, :]).then_inc(top_i_done, 1)
                if norm.yes:
                    dve.wait_ge(z_done, norm.next)
                    after(dve, xq_turned, norm.i - 1)
                    dve.tensor_scalar(xq[norm.b][:, :], z[norm.b][:, :], -ROUNDER, None, ALU.add).then_inc(xq_done, 1)
                if route.yes:
                    dve.tensor_scalar(row(gate_values, route.i), top_v[:, 0:TOP], 1.0, None, ALU.mult).then_inc(gates_kept, 1)
                    dve.wait_ge(top_i_done, route.next)
                    dve.tensor_scalar(row(gate_experts, route.i), top_i[:, 0:TOP], 1.0, None, ALU.mult).then_inc(gates_kept, 1)

            steps(dve, body)
            dve.wait_ge(gates_kept, 2 * SEQS)

        @block.tensor
        def _(pe):
            pe.wait_ge(const, 8)
            pe.wait_ge(w_in, 16)
            T1, X2T_BANK, Q_BANK, V_BANK = 0, 1, 2, 3

            def turn(to, tile, identity):
                for k in range(KT):
                    mm = pe.transpose(to[:, k * T:(k + 1) * T], tile[:, k * P:(k + 1) * P], identity[:, :])
                return mm

            def body(norm, proj, score, out, route):
                if score.yes:
                    pe.wait_ge(QT_done, score.next)
                    pe.wait_ge(KT_done, score.next)
                    after(pe, attn_done, score.i * GROUPS)
                    for j in range(GROUPS):
                        for m in range(PER_GROUP):
                            mm = pe.matmul(S[:, j, m * T:(m + 1) * T], QT[score.b][DH * j:DH * (j + 1), m, :], KTr[score.b][DH * j:DH * (j + 1), m, :],
                                           start=(m == 0), stop=(m == PER_GROUP - 1), skip_group_check=True)
                        mm.then_inc(scores_done, 1)
                if proj.yes:
                    pe.wait_ge(xq_done, proj.next)
                    if score.yes and out.yes:
                        pe.wait_ge(even_probT, proj.i * 2 - 2)
                    else:
                        after(pe, KT_done, proj.i)
                    turn(bank[0].bitcast(BF16), xq[proj.b], ident_b).then_inc(xq_turned, 1)
                    pe.wait_ge(diag_done, proj.next)
                    if route.yes and not (isinstance(route.i, int) and route.i < 1):
                        pe.wait_ge(e_done, route.i)
                    else:
                        after(pe, V_done, proj.i)
                    pe.matmul(bank[3][:, 0:T], ones[:, :], diag[proj.b][:, :], start=True, stop=True).then_inc(spread_done, 1)
                if route.yes:
                    pe.wait_ge(x2_done, route.next)
                    turn(bank[1], x2[route.b], ident).then_inc(x2_turned, 1)
                if proj.yes:
                    pe.wait_ge(xqT_done, proj.next)
                    if not out.yes:
                        after(pe, QT_done, proj.i)
                    for which, to, done in ((0, 2, q_done), (1, 0, k_done)):
                        for m in range(KT):
                            for k in range(KT):
                                mm = pe.matmul(bank[to][:, m * T:(m + 1) * T], wT[which][:, k, m * P:(m + 1) * P], xqT[proj.b][:, k, :],
                                               start=(k == 0), stop=(k == KT - 1))
                        mm.then_inc(done, 1)
                if score.yes:
                    pe.wait_ge(neg_lo, score.next)
                    if route.yes:
                        pe.wait_ge(x2T_done, route.next)
                    pe.transpose(bank[1][0:2 * HEADS, 0:P], negmax[:, :].bitcast(F32), ident[:, :]).then_inc(neg_turned, 1)
                if proj.yes:
                    pe.wait_ge(scale_bc_done, proj.next)
                    for k in range(KT):
                        mm = pe.matmul(bank[3][:, :], xqT[proj.b][:, k, :], wT[2][:, k, :], start=(k == 0), stop=(k == KT - 1))
                    mm.then_inc(v_done, 1)
                if out.yes:
                    pe.wait_ge(aq_done, out.next)
                    if proj.yes:
                        pe.wait_ge(QT_done, proj.next)
                    turn(bank[2].bitcast(BF16), aq, ident_b).then_inc(aq_turned, 1)
                if route.yes:
                    pe.wait_ge(x2T_done, route.next)
                    if proj.yes:
                        pe.wait_ge(V_done, proj.next)
                    else:
                        after(pe, e_done, route.i)
                    for k in range(KT):
                        mm = pe.matmul(bank[3][:, 0:EXPERTS], x2T[:, k, :], wr[:, k, :], start=(k == 0), stop=(k == KT - 1))
                    mm.then_inc(logits_done, 1)
                if score.yes:
                    pe.wait_ge(neg_t_done, score.next)
                    for j in range(GROUPS):
                        pe.matmul(S[:, j, :], negmax_t[:, :], head_ones[:, j, :], start=False, stop=True, skip_group_check=True).then_inc(shifted, 1)

                def turn_probs(j):
                    to = bank[(0, 2, 0, 1)[j]]
                    for m in range(PER_GROUP):
                        mm = pe.transpose(to[:, m * T:(m + 1) * T], prob[:, j, m * T:(m + 1) * T], ident[:, :])
                    mm.then_inc(prob_turned, 1)

                def heads(j):
                    copied, n = ((even_probT, j // 2), (odd_probT, j // 2))[j % 2]
                    pe.wait_ge(copied, score.i * 2 + n + 1)
                    for m in range(PER_GROUP):
                        mm = pe.matmul(S[:, j, m * (DH + 1):(m + 1) * (DH + 1)], probT[:, j, m * T:(m + 1) * T],
                                       VX[score.b][:, m * GROUPS + j, :], start=True, stop=True)
                    mm.then_inc(heads_done, 1)

                if score.yes:
                    pe.wait_ge(exp_done, score.i * 2 + 1)
                    if proj.yes:
                        pe.wait_ge(KT_done, proj.next)
                    turn_probs(0)
                if out.yes:
                    pe.wait_ge(aqT_done, out.next)
                    if score.yes:
                        pe.wait_ge(neg_t_done, score.next)
                    for k in range(KT):
                        mm = pe.matmul(bank[1][:, :], aqT[:, k, :], wT[3][:, k, :], start=(k == 0), stop=(k == KT - 1))
                    mm.then_inc(projected, 1)
                if score.yes:
                    if not out.yes and proj.yes:
                        pe.wait_ge(QT_done, proj.next)
                    turn_probs(1)
                    pe.wait_ge(V_done, score.next)
                    heads(0)
                    pe.wait_ge(exp_done, score.i * 2 + 2)
                    turn_probs(2)
                    heads(1)
                    if out.yes:
                        pe.wait_ge(residual_done, out.next)
                    turn_probs(3)
                    heads(2)
                    heads(3)

            steps(pe, body)


ROUTED_F = 352
F_TILES = ((0, 128), (128, 128), (256, 96))
UP_COLS = KT * 2 * ROUTED_F
DOWN_COLS = len(F_TILES) * D
PACKED = UP_COLS + DOWN_COLS
PIECES = ((0, UP_COLS // 2), (UP_COLS // 2, UP_COLS), (UP_COLS, PACKED))
BLOCK = 2 * P
TOKENS = SEQS * T
SHARED_BLOCKS = TOKENS // BLOCK
ROUTED_BLOCKS = TOP * TOKENS // BLOCK + EXPERTS - 1
SLOT_TILES = ROUTED_BLOCKS * BLOCK // P


def experts(nc, packed, x2_dram, slot_token, y_dram, out, H, ident, ones, gate_values, gate_experts):
    with ExitStack() as ctx:
        def sb(name, shape, dt=F32):
            return ctx.enter_context(nc.sbuf_tensor(name, shape, dt))

        def ps(name, shape, dt=F32):
            return ctx.enter_context(nc.psum_tensor(name, shape, dt))

        def sem(name):
            return ctx.enter_context(nc.semaphore(name))

        w_stage = sb("w_stage", [P, PACKED])
        w_hi = [sb(f"w_hi{i}", [P, PACKED], F32R) for i in range(2)]
        w_lo = [sb(f"w_lo{i}", [P, PACKED], F32R) for i in range(2)]
        xr = [sb(f"xr{i}", [P, 2, D]) for i in range(2)]
        xT_hi = [sb(f"xT_hi{i}", [P, KT, BLOCK], F32R) for i in range(2)]
        xT_lo = [sb(f"xT_lo{i}", [P, KT, BLOCK], F32R) for i in range(2)]
        act_g = sb("act_g", [P, 3, BLOCK])
        h = sb("h", [P, 3, BLOCK])
        h_hi = [sb(f"h_hi{i}", [P, 3, BLOCK], F32R) for i in range(2)]
        h_lo = [sb(f"h_lo{i}", [P, 3, BLOCK], F32R) for i in range(2)]
        y = sb("y_rows", [P, 2, D])
        comb = [sb(f"comb{i}", [P, TOP, D]) for i in range(2)]
        slot_i = sb("slot_i", [P, TOP * SEQS], I32)
        table_i = sb("table_i", [P, TOP * SEQS], I32)
        token_i = sb("token_i", [P, SEQS], I32)
        slot_tokens = sb("slot_tokens", [P, SLOT_TILES], I32)
        block_expert = sb("block_expert", [P, ROUTED_BLOCKS], I32)

        def early(tile, start, a, b, dt=F32):
            v = tile[:, :] if len(tile.shape) == 2 else tile[:, :, :].rearrange("p a b -> p (a b)")
            v = v[:, start:start + a * b]
            return (v if dt == F32 else v.bitcast(dt)).rearrange("p (a b) -> p a b", a=a)

        E, SE = EXPERTS, EXPERTS * SEQS
        expert_no = early(comb[0], 0, E, SEQS)
        hot = [early(comb[0], SE, E, SEQS), early(comb[0], 2 * SE, E, SEQS)]
        chosen = early(comb[0], 3 * SE, E, SEQS)
        before = early(comb[1], 0, E, SEQS)
        in_seq = early(comb[1], SE, E, SEQS)
        upto = early(comb[1], 2 * SE, E, SEQS)
        zeros = early(comb[1], 3 * SE, E, SEQS)
        block_no = early(y, 0, ROUTED_BLOCKS, E)
        slot_f = early(y, 512, 1, TOP * SEQS)
        tile_f = early(y, 576, 1, TOP * SEQS)
        block_f = early(y, 640, 1, ROUTED_BLOCKS)
        count = early(y, 700, 1, E)
        count_i = early(y, 708, 1, E, I32)
        blocks = early(y, 716, 1, E)
        ends = early(y, 724, 1, E)
        starts = early(y, 732, 1, E)
        tile_i = early(y, 768, 1, TOP * SEQS, I32)
        nothing = early(y, 896, 1, SLOT_TILES, I32)
        below = sb("below", [P, P])

        xT_ps = ps("xT_ps", [P, KT, BLOCK])
        up_ps = [ps(f"up_ps{j}", [P, 512]) for j in range(3)]
        down_ps = [ps(f"down_ps{j}", [P, 512]) for j in range(2)]
        route_ps = ps("route_ps", [P, 512])

        made, masked, plan, counted, blocks_known = sem("made"), sem("masked"), sem("plan"), sem("counted"), sem("blocks_known")
        table_zeroed, scattered, table_in = sem("table_zeroed"), sem("scattered"), sem("table_in")
        stage_in = [sem(f"stage_in{i}") for i in range(3)]
        w_hi_done = [sem(f"w_hi_done{i}") for i in range(3)]
        w_lo_done = [sem(f"w_lo_done{i}") for i in range(3)]
        rows_in = [sem(f"rows_in{i}") for i in range(2)]
        rows_gathered = [sem(f"rows_gathered{i}") for i in range(2)]
        x_turned, xT_hi_done, xT_lo_done = sem("x_turned"), sem("xT_hi_done"), sem("xT_lo_done")
        up_done, silu_done, h_done, h_hi_done, h_lo_done = sem("up_done"), sem("silu_done"), sem("h_done"), sem("h_hi_done"), sem("h_lo_done")
        down_done, y_taken, y_stored = sem("down_done"), sem("y_taken"), sem("y_stored")
        comb_in = [sem(f"comb_in{i}") for i in range(2)]
        combined, out_stored = sem("combined"), sem("out_stored")

        block = ctx.enter_context(nc.Block())

        B_FROM = SHARED_BLOCKS
        C_FROM = B_FROM + ROUTED_BLOCKS
        N = C_FROM + SHARED_BLOCKS
        LAST_W = ROUTED_BLOCKS + 1
        assert (C_FROM - B_FROM) % 2 == 1 and B_FROM % 2 == 0

        def w_of(n, kind):
            return 0 if kind == "A" else LAST_W if kind == "C" else n - (B_FROM - 1)

        def w_buffer(odd, kind):
            return (odd + 1) % 2 if kind == "B" else 0

        def each_block(eng, body):
            body(0, 0, "A", None, "A")
            with eng.Fori(0, (B_FROM - 2) // 2) as m:
                for u in range(2):
                    body(m * 2 + (1 + u), (1 + u) % 2, "A", "A", "A")
            body(B_FROM - 1, 1, "A", "A", "B")
            body(B_FROM, 0, "B", "A", "B")
            with eng.Fori(0, (ROUTED_BLOCKS - 3) // 2) as m:
                for u in range(2):
                    body(m * 2 + (B_FROM + 1 + u), (1 + u) % 2, "B", "B", "B")
            body(C_FROM - 2, 1, "B", "B", "B")
            body(C_FROM - 1, 0, "B", "B", "C")
            body(C_FROM, 1, "C", "B", "C")
            with eng.Fori(0, (SHARED_BLOCKS - 2) // 2) as m:
                for u in range(2):
                    body(m * 2 + (C_FROM + 1 + u), u % 2, "C", "C", "C")
            body(N - 1, 0, "C", "C", None)

        @block.sync
        def _(sp):
            def load_weights(w, expert):
                for piece, (a, b) in enumerate(PIECES):
                    after(sp, w_lo_done[piece], w)
                    sp.dma_start(w_stage[:, a:b], packed[bass.ds(expert, 1), :, a:b].rearrange("e p c -> (e p) c")).then_inc(stage_in[piece], 16)

            def load_rows(n, odd, first):
                after(sp, x_turned, n - 1)
                for r in range(2):
                    sp.dma_start(xr[odd][:, r, :], x2_dram[bass.ds((n - first) * BLOCK + r * P, P), :]).then_inc(rows_in[odd], 16)

            def block_weights(r):
                load_weights(r + 1, sp.value_load(block_expert[0:1, bass.ds(r, 1)], min_val=0, max_val=EXPERTS - 1))

            def store_rows(r):
                sp.wait_ge(y_taken, (r + B_FROM + 1) * 2)
                sp.dma_start(y_dram[bass.ds(r * BLOCK, BLOCK), :].rearrange("(a p) d -> p a d", p=P), y[:, :, :]).then_inc(y_stored, 16)

            load_rows(0, 0, 0)
            load_weights(0, EXPERTS)
            load_rows(1, 1, 0)
            sp.wait_ge(made, 5)
            sp.dma_start(slot_token.rearrange("(p c) x -> p (c x)", p=P), nothing[:, 0, :]).then_inc(table_zeroed, 16)
            sp.wait_ge(blocks_known, 1)
            block_weights(0)
            with sp.Fori(0, (SHARED_BLOCKS - 2) // 2) as m:
                for u in range(2):
                    load_rows(m * 2 + (2 + u), u, 0)
            for r in range(1, 3):
                block_weights(r)
            with sp.Fori(0, ROUTED_BLOCKS - 3) as r:
                block_weights(r + 3)
                store_rows(r)
            load_rows(C_FROM, C_FROM % 2, C_FROM)
            load_weights(LAST_W, EXPERTS + 1)
            store_rows(ROUTED_BLOCKS - 3)
            load_rows(C_FROM + 1, 1 - C_FROM % 2, C_FROM)
            store_rows(ROUTED_BLOCKS - 2)
            store_rows(ROUTED_BLOCKS - 1)
            with sp.Fori(0, (SHARED_BLOCKS - 2) // 2) as m:
                for u in range(2):
                    load_rows(m * 2 + (C_FROM + 2 + u), u % 2 ^ (C_FROM % 2), C_FROM)

            def store_out(i):
                sp.wait_ge(combined, (i + 1) * TOP)
                sp.dma_start(out[bass.ds(i, 1), :, :].rearrange("s p d -> (s p) d"), row(H, i)).then_inc(out_stored, 16)

            with sp.Fori(0, SEQS) as i:
                store_out(i)
            sp.wait_ge(out_stored, 16 * SEQS)
            sp.wait_ge(y_stored, 16 * ROUTED_BLOCKS)

        @block.gpsimd
        def _(pool):
            pool.iota(expert_no, pattern=[[1, E], [0, SEQS]], base=0, channel_multiplier=0, allow_small_or_imprecise_dtypes=True).then_inc(made, 1)
            pool.iota(block_no, pattern=[[1, ROUTED_BLOCKS], [0, E]], base=0, channel_multiplier=0, allow_small_or_imprecise_dtypes=True).then_inc(made, 1)
            pool.iota(token_i[:, :], pattern=[[T, SEQS]], base=0, channel_multiplier=1).then_inc(made, 1)
            pool.memset(nothing, 0).then_inc(made, 1)
            pool.memset(zeros, 0.0).then_inc(made, 1)
            pool.memset(below[:, :], 1.0).then_inc(masked, 1)
            pool.wait_ge(masked, 1)
            pool.affine_select(out=below[:, :], in_=below[:, :], compare_op=ALU.is_gt, fill=0.0, base=0, pattern=[[1, P]],
                               channel_multiplier=-1).then_inc(masked, 1)
            pool.wait_ge(table_zeroed, 16)
            pool.wait_ge(plan, 1)
            for t in range(TOP):
                for i in range(SEQS):
                    pool.indirect_dma_start(out=slot_token, out_offset=bass.IndirectOffsetOnAxis(ap=table_i[:, t * SEQS + i:t * SEQS + i + 1], axis=0),
                                            in_=token_i[:, i:i + 1], in_offset=None).then_inc(scattered, 16)
            pool.wait_ge(scattered, 16 * TOP * SEQS)
            pool.dma_start(slot_tokens[:, :], slot_token.rearrange("(p c) x -> p (c x)", p=P)).then_inc(table_in, 16)
            pool.wait_ge(table_in, 16)
            for r in range(ROUTED_BLOCKS):
                n = B_FROM + r
                pool.wait_ge(x_turned, n - 1)
                for a in range(2):
                    pool.indirect_dma_start(out=xr[n % 2][:, a, :], out_offset=None, in_=x2_dram,
                                            in_offset=bass.IndirectOffsetOnAxis(ap=slot_tokens[:, 2 * r + a:2 * r + a + 1], axis=0)).then_inc(rows_gathered[n % 2], 16)
            pool.wait_ge(y_stored, 16 * ROUTED_BLOCKS)
            for i in range(SEQS):
                after(pool, combined, (i - 1) * TOP)
                for t in range(TOP):
                    pool.indirect_dma_start(out=comb[i % 2][:, t, :], out_offset=None, in_=y_dram,
                                            in_offset=bass.IndirectOffsetOnAxis(ap=slot_i[:, t * SEQS + i:t * SEQS + i + 1], axis=0)).then_inc(comb_in[i % 2], 16)

        @block.scalar
        def _(act):
            def turned_hi(n, odd):
                act.wait_ge(x_turned, n + 1)
                after(act, up_done, (n - 1) * 3)
                act.activation(xT_hi[odd][:, :, :], xT_ps[:, :, :], ACT.Copy).then_inc(xT_hi_done, 1)

            def weights_hi(w, piece, buffer):
                a, b = PIECES[piece]
                act.wait_ge(stage_in[piece], (w + 1) * 16)
                act.activation(w_hi[buffer][:, a:b], w_stage[:, a:b], ACT.Copy).then_inc(w_hi_done[piece], 1)

            def take_y(n, kind):
                if kind == "B":
                    act.wait_ge(down_done, n * 2 + 2)
                    after(act, y_stored, (n - B_FROM) * 16)
                    act.activation(y[:, 1, :], down_ps[1][:, :], ACT.Copy).then_inc(y_taken, 1)

            def body(n, odd, kind, kind_before, kind_after):
                if kind_after:
                    turned_hi(n + 1, 1 - odd)
                new = kind_after == "B" or (kind, kind_after) == ("B", "C")
                w = w_of(n + 1, kind_after) if new else None
                buffer = w_buffer(1 - odd, kind_after) if new else None
                if new:
                    act.wait_ge(up_done, n * 3)
                    weights_hi(w, 0, buffer)
                    weights_hi(w, 1, buffer)
                for j, (_, f) in enumerate(F_TILES):
                    act.wait_ge(up_done, n * 3 + j + 1)
                    after(act, h_done, (n - 1) * 3 + j + 1)
                    act.activation(act_g[0:f, j, :], up_ps[j][0:f, 0:BLOCK], ACT.Silu).then_inc(silu_done, 1)
                    act.wait_ge(h_done, n * 3 + j + 1)
                    after(act, down_done, (n - 1) * 2)
                    act.activation(h_hi[odd][0:f, j, :], h[0:f, j, :], ACT.Copy).then_inc(h_hi_done, 1)
                take_y(n - 1, kind_before)
                if new:
                    act.wait_ge(down_done, n * 2)
                    weights_hi(w, 2, buffer)

            turned_hi(0, 0)
            for piece in range(3):
                weights_hi(0, piece, 0)
            each_block(act, body)

        @block.vector
        def _(dve):
            dve.wait_ge(made, 5)
            step = 0

            def did(ins):
                nonlocal step
                step += 1
                ins.then_inc(counted, 1)
                dve.wait_ge(counted, step)

            for t in range(TOP):
                choice = gate_experts[:, :, t].unsqueeze(1).to_broadcast([P, E, SEQS])
                did(dve.tensor_tensor(hot[t], expert_no, choice, ALU.is_equal))
            did(dve.tensor_tensor(chosen, hot[0], hot[1], ALU.add))
            dve.wait_ge(masked, 3)
            sums = route_ps[:, 0:2 * SE].rearrange("p (a e s) -> p a e s", a=2, e=E)
            did(dve.tensor_copy(before, sums[:, 0]))
            did(dve.tensor_copy(in_seq, sums[:, 1]))
            for e in range(E):
                did(dve.tensor_tensor_scan(upto[:, e, :], in_seq[:, e, :], zeros[:, e, :], 0.0, ALU.add, ALU.add))
            did(dve.tensor_scalar(count[:, 0, :], upto[:, :, SEQS - 1], float(BLOCK - 1), None, ALU.add))
            did(dve.tensor_copy(count_i[:, 0, :], count[:, 0, :]))
            did(dve.tensor_scalar(count_i[:, 0, :], count_i[:, 0, :], BLOCK.bit_length() - 1, None, ALU.logical_shift_right))
            did(dve.tensor_copy(blocks[:, 0, :], count_i[:, 0, :]))
            did(dve.tensor_tensor_scan(ends[:, 0, :], blocks[:, 0, :], zeros[:, 0, 0:E], 0.0, ALU.add, ALU.add))
            did(dve.tensor_tensor(block_no, block_no, ends[:, 0, :].unsqueeze(1).to_broadcast([P, ROUTED_BLOCKS, E]), ALU.is_ge))
            did(dve.tensor_reduce(block_f[:, 0, :], block_no, X_AXIS, ALU.add))
            did(dve.tensor_scalar(block_f[:, 0, :], block_f[:, 0, :], float(E - 1), None, ALU.min))
            dve.tensor_copy(block_expert[:, :], block_f[:, 0, :]).then_inc(blocks_known, 1)
            did(dve.tensor_tensor(starts[:, 0, :], ends[:, 0, :], blocks[:, 0, :], ALU.subtract))
            did(dve.tensor_scalar(starts[:, 0, :], starts[:, 0, :], float(BLOCK), None, ALU.mult))
            did(dve.tensor_tensor(upto, upto, in_seq, ALU.subtract))
            did(dve.tensor_tensor(upto, upto, before, ALU.add))
            did(dve.tensor_tensor(upto, upto, starts[:, 0, :].unsqueeze(2).to_broadcast([P, E, SEQS]), ALU.add))
            for t in range(TOP):
                did(dve.tensor_tensor(hot[t], hot[t], upto, ALU.mult))
                did(dve.tensor_reduce(slot_f[:, 0, t * SEQS:(t + 1) * SEQS], hot[t].rearrange("p e s -> p s e"), X_AXIS, ALU.add))
            did(dve.tensor_copy(slot_i[:, :], slot_f[:, 0, :]))
            did(dve.tensor_scalar(tile_i[:, 0, :], slot_i[:, :], P.bit_length() - 1, None, ALU.logical_shift_right))
            did(dve.tensor_copy(tile_f[:, 0, :], tile_i[:, 0, :]))
            did(dve.tensor_scalar(tile_f[:, 0, :], tile_f[:, 0, :], float(1 - P * SLOT_TILES), None, ALU.mult))
            did(dve.scalar_tensor_tensor(out=tile_f[:, 0, :], in0=slot_f[:, 0, :], scalar=float(SLOT_TILES), in1=tile_f[:, 0, :],
                                         op0=ALU.mult, op1=ALU.add))
            dve.tensor_copy(table_i[:, :], tile_f[:, 0, :]).then_inc(plan, 1)

            def turned_lo(n, odd):
                dve.wait_ge(xT_hi_done, n + 1)
                after(dve, up_done, (n - 1) * 3)
                dve.tensor_tensor(xT_lo[odd][:, :, :], xT_ps[:, :, :], xT_hi[odd][:, :, :].bitcast(F32), ALU.subtract).then_inc(xT_lo_done, 1)

            def weights_lo(w, piece, buffer):
                a, b = PIECES[piece]
                dve.wait_ge(w_hi_done[piece], w + 1)
                dve.tensor_tensor(w_lo[buffer][:, a:b], w_stage[:, a:b], w_hi[buffer][:, a:b].bitcast(F32), ALU.subtract).then_inc(w_lo_done[piece], 1)

            def take_y(n, kind):
                if kind == "B":
                    dve.wait_ge(down_done, n * 2 + 1)
                    after(dve, y_stored, (n - B_FROM) * 16)
                    dve.tensor_copy(y[:, 0, :], down_ps[0][:, :]).then_inc(y_taken, 1)
                elif kind:
                    first = 0 if kind == "A" else C_FROM
                    for r in range(2):
                        i = (n - first) * 2 + r
                        dve.wait_ge(down_done, n * 2 + r + 1)
                        dve.tensor_tensor(row(H, i), row(H, i), down_ps[r][:, :], ALU.add).then_inc(y_taken, 1)

            def combine(i, odd):
                dve.wait_ge(comb_in[odd], (i - odd) * TOP * 8 + TOP * 16)
                for t in range(TOP):
                    if t:
                        dve.wait_ge(combined, i * TOP + t)
                    dve.scalar_tensor_tensor(out=row(H, i), in0=comb[odd][:, t, :], scalar=gate_values[:, bass.ds(i, 1), t],
                                             in1=row(H, i), op0=ALU.mult, op1=ALU.add).then_inc(combined, 1)

            def body(n, odd, kind, kind_before, kind_after):
                if kind_after:
                    turned_lo(n + 1, 1 - odd)
                new = kind_after == "B" or (kind, kind_after) == ("B", "C")
                w = w_of(n + 1, kind_after) if new else None
                buffer = w_buffer(1 - odd, kind_after) if new else None
                if new:
                    weights_lo(w, 0, buffer)
                    weights_lo(w, 1, buffer)
                for j, (_, f) in enumerate(F_TILES):
                    dve.wait_ge(silu_done, n * 3 + j + 1)
                    after(dve, h_lo_done, (n - 1) * 3 + j + 1)
                    dve.tensor_tensor(h[0:f, j, :], act_g[0:f, j, :], up_ps[j][0:f, BLOCK:2 * BLOCK], ALU.mult).then_inc(h_done, 1)
                    dve.wait_ge(h_hi_done, n * 3 + j + 1)
                    dve.tensor_tensor(h_lo[odd][0:f, j, :], h[0:f, j, :], h_hi[odd][0:f, j, :].bitcast(F32), ALU.subtract).then_inc(h_lo_done, 1)
                take_y(n - 1, kind_before)
                if new:
                    weights_lo(w, 2, buffer)
                if kind == "C" and kind_before == "C":
                    dve.wait_ge(y_taken, n * 2)
                    if not isinstance(n, int) or n > C_FROM + 1:
                        for r in range(2):
                            combine((n - (C_FROM + 1)) * 2 + r, r)

            turned_lo(0, 0)
            for piece in range(3):
                weights_lo(0, piece, 0)
            each_block(dve, body)
            take_y(N - 1, "C")
            dve.wait_ge(y_taken, 2 * N)
            for i in range(SEQS - 2, SEQS):
                combine(i, i % 2)

        @block.tensor
        def _(pe):
            pe.wait_ge(masked, 2)
            pe.wait_ge(counted, 3)
            flat = chosen.rearrange("p e s -> p (e s)")
            pe.matmul(route_ps[:, 0:SE], below[:, :], flat, start=True, stop=True)
            pe.matmul(route_ps[:, SE:2 * SE], ones[:, :], flat, start=True, stop=True).then_inc(masked, 1)

            def three(out, a_hi, a_lo, b_hi, b_lo, first, last):
                pe.matmul(out, a_hi, b_hi, start=first, stop=False)
                pe.matmul(out, a_hi, b_lo, start=False, stop=False)
                return pe.matmul(out, a_lo, b_hi, start=False, stop=last)

            def up(n, odd, w, buffer):
                pe.wait_ge(xT_lo_done, n + 1)
                pe.wait_ge(w_lo_done[0], w + 1)
                pe.wait_ge(w_lo_done[1], w + 1)
                for j, (start, f) in enumerate(F_TILES):
                    after(pe, h_done, (n - 1) * 3 + j + 1)
                    for half in range(2):
                        for k in range(KT):
                            c = k * 2 * ROUTED_F + half * ROUTED_F + start
                            mm = three(up_ps[j][0:f, half * BLOCK:(half + 1) * BLOCK], w_hi[buffer][:, c:c + f], w_lo[buffer][:, c:c + f],
                                       xT_hi[odd][:, k, :], xT_lo[odd][:, k, :], k == 0, k == KT - 1)
                    mm.then_inc(up_done, 1)

            def down(n, odd, w, buffer):
                pe.wait_ge(h_lo_done, n * 3 + 3)
                pe.wait_ge(w_lo_done[2], w + 1)
                for r in range(2):
                    after(pe, y_taken, n * 2)
                    for j, (_, f) in enumerate(F_TILES):
                        c = UP_COLS + j * D
                        mm = three(down_ps[r][:, :], h_hi[odd][0:f, j, r * P:(r + 1) * P], h_lo[odd][0:f, j, r * P:(r + 1) * P],
                                   w_hi[buffer][0:f, c:c + D], w_lo[buffer][0:f, c:c + D], j == 0, j == 2)
                    mm.then_inc(down_done, 1)

            def body(n, odd, kind, kind_before, kind_after):
                if kind_after:
                    turn(n + 1, 1 - odd, kind_after)
                up(n, odd, w_of(n, kind), w_buffer(odd, kind))
                if kind_before:
                    down(n - 1, 1 - odd, w_of(n - 1, kind_before), w_buffer(1 - odd, kind_before))

            def turn(n, odd, kind):
                if kind == "A":
                    pe.wait_ge(rows_in[odd], (n - odd) * 16 + 32)
                elif kind == "B":
                    pe.wait_ge(rows_gathered[odd], (n - B_FROM - odd) * 16 + 32)
                else:
                    pe.wait_ge(rows_in[odd], (n - C_FROM - (1 - odd)) * 16 + 32 + B_FROM * 16)
                after(pe, xT_lo_done, n)
                for r in range(2):
                    for k in range(KT):
                        mm = pe.transpose(xT_ps[:, k, r * P:(r + 1) * P], xr[odd][:, r, k * P:(k + 1) * P], ident[:, :])
                mm.then_inc(x_turned, 1)

            turn(0, 0, "A")
            each_block(pe, body)
            down(N - 1, 0, LAST_W, 0)


def tower(nc, a, out):
    x2_dram = nc.dram_tensor("x2_rows", [TOKENS, D], F32, kind="Internal").ap()
    y_dram = nc.dram_tensor("slot_rows", [SLOT_TILES * P, D], F32, kind="Internal").ap()
    slot_token = nc.dram_tensor("slot_token", [SLOT_TILES * P, 1], I32, kind="Internal").ap()
    with ExitStack() as ctx:
        def sb(name, shape, dt=F32):
            return ctx.enter_context(nc.sbuf_tensor(name, shape, dt))

        H = sb("H", [P, SEQS, D])
        ident, ones = sb("ident", [P, P]), sb("ones", [P, P])
        gate_values, gate_experts = sb("gate_values", [P, SEQS, TOP]), sb("gate_experts", [P, SEQS, TOP])
        with ExitStack() as attention:
            wT = [attention.enter_context(nc.sbuf_tensor(f"wT_{n}", [P, KT, D], BF16)) for n in "qkvo"]
            w_scale = attention.enter_context(nc.sbuf_tensor("w_scale", [P, 4], F32))
            S_bc = attention.enter_context(nc.sbuf_tensor("S_bc", [P, D], F32))
            embed(nc, a["ids"], a["table"], a["table_t"], a["lora_a"], a["lora_a_t"], a["lora_b_t"], a["magnitude_t"],
                  [a["w_q_t"], a["w_k_t"], a["w_v_t"], a["w_o_t"]], H, wT, w_scale, S_bc, ident, ones)
            attend(nc, a["router_t"], x2_dram, H, wT, w_scale, S_bc, ident, ones, gate_values, gate_experts)
        experts(nc, a["packed"], x2_dram, slot_token, y_dram, out, H, ident, ones, gate_values, gate_experts)


def kernel(x, L0_tok_weight, L0_tok_lora_A, L0_tok_lora_B, L0_tok_magnitude, L0_attn_w_q, L0_attn_w_k, L0_attn_w_v, L0_attn_w_o,
           L0_ffn_Wr, L0_ffn_Wg, L0_ffn_Wu, L0_ffn_Wd, L0_ffn_Wsg, L0_ffn_Wsu, L0_ffn_Wsd):
    import numpy as np
    import concourse.bacc as bacc
    from concourse.bass_utils import run_bass_kernel_spmd

    def turned(w):
        return np.ascontiguousarray(np.asarray(w).T)

    gates = np.concatenate([L0_ffn_Wg, np.asarray(L0_ffn_Wsg).reshape(2, ROUTED_F, D)])
    ups = np.concatenate([L0_ffn_Wu, np.asarray(L0_ffn_Wsu).reshape(2, ROUTED_F, D)])
    downs = np.concatenate([np.asarray(L0_ffn_Wd).transpose(0, 2, 1), turned(L0_ffn_Wsd).reshape(2, ROUTED_F, D)])
    n = len(gates)
    packed = np.zeros((n, P, PACKED), gates.dtype)
    both = packed[:, :, :UP_COLS].reshape(n, P, KT, 2, ROUTED_F)
    both[:, :, :, 0] = gates.reshape(n, ROUTED_F, KT, P).transpose(0, 3, 2, 1)
    both[:, :, :, 1] = ups.reshape(n, ROUTED_F, KT, P).transpose(0, 3, 2, 1)
    packed[:, :, :UP_COLS] = both.reshape(n, P, UP_COLS)
    for j, (start, f) in enumerate(F_TILES):
        packed[:, :f, UP_COLS + j * D:UP_COLS + (j + 1) * D] = downs[:, start:start + f]

    arrays = {
        "ids": turned(x),
        "table": np.ascontiguousarray(L0_tok_weight),
        "table_t": turned(L0_tok_weight),
        "lora_a": np.ascontiguousarray(L0_tok_lora_A),
        "lora_a_t": turned(L0_tok_lora_A),
        "lora_b_t": turned(L0_tok_lora_B),
        "magnitude_t": turned(np.asarray(L0_tok_magnitude).reshape(KT, P)),
        "w_q_t": turned(L0_attn_w_q), "w_k_t": turned(L0_attn_w_k), "w_v_t": turned(L0_attn_w_v), "w_o_t": turned(L0_attn_w_o),
        "router_t": turned(L0_ffn_Wr),
        "packed": packed,
    }
    nc = bacc.Bacc("TRN2", target_bir_lowering=False, num_devices=1)
    inputs = {name: nc.dram_tensor(name, v.shape, mybir.dt.from_np(v.dtype), kind="ExternalInput").ap() for name, v in arrays.items()}
    out = nc.dram_tensor("out", (SEQS, T, D), F32, kind="ExternalOutput").ap()
    tower(nc, inputs, out)
    result = run_bass_kernel_spmd(nc, [arrays], core_ids=[0])
    return result.results[0]["out"]
```

```python
from contextlib import ExitStack

import concourse.bass as bass
from concourse import mybir

F32 = mybir.dt.float32
F32R = mybir.dt.float32r
BF16 = mybir.dt.bfloat16
I32 = mybir.dt.int32
U32 = mybir.dt.uint32
ALU = mybir.AluOpType
ACT = mybir.ActivationFunctionType
X_AXIS = mybir.AxisListType.X

P = 128
SEQS, T = 32, 128
D = 512
KT = D // P
HEADS, DH = 16, 32
GROUPS = P // DH
PER_GROUP = HEADS // GROUPS
VOCAB, RANK = 32000, 16
LORA_SCALE = 2.0
EXPERTS, TOP = 8, 2
LN_EPS = 1e-5
QUANT_MIN = 1e-5
QMAX = 127.0
ROUNDER = 1.5 * 2.0**23

CHUNK = 1000
CHUNKS = VOCAB // CHUNK
HALF = CHUNK // 2
SEQ_GROUP = 4
assert CHUNKS == SEQS


def after(eng, semaphore, value):
    if not isinstance(value, int) or value > 0:
        eng.wait_ge(semaphore, value)


def row(tile, i):
    return tile[:, bass.ds(i, 1), :].rearrange("p a d -> p (a d)")


def embed(nc, ids, table, table_t, lora_a, lora_a_t, lora_b_t, magnitude_t, attn_ws, H, wT, w_scale, S_bc, ident, ones):
    with ExitStack() as ctx:
        def sb(name, shape, dt=F32):
            return ctx.enter_context(nc.sbuf_tensor(name, shape, dt))

        def ps(name, shape):
            return ctx.enter_context(nc.psum_tensor(name, shape, F32))

        def sem(name):
            return ctx.enter_context(nc.semaphore(name))

        ids_i = sb("ids_i", [P, SEQS], I32)
        ids_f = sb("ids_f", [P, SEQS])
        wrap = sb("wrap", [P, SEQS])
        rows_i = sb("rows_i", [P, SEQS], I32)
        a_rows = sb("a_rows", [P, SEQS, DH])
        a_group = sb("a_group", [P, P])
        a_group_t = sb("a_group_t", [P, P])
        b_rep = sb("b_rep", [P, D])
        b_f = sb("b_f", [96, D])
        b_split = sb("b_split", [96, D], F32R)
        a_f = sb("a_f", [64, 4, CHUNK])
        a_split = [sb(f"a_split{i}", [96, CHUNK], F32R) for i in range(2)]
        W = sb("W", [P, 4, KT, CHUNK])
        part = sb("part", [P, 2, KT])
        total = sb("total", [P, KT])
        root = sb("root", [P, KT])
        half = sb("half", [P, KT])
        mag = sb("mag", [P, KT])
        col_scale = sb("col_scale", [P, KT])
        diag = sb("diag", [P, KT, P])
        w_sum = sb("w_sum", [P, 4])
        w_inv = sb("w_inv", [P, 4])
        norm_ps = [ps(f"norm_ps{i}", [P, 2, 512]) for i in range(2)]
        lora_ps = [ps(f"lora_ps{i}", [P, 512]) for i in range(2)]
        turn_ps = ps("turn_ps", [P, 512])
        misc_ps = ps("misc_ps", [P, 512])

        ids_in, ids_step = sem("ids_in"), sem("ids_step")
        rows_zeroed, operands_zeroed, const_ready, id_zero = sem("rows_zeroed"), sem("operands_zeroed"), sem("const_ready"), sem("id_zero")
        b_in = sem("b_in")
        gathered, rows_ready = sem("gathered"), sem("rows_ready")
        a_in = [sem(f"a_in{i}") for i in range(4)]
        w_in = [sem(f"w_in{i}") for i in range(4)]
        attn_in = sem("attn_in")
        b_hi, b_lo, a_hi, a_lo = sem("b_hi"), sem("b_lo"), sem("a_hi"), sem("a_lo")
        normed, added, squared, part_added, lora_free = sem("normed"), sem("added"), sem("squared"), sem("part_added"), sem("lora_free")
        grouped, group_turned, group_copied, lora_done = sem("grouped"), sem("group_turned"), sem("group_copied"), sem("lora_done")
        w_abs, w_tot, w_scaled, w_step = sem("w_abs"), sem("w_tot"), sem("w_scaled"), sem("w_step")
        rooted, scaled, diagonal, spread, norm_out = sem("rooted"), sem("scaled"), sem("diagonal"), sem("spread"), sem("norm_out")

        block = ctx.enter_context(nc.Block())
        trips = CHUNKS // 4
        w_f = [H[:, SEQS - (4 - n) * KT:SEQS - (3 - n) * KT, :] for n in range(4)]
        table_t_v = table_t.rearrange("(k p) v -> p k v", p=P)

        @block.sync
        def _(sp):
            sp.dma_start(ids_i[:, :], ids).then_inc(ids_in, 16)
            sp.wait_ge(operands_zeroed, 3)
            for r in range(3):
                sp.dma_start(b_f[32 * r:32 * r + RANK, :], lora_b_t).then_inc(b_in, 16)
            for j in range(GROUPS):
                sp.dma_start(b_rep[DH * j:DH * j + RANK, :], lora_b_t).then_inc(b_in, 16)
            sp.dma_start(mag[:, :], magnitude_t).then_inc(b_in, 16)
            sp.sem_inc(squared, 4 * KT)
            sp.sem_inc(a_lo, 4)
            with sp.Fori(0, trips) as g:
                for q in range(4):
                    c = g * 4 + q
                    sp.wait_ge(a_lo, c + 1)
                    for r in range(2):
                        sp.dma_start(a_f[32 * r:32 * r + RANK, q, :], lora_a[:, bass.ds(c * CHUNK, CHUNK)]).then_inc(a_in[q], 16)
                    sp.wait_ge(squared, (c + 1) * KT)
                    sp.dma_start(W[:, q, :, :], table_t_v[:, :, bass.ds(c * CHUNK, CHUNK)]).then_inc(w_in[q], 16)

        @block.gpsimd
        def _(pool):
            pool.memset(ident[:, :], 0.0).then_inc(id_zero, 1)
            pool.memset(ones[:, :], 1.0).then_inc(const_ready, 1)
            pool.memset(a_rows[:, :, :], 0.0).then_inc(rows_zeroed, 1)
            pool.memset(half[:, :], 0.5).then_inc(const_ready, 1)
            pool.wait_ge(id_zero, 1)
            pool.affine_select(out=ident[:, :], in_=ident[:, :], compare_op=ALU.not_equal, fill=1.0, base=0,
                               pattern=[[-1, P]], channel_multiplier=1).then_inc(const_ready, 1)
            pool.wait_ge(ids_step, 5)
            pool.wait_ge(rows_zeroed, 1)
            for i in range(SEQS):
                if i == SEQS - 4 * KT:
                    pool.wait_ge(w_step, 12)
                at = bass.IndirectOffsetOnAxis(ap=rows_i[:, i:i + 1], axis=0)
                pool.indirect_dma_start(out=H[:, i, :], out_offset=None, in_=table, in_offset=at).then_inc(gathered, 16)
                pool.indirect_dma_start(out=a_rows[:, i, 0:RANK], out_offset=None, in_=lora_a_t, in_offset=at).then_inc(gathered, 16)
                if i % SEQ_GROUP == SEQ_GROUP - 1:
                    pool.wait_ge(gathered, 32 * (i + 1))
                    pool.sem_inc(rows_ready, 1)
            pool.wait_ge(part_added, 2 + CHUNKS)
            pool.tensor_tensor(root[:, :], total[:, :], half[:, :], ALU.pow).then_inc(rooted, 1)

        @block.scalar
        def _(act):
            for n in range(4):
                act.dma_start(w_f[n], attn_ws[n].rearrange("(k p) c -> p k c", p=P)).then_inc(attn_in, 16)
            act.sem_inc(added, 2)
            act.wait_ge(attn_in, 16 * 4)
            for n in range(4):
                act.activation(wT[n][:, :, :], w_f[n], ACT.Abs, accum_out=w_sum[:, n:n + 1]).then_inc(w_abs, 1)
            act.wait_ge(b_in, 16 * 8)
            act.activation(b_split[:, :], b_f[:, :], ACT.Copy, scale=LORA_SCALE).then_inc(b_hi, 1)

            def high_part(c, g, q):
                act.wait_ge(a_in[q], (g + 1) * 32)
                act.wait_ge(normed, (c + 1) * KT)
                act.activation(a_split[q % 2][0:64, :], a_f[:, q, :], ACT.Copy).then_inc(a_hi, 1)

            def squares(c, q, first, last):
                for k in range(first, last):
                    if k == 0:
                        act.wait_ge(part_added, c + 1)
                    act.wait_ge(added, c * KT + k + 3)
                    act.activation(W[:, q, k, :], W[:, q, k, :], ACT.Square, accum_out=part[:, q % 2, k:k + 1]).then_inc(squared, 1)

            def copy_group(g):
                act.wait_ge(group_turned, g + 1)
                act.activation(a_group_t[:, :], turn_ps[:, 0:P], ACT.Copy).then_inc(group_copied, 1)

            def trip(g, last):
                for q in range(4):
                    c = g * 4 + q
                    squares(c, q, 0, 1)
                    if not (last and q == 3):
                        high_part(c + 1, g + (q + 1) // 4, (q + 1) % 4)
                    squares(c, q, 1, KT)
                if not last:
                    copy_group(g + 1)

            high_part(0, 0, 0)
            copy_group(0)
            with act.Fori(0, trips - 1) as g:
                trip(g, False)
            trip(trips - 1, True)

        @block.vector
        def _(dve):
            dve.memset(b_f[:, :], 0.0).then_inc(operands_zeroed, 1)
            dve.memset(b_rep[:, :], 0.0).then_inc(operands_zeroed, 1)
            dve.memset(a_f[:, :, :], 0.0).then_inc(operands_zeroed, 1)
            dve.memset(total[:, :], 0.0).then_inc(const_ready, 1)
            dve.sem_inc(part_added, 2)
            dve.wait_ge(ids_in, 16)
            dve.tensor_copy(ids_f[:, :], ids_i[:, :]).then_inc(ids_step, 1)
            dve.wait_ge(ids_step, 1)
            dve.tensor_scalar(wrap[:, :], ids_f[:, :], 0.0, float(VOCAB), ALU.is_lt, ALU.mult).then_inc(ids_step, 1)
            dve.wait_ge(ids_step, 2)
            dve.tensor_tensor(ids_f[:, :], ids_f[:, :], wrap[:, :], ALU.add).then_inc(ids_step, 1)
            dve.wait_ge(ids_step, 3)
            dve.tensor_scalar(ids_f[:, :], ids_f[:, :], 0.0, float(VOCAB - 1), ALU.max, ALU.min).then_inc(ids_step, 1)
            dve.wait_ge(ids_step, 4)
            dve.tensor_copy(rows_i[:, :], ids_f[:, :]).then_inc(ids_step, 1)
            dve.wait_ge(b_hi, 1)
            dve.scalar_tensor_tensor(out=b_split[32:64, :], in0=b_f[32:64, :], scalar=LORA_SCALE, in1=b_split[32:64, :].bitcast(F32),
                                     op0=ALU.mult, op1=ALU.subtract).then_inc(b_lo, 1)

            def low_part(c, q):
                dve.wait_ge(a_hi, c + 1)
                dve.tensor_tensor(a_split[q % 2][64:96, :], a_f[0:32, q, :], a_split[q % 2][0:32, :].bitcast(F32),
                                  ALU.subtract).then_inc(a_lo, 1)

            def add_products(c, g, q, first, last):
                for k in range(first, last):
                    if k == 0:
                        dve.wait_ge(w_in[q], (g + 1) * 16)
                    dve.wait_ge(normed, 2 * KT + c * KT + k + 1)
                    w = W[:, q, k, :].rearrange("p (h n) -> p h n", h=2)
                    dve.tensor_tensor(w, w, norm_ps[k % 2][:, :, 0:HALF], ALU.add).then_inc(added, 1)

            def add_part(c, q):
                dve.wait_ge(squared, 4 * KT + (c + 1) * KT)
                dve.wait_ge(part_added, c + 2)
                dve.tensor_tensor(total[:, :], total[:, :], part[:, q % 2, :], ALU.add).then_inc(part_added, 1)

            def group_rows(g):
                dve.wait_ge(rows_ready, g + 1)
                after(dve, group_turned, g)
                dve.tensor_scalar(a_group[:, :].rearrange("p (s r) -> p s r", s=SEQ_GROUP), a_rows[:, bass.ds(g * SEQ_GROUP, SEQ_GROUP), :],
                                  LORA_SCALE, None, ALU.mult).then_inc(grouped, 1)

            def add_lora(i, j):
                dve.wait_ge(lora_done, i + 1)
                dve.tensor_tensor(row(H, i), row(H, i), lora_ps[j % 2][:, :], ALU.add).then_inc(lora_free, 1)

            def trip(g, last):
                for q in range(4):
                    c = g * 4 + q
                    add_products(c, g, q, 0, 3)
                    if not (last and q == 3):
                        low_part(c + 1, (q + 1) % 4)
                    add_products(c, g, q, 3, KT)
                    add_lora(c, q)
                    if q:
                        add_part(c - 1, q - 1)
                    if q == 2 and not last:
                        group_rows(g + 1)
                add_part(g * 4 + 3, 3)

            dve.wait_ge(const_ready, 4)
            low_part(0, 0)
            dve.wait_ge(w_tot, 1)
            dve.tensor_scalar(w_scale[:, :], misc_ps[:, 0:4], 1.0 / (D * D), QUANT_MIN, ALU.mult, ALU.max).then_inc(w_scaled, 1)
            dve.wait_ge(w_scaled, 1)
            dve.reciprocal(w_inv[:, :], w_scale[:, :]).then_inc(w_scaled, 1)
            dve.wait_ge(w_scaled, 2)
            for n in range(4):
                dve.tensor_scalar(w_f[n], w_f[n], w_inv[:, n:n + 1], ROUNDER, ALU.mult, ALU.add).then_inc(w_step, 1)
            for n in range(4):
                dve.wait_ge(w_step, n + 1)
                dve.tensor_scalar(w_f[n], w_f[n], -ROUNDER, 1.0, ALU.add, ALU.min).then_inc(w_step, 1)
            for n in range(4):
                dve.wait_ge(w_step, 4 + n + 1)
                dve.tensor_scalar(wT[n][:, :, :], w_f[n], -1.0, None, ALU.max).then_inc(w_step, 1)
            group_rows(0)
            with dve.Fori(0, trips - 1) as g:
                trip(g, False)
            trip(trips - 1, True)
            dve.wait_ge(rooted, 1)
            dve.tensor_tensor(col_scale[:, :], root[:, :], mag[:, :], ALU.mult).then_inc(scaled, 1)
            dve.wait_ge(scaled, 1)
            for k in range(KT):
                dve.tensor_scalar(diag[:, k, :], ident[:, :], col_scale[:, k:k + 1], None, ALU.mult).then_inc(diagonal, 1)
            dve.wait_ge(spread, 1)
            dve.tensor_copy(S_bc[:, :], misc_ps[:, :]).then_inc(norm_out, 1)
            dve.wait_ge(norm_out, 1)

        @block.tensor
        def _(pe):
            pe.sem_inc(normed, 2 * KT)
            pe.sem_inc(lora_free, 2)
            pe.wait_ge(const_ready, 4)
            pe.wait_ge(b_lo, 1)

            def products(c, q):
                pe.wait_ge(a_lo, 4 + c + 1)
                for k in range(KT):
                    pe.wait_ge(added, c * KT + k + 1)
                    for h in range(2):
                        mm = pe.matmul(norm_ps[k % 2][:, h, 0:HALF], b_split[:, k * P:(k + 1) * P],
                                       a_split[q % 2][:, h * HALF:(h + 1) * HALF], start=True, stop=True)
                    mm.then_inc(normed, 1)

            def turn_group(g):
                pe.wait_ge(grouped, g + 1)
                pe.transpose(turn_ps[:, 0:P], a_group[:, :], ident[:, :]).then_inc(group_turned, 1)

            def lora_rows(i, j, g):
                pe.wait_ge(group_copied, g + 1)
                pe.wait_ge(lora_free, i + 1)
                pe.matmul(lora_ps[j % 2][:, :], a_group_t[DH * j:DH * (j + 1), :], b_rep[DH * j:DH * (j + 1), :],
                          start=True, stop=True).then_inc(lora_done, 1)

            def trip(g, last):
                for q in range(4):
                    products(g * 4 + q, q)
                    lora_rows(g * 4 + q, q, g)
                if not last:
                    turn_group(g + 1)

            pe.wait_ge(w_abs, 4)
            pe.matmul(misc_ps[:, 0:4], ones[:, :], w_sum[:, :], start=True, stop=True).then_inc(w_tot, 1)
            turn_group(0)
            with pe.Fori(0, trips - 1) as g:
                trip(g, False)
            trip(trips - 1, True)
            for k in range(KT):
                pe.wait_ge(diagonal, k + 1)
                mm = pe.matmul(misc_ps[:, k * P:(k + 1) * P], ones[:, :], diag[:, k, :], start=(k == 0), stop=(k == KT - 1),
                               skip_group_check=True)
            mm.then_inc(spread, 1)


class Live:

    def __init__(self, step, odd, back):
        self.i = step - back
        self.b = (odd + back) % 2
        self.yes = not isinstance(self.i, int) or 0 <= self.i < SEQS
        self.next = self.i + 1


def attend(nc, router_t, x2_dram, H, wT, w_scale, S_bc, ident, ones, gate_values, gate_experts):
    with ExitStack() as ctx:
        def sb(name, shape, dt=F32):
            return ctx.enter_context(nc.sbuf_tensor(name, shape, dt))

        def pair(name, shape, dt=F32):
            return [sb(f"{name}{i}", shape, dt) for i in range(2)]

        def ps(name, shape, dt=F32):
            return ctx.enter_context(nc.psum_tensor(name, shape, dt))

        def sem(name):
            return ctx.enter_context(nc.semaphore(name))

        wr = sb("wr", [P, KT, EXPERTS])
        ident_b = sb("ident_b", [P, P], BF16)
        head_ones = sb("head_ones", [P, GROUPS, PER_GROUP * T], F32R)
        head_ones_f = sb("head_ones_f", [P, GROUPS * PER_GROUP, T])
        eps = sb("eps", [P, 1])
        minus_half = sb("minus_half", [P, 1])
        qk_scale = sb("qk_scale", [P, 1])
        carried = sb("carried", [P, 6])
        carried_b = sb("carried_b", [P, 1])
        stats = sb("stats", [P, 6])
        moments = pair("moments", [P, 2])
        rstd = pair("rstd", [P, 2])
        y = pair("y", [P, D])
        absmax = sb("absmax", [P, 1])
        dequant = pair("dequant", [P, 1])
        quant = pair("quant", [P, 1])
        v_scale = pair("v_scale", [P, 1])
        z = pair("z", [P, D])
        xq = pair("xq", [P, D], BF16)
        xqT = pair("xqT", [P, KT, T], BF16)
        diag = pair("diag_t", [P, P])
        scale_bc = sb("scale_bc", [P, T])
        QT = pair("QT", [P, KT, T])
        K_T = sb("K_T", [P, KT, T])
        KTx = pair("KTx", [P, KT, GROUPS, T])
        VX = pair("VX", [P, HEADS, DH + 1])
        rowmax = sb("rowmax", [P, HEADS])
        negmax = sb("negmax", [P, P], F32R)
        negmax_t = sb("negmax_t", [P, P], F32R)
        prob = sb("prob", [P, GROUPS, PER_GROUP * T])
        probT = sb("probT", [P, GROUPS, PER_GROUP * T])
        inv_sum = sb("inv_sum", [P, GROUPS, PER_GROUP])
        attn = sb("attn", [P, D])
        absmax2 = sb("absmax2", [P, 1])
        dequant2 = sb("dequant2", [P, 1])
        quant2 = sb("quant2", [P, 1])
        o_scale = sb("o_scale", [P, 1])
        z2 = sb("z2", [P, D])
        aq = sb("aq", [P, D], BF16)
        aqT = sb("aqT", [P, KT, T], BF16)
        stats2 = sb("stats2", [P, 6])
        moments2 = sb("moments2", [P, 2])
        rstd2 = sb("rstd2", [P, 2])
        x2 = pair("x2", [P, D])
        x2T = sb("x2T", [P, KT, T])
        neg_logit = sb("neg_logit", [P, 1])
        e_logit = sb("e_logit", [P, EXPERTS])
        e_sum = sb("e_sum", [P, 1])
        e_inv = sb("e_inv", [P, 1])
        gate = sb("gate", [P, EXPERTS])
        top_v = sb("top_v", [P, 8])
        top_i = sb("top_i", [P, 8], U32)

        S = ps("S", [P, GROUPS, 512])
        bank = [ps(f"bank{i}", [P, 512]) for i in range(4)]

        w_in, const, const_step = sem("wr_in"), sem("const2"), sem("const2_step")
        names = ("rows_scaled stats_done moments_done eps_added rstd_done y_done absmax_done dequant_done quant_done v_scaled z_done xq_done"
                 " diag_done xq_turned xqT_done spread_done scale_bc_done q_done QT_done k_done K_scaled KTx_even KTx_odd v_done V_done"
                 " scores_done max_done neg_hi neg_lo neg_turned neg_t_done shifted exp_done prob_turned probT_done heads_done"
                 " inv_done attn_done absmax2_done dequant2_done quant2_done o_scaled z2_done aq_done aq_turned aqT_done projected residual_done"
                 " stats2_done moments2_done eps2_added rstd2_done x2_done x2_turned x2T_done logits_done neg_logit_done e_done e_inv_done"
                 " gate_done top_v_done top_i_done gates_kept").split()
        s = {n: sem(n) for n in names}
        x2_out = [sem(f"x2_out{i}") for i in range(2)]
        (rows_scaled, stats_done, moments_done, eps_added, rstd_done, y_done, absmax_done, dequant_done, quant_done, v_scaled, z_done, xq_done,
         diag_done, xq_turned, xqT_done, spread_done, scale_bc_done, q_done, QT_done, k_done, K_scaled, KTx_even, KTx_odd, v_done, V_done,
         scores_done, max_done, neg_hi, neg_lo, neg_turned, neg_t_done, shifted, exp_done, prob_turned, probT_done, heads_done,
         inv_done, attn_done, absmax2_done, dequant2_done, quant2_done, o_scaled, z2_done, aq_done, aq_turned, aqT_done, projected, residual_done,
         stats2_done, moments2_done, eps2_added, rstd2_done, x2_done, x2_turned, x2T_done, logits_done, neg_logit_done, e_done, e_inv_done,
         gate_done, top_v_done, top_i_done, gates_kept) = s.values()

        block = ctx.enter_context(nc.Block())

        FIRST, LAST = -2, SEQS + 2
        LOOP_FROM, LOOP_TO = 6, SEQS - 2

        PROBS_BANK = (1, 0, 2, 1)

        def steps(eng, body):
            def run(k, odd):
                body(Live(k, odd, -2), Live(k, odd, -1), Live(k, odd, 0), Live(k, odd, 1), Live(k, odd, 2), Live(k, odd, 3))
            for k in range(FIRST, LOOP_FROM):
                run(k, k % 2)
            with eng.Fori(0, (LOOP_TO - LOOP_FROM) // 2) as pair_of_steps:
                for u in range(2):
                    run(pair_of_steps * 2 + (LOOP_FROM + u), (LOOP_FROM + u) % 2)
            for k in range(LOOP_TO, LAST + 1):
                run(k, k % 2)

        @block.sync
        def _(sp):
            sp.dma_start(wr[:, :, :], router_t.rearrange("(k p) e -> p k e", p=P)).then_inc(w_in, 16)

            def body(norm, fit, proj, score, out, route):
                if route.yes:
                    sp.wait_ge(x2_done, route.next)
                    sp.dma_start(x2_dram[bass.ds(route.i * T, T), :], x2[route.b][:, :]).then_inc(x2_out[route.b], 16)

            steps(sp, body)
            for b in range(2):
                sp.wait_ge(x2_out[b], 16 * SEQS // 2)

        @block.gpsimd
        def _(pool):
            pool.memset(eps[:, :], LN_EPS).then_inc(const, 1)
            pool.memset(minus_half[:, :], -0.5).then_inc(const, 1)
            for b in range(2):
                pool.memset(VX[b][:, :, DH:DH + 1], 1.0).then_inc(const, 1)
                pool.memset(KTx[b][:, :, :, :], 0.0).then_inc(const, 1)
            pool.memset(head_ones_f[:, :, :], 0.0).then_inc(const_step, 1)
            pool.wait_ge(const_step, 1)
            for n in range(2):
                pool.affine_select(out=head_ones_f[:, :, :], in_=head_ones_f[:, :, :], compare_op=ALU.not_equal, fill=1.0,
                                   base=-n * HEADS, pattern=[[-1, HEADS], [0, T]], channel_multiplier=1).then_inc(const_step, 1)
                pool.wait_ge(const_step, 2 + n)
            pool.tensor_copy(ident_b[:, :], ident[:, :]).then_inc(const, 1)
            pool.tensor_copy(head_ones[:, :, :].rearrange("r a b -> r (a b)"), head_ones_f[:, :, :].rearrange("r a b -> r (a b)")).then_inc(const, 1)
            pool.wait_ge(const, 11)

            def body(norm, fit, proj, score, out, route):
                if norm.yes:
                    pool.tensor_tensor(row(H, norm.i), row(H, norm.i), S_bc[:, :], ALU.mult).then_inc(rows_scaled, 1)
                    pool.wait_ge(rows_scaled, norm.next)
                if fit.yes:
                    pool.wait_ge(dequant_done, fit.next)
                    after(pool, spread_done, fit.i - 1)
                    pool.tensor_tensor(diag[fit.b][:, :], ident[:, :], dequant[fit.b][:, 0:1].to_broadcast([P, P]), ALU.mult).then_inc(diag_done, 1)
                    pool.wait_ge(diag_done, fit.next)
                if proj.yes:
                    pool.wait_ge(K_scaled, proj.next)
                    after(pool, scores_done, (proj.i - 1) * GROUPS)
                    for n, j in enumerate((1, 3)):
                        at = slice(DH * j, DH * (j + 1))
                        pool.tensor_tensor(KTx[proj.b][at, :, j, :], K_T[at, :, :], ones[at, :].unsqueeze(1).to_broadcast([DH, KT, T]),
                                           ALU.mult).then_inc(KTx_odd, 1)
                        pool.wait_ge(KTx_odd, proj.i * 2 + n + 1)
                if norm.yes:
                    pool.wait_ge(moments_done, norm.next)
                    after(pool, y_done, norm.i)
                    pool.tensor_tensor(rstd[norm.b][:, 0:1], moments[norm.b][:, 1:2], eps[:, :], ALU.add).then_inc(eps_added, 1)
                    pool.wait_ge(eps_added, norm.next)
                    pool.tensor_tensor(rstd[norm.b][:, 1:2], rstd[norm.b][:, 0:1], minus_half[:, :], ALU.pow).then_inc(rstd_done, 1)
                    pool.wait_ge(rstd_done, norm.next)
                if out.yes:
                    pool.wait_ge(moments2_done, out.next)
                    pool.tensor_tensor(rstd2[:, 0:1], moments2[:, 1:2], eps[:, :], ALU.add).then_inc(eps2_added, 1)
                    pool.wait_ge(eps2_added, out.next)
                    after(pool, x2_done, out.i)
                    pool.tensor_tensor(rstd2[:, 1:2], rstd2[:, 0:1], minus_half[:, :], ALU.pow).then_inc(rstd2_done, 1)
                    pool.wait_ge(rstd2_done, out.next)

            steps(pool, body)

        @block.scalar
        def _(act):
            def body(norm, fit, proj, score, out, route):
                if fit.yes:
                    act.wait_ge(quant_done, fit.next)
                    after(act, xq_done, fit.i - 1)
                    act.activation(z[fit.b][:, :], y[fit.b][:, :], ACT.Copy, bias=ROUNDER, scale=quant[fit.b][:, 0:1]).then_inc(z_done, 1)
                if route.yes:
                    act.wait_ge(x2_turned, route.next)
                    after(act, logits_done, route.i)
                    act.activation(x2T[:, :, :], bank[1][:, :].rearrange("p (k t) -> p k t", k=KT), ACT.Copy).then_inc(x2T_done, 1)
                if proj.yes:
                    act.wait_ge(v_done, proj.next)
                    act.wait_ge(v_scaled, proj.next)
                    after(act, heads_done, (proj.i - 1) * GROUPS)
                    act.activation(VX[proj.b][:, :, 0:DH], bank[3][:, :].rearrange("p (h d) -> p h d", h=HEADS), ACT.Copy,
                                   scale=v_scale[proj.b][:, 0:1]).then_inc(V_done, 1)
                if out.yes:
                    act.wait_ge(quant2_done, out.next)
                    after(act, aq_done, out.i)
                    act.activation(z2[:, :], attn[:, :], ACT.Copy, bias=ROUNDER, scale=quant2[:, 0:1]).then_inc(z2_done, 1)
                if proj.yes:
                    act.wait_ge(K_scaled, proj.next)
                    after(act, scores_done, (proj.i - 1) * GROUPS)
                    for j in (0, 2):
                        at = slice(DH * j, DH * (j + 1))
                        act.activation(KTx[proj.b][at, :, j, :], K_T[at, :, :], ACT.Copy).then_inc(KTx_even, 1)
                if out.yes:
                    act.wait_ge(aq_turned, out.next)
                    after(act, projected, out.i)
                    act.activation(aqT[:, :, :], bank[0].bitcast(BF16)[:, 0:D].rearrange("p (k t) -> p k t", k=KT), ACT.Copy).then_inc(aqT_done, 1)
                if score.yes:
                    act.wait_ge(neg_turned, score.next)
                    after(act, shifted, score.i * GROUPS)
                    act.activation(negmax_t[:, :], bank[1][:, 0:P], ACT.Copy).then_inc(neg_t_done, 1)
                    for n in range(2):
                        act.wait_ge(shifted, score.i * GROUPS + 2 * n + 2)
                        after(act, prob_turned, score.i * GROUPS)
                        act.activation(prob[:, 2 * n:2 * n + 2, :], S[:, 2 * n:2 * n + 2, :], ACT.Exp).then_inc(exp_done, 1)
                if route.yes:
                    act.wait_ge(neg_logit_done, route.next)
                    after(act, gate_done, route.i)
                    act.activation(e_logit[:, :], bank[3][:, 0:EXPERTS], ACT.Exp, bias=neg_logit[:, 0:1], accum_out=e_sum[:, 0:1]).then_inc(e_done, 1)
                if score.yes:
                    for j in range(GROUPS):
                        act.wait_ge(prob_turned, score.i * GROUPS + j + 1)
                        after(act, heads_done, score.i * GROUPS)
                        act.activation(probT[:, j, :], bank[PROBS_BANK[j]][:, :], ACT.Copy).then_inc(probT_done, 1)
                if fit.yes:
                    act.wait_ge(xq_turned, fit.next)
                    after(act, v_done, fit.i - 1)
                    act.activation(xqT[fit.b][:, :, :], bank[0].bitcast(BF16)[:, 0:D].rearrange("p (k t) -> p k t", k=KT), ACT.Copy).then_inc(xqT_done, 1)
                    act.wait_ge(spread_done, fit.next)
                    after(act, K_scaled, fit.i)
                    act.activation(scale_bc[:, :], bank[3][:, 0:T], ACT.Copy).then_inc(scale_bc_done, 1)

            steps(act, body)

        @block.vector
        def _(dve):
            dve.tensor_scalar(qk_scale[:, :], w_scale[:, 0:1], w_scale[:, 1:2], DH**-0.5, ALU.mult, ALU.mult).then_inc(const, 1)
            dve.memset(carried_b[:, :], 0.0).then_inc(const, 1)
            dve.memset(negmax[:, 2 * HEADS:P].bitcast(F32), 0.0).then_inc(const, 1)
            dve.wait_ge(const, 11)

            carriers = (residual_done, stats2_done, rows_scaled, stats_done, gate_done, top_v_done)

            def carry(semaphore, value):
                c = carriers.index(semaphore)
                dve.wait_ge(semaphore, value)
                dve.tensor_copy(carried[:, c:c + 1], carried_b[:, :])

            def body(norm, fit, proj, score, out, route):
                def row_maxima(j):
                    dve.wait_ge(scores_done, score.i * GROUPS + j + 1)
                    dve.tensor_reduce(rowmax[:, j * PER_GROUP:(j + 1) * PER_GROUP], S[:, j, :].rearrange("p (m t) -> p m t", m=PER_GROUP),
                                      X_AXIS, ALU.max).then_inc(max_done, 1)

                if out.yes:
                    dve.wait_ge(heads_done, out.next * GROUPS)
                    dve.reciprocal(inv_sum[:, :, :], S[:, :, 0:PER_GROUP * (DH + 1)].rearrange("p j (m d) -> p j m d", m=PER_GROUP)[:, :, :, DH]).then_inc(inv_done, 1)
                    dve.wait_ge(inv_done, out.next)
                    after(dve, z2_done, out.i)
                    heads = attn[:, :].rearrange("p (j m d) -> p j m d", j=GROUPS, m=PER_GROUP)
                    found = S[:, :, 0:PER_GROUP * (DH + 1)].rearrange("p j (m d) -> p j m d", m=PER_GROUP)[:, :, :, 0:DH]
                    dve.tensor_tensor(heads, found, inv_sum[:, :, :].unsqueeze(3).to_broadcast([P, GROUPS, PER_GROUP, DH]), ALU.mult).then_inc(attn_done, 1)
                bc = scale_bc[:, :].unsqueeze(1).to_broadcast([P, KT, T])
                if proj.yes:
                    dve.wait_ge(scale_bc_done, proj.next)
                    dve.wait_ge(q_done, proj.next)
                    dve.scalar_tensor_tensor(out=QT[proj.b][:, :, :], in0=bank[0][:, :].rearrange("p (k t) -> p k t", k=KT), scalar=qk_scale[:, 0:1],
                                             in1=bc, op0=ALU.mult, op1=ALU.mult).then_inc(QT_done, 1)
                if out.yes:
                    dve.wait_ge(attn_done, out.next)
                    dve.tensor_reduce(absmax2[:, :], attn[:, :], X_AXIS, ALU.max, apply_absolute_value=True).then_inc(absmax2_done, 1)
                if out.yes:
                    dve.wait_ge(absmax2_done, out.next)
                    dve.tensor_scalar(dequant2[:, :], absmax2[:, :], QUANT_MIN, 1.0 / QMAX, ALU.max, ALU.mult).then_inc(dequant2_done, 1)
                if out.yes:
                    dve.wait_ge(dequant2_done, out.next)
                    dve.reciprocal(quant2[:, :], dequant2[:, :]).then_inc(quant2_done, 1)
                    after(dve, residual_done, out.i)
                    dve.tensor_scalar(o_scale[:, :], dequant2[:, :], w_scale[:, 3:4], None, ALU.mult).then_inc(o_scaled, 1)
                if proj.yes:
                    after(dve, KTx_even, proj.i * 2)
                    after(dve, KTx_odd, proj.i * 2)
                    dve.wait_ge(k_done, proj.next)
                    dve.tensor_tensor(K_T[:, :, :], bank[2][:, :].rearrange("p (k t) -> p k t", k=KT), bc, ALU.mult).then_inc(K_scaled, 1)
                if score.yes:
                    row_maxima(0)
                if score.yes:
                    row_maxima(1)
                if out.yes:
                    dve.wait_ge(z2_done, out.next)
                    dve.tensor_scalar(aq[:, :], z2[:, :], -ROUNDER, None, ALU.add).then_inc(aq_done, 1)
                if score.yes:
                    row_maxima(2)
                    row_maxima(3)
                    dve.wait_ge(max_done, score.next * GROUPS)
                    dve.tensor_scalar(negmax[:, 0:HEADS], rowmax[:, :], -1.0, None, ALU.mult).then_inc(neg_hi, 1)
                    dve.wait_ge(neg_hi, score.next)
                    dve.scalar_tensor_tensor(out=negmax[:, HEADS:2 * HEADS], in0=rowmax[:, :], scalar=-1.0, in1=negmax[:, 0:HEADS].bitcast(F32),
                                             op0=ALU.mult, op1=ALU.subtract).then_inc(neg_lo, 1)
                if norm.yes:
                    carry(rows_scaled, norm.next)
                    dve.bn_stats(stats[:, :], row(H, norm.i)).then_inc(stats_done, 1)
                if route.yes:
                    dve.wait_ge(logits_done, route.next)
                    dve.tensor_reduce(neg_logit[:, :], bank[3][:, 0:EXPERTS], X_AXIS, ALU.max, negate=True).then_inc(neg_logit_done, 1)
                if norm.yes:
                    carry(stats_done, norm.next)
                    dve.bn_aggr(moments[norm.b][:, :], stats[:, :]).then_inc(moments_done, 1)
                if fit.yes:
                    dve.wait_ge(z_done, fit.next)
                    after(dve, xq_turned, fit.i - 1)
                    dve.tensor_scalar(xq[fit.b][:, :], z[fit.b][:, :], -ROUNDER, None, ALU.add).then_inc(xq_done, 1)
                    dve.wait_ge(dequant_done, fit.next)
                    after(dve, V_done, fit.i - 1)
                    dve.tensor_scalar(v_scale[fit.b][:, :], dequant[fit.b][:, :], w_scale[:, 2:3], None, ALU.mult).then_inc(v_scaled, 1)
                if out.yes:
                    dve.wait_ge(projected, out.next)
                    dve.scalar_tensor_tensor(out=row(H, out.i), in0=bank[2][:, :], scalar=o_scale[:, 0:1], in1=row(H, out.i),
                                             op0=ALU.mult, op1=ALU.add).then_inc(residual_done, 1)
                if out.yes:
                    carry(residual_done, out.next)
                    dve.bn_stats(stats2[:, :], row(H, out.i)).then_inc(stats2_done, 1)
                if norm.yes:
                    dve.wait_ge(rstd_done, norm.next)
                    after(dve, z_done, norm.i - 1)
                    dve.tensor_scalar(y[norm.b][:, :], row(H, norm.i), moments[norm.b][:, 0:1], rstd[norm.b][:, 1:2], ALU.subtract, ALU.mult).then_inc(y_done, 1)
                if out.yes:
                    carry(stats2_done, out.next)
                    dve.bn_aggr(moments2[:, :], stats2[:, :]).then_inc(moments2_done, 1)
                if norm.yes:
                    dve.wait_ge(y_done, norm.next)
                    dve.tensor_reduce(absmax[:, :], y[norm.b][:, :], X_AXIS, ALU.max, apply_absolute_value=True).then_inc(absmax_done, 1)
                    dve.wait_ge(absmax_done, norm.next)
                    after(dve, diag_done, norm.i - 1)
                    dve.tensor_scalar(dequant[norm.b][:, :], absmax[:, :], QUANT_MIN, 1.0 / QMAX, ALU.max, ALU.mult).then_inc(dequant_done, 1)
                    dve.wait_ge(dequant_done, norm.next)
                    dve.reciprocal(quant[norm.b][:, :], dequant[norm.b][:, :]).then_inc(quant_done, 1)
                if out.yes:
                    dve.wait_ge(rstd2_done, out.next)
                    after(dve, x2_out[out.b], (out.i // 2) * 16 if isinstance(out.i, int) else (out.i - out.b) * 8)
                    dve.tensor_scalar(x2[out.b][:, :], row(H, out.i), moments2[:, 0:1], rstd2[:, 1:2], ALU.subtract, ALU.mult).then_inc(x2_done, 1)
                if route.yes:
                    dve.wait_ge(e_done, route.next)
                    dve.reciprocal(e_inv[:, :], e_sum[:, :]).then_inc(e_inv_done, 1)
                    dve.wait_ge(e_inv_done, route.next)
                    dve.tensor_scalar(gate[:, :], e_logit[:, :], e_inv[:, 0:1], None, ALU.mult).then_inc(gate_done, 1)
                    carry(gate_done, route.next)
                    dve.max(top_v[:, :], gate[:, :]).then_inc(top_v_done, 1)
                    carry(top_v_done, route.next)
                    dve.max_index(top_i[:, :], top_v[:, :], gate[:, :]).then_inc(top_i_done, 1)
                    dve.tensor_scalar(row(gate_values, route.i), top_v[:, 0:TOP], 1.0, None, ALU.mult).then_inc(gates_kept, 1)
                    dve.wait_ge(top_i_done, route.next)
                    dve.tensor_scalar(row(gate_experts, route.i), top_i[:, 0:TOP], 1.0, None, ALU.mult).then_inc(gates_kept, 1)

            steps(dve, body)
            dve.wait_ge(gates_kept, 2 * SEQS)

        @block.tensor
        def _(pe):
            pe.wait_ge(const, 11)
            pe.wait_ge(w_in, 16)
            T1, X2T_BANK, Q_BANK, V_BANK = 0, 1, 2, 3

            def turn(to, tile, identity):
                for k in range(KT):
                    mm = pe.transpose(to[:, k * T:(k + 1) * T], tile[:, k * P:(k + 1) * P], identity[:, :])
                return mm

            def body(norm, fit, proj, score, out, route):
                def project(k):
                    return pe.matmul(bank[2][:, :], aqT[:, k, :], wT[3][:, k, :], start=(k == 0), stop=(k == KT - 1))

                def shift(j):
                    pe.matmul(S[:, j, :], negmax_t[:, :], head_ones[:, j, :], start=False, stop=True, skip_group_check=True).then_inc(shifted, 1)

                def turn_probs(j):
                    for m in range(PER_GROUP):
                        mm = pe.transpose(bank[PROBS_BANK[j]][:, m * T:(m + 1) * T], prob[:, j, m * T:(m + 1) * T], ident[:, :])
                    mm.then_inc(prob_turned, 1)

                def heads(j):
                    pe.wait_ge(probT_done, score.i * GROUPS + j + 1)
                    for m in range(PER_GROUP):
                        mm = pe.matmul(S[:, j, m * (DH + 1):(m + 1) * (DH + 1)], probT[:, j, m * T:(m + 1) * T],
                                       VX[score.b][:, j * PER_GROUP + m, :], start=True, stop=True)
                    mm.then_inc(heads_done, 1)

                if proj.yes:
                    pe.wait_ge(xqT_done, proj.next)
                    after(pe, probT_done, score.i * GROUPS)
                    after(pe, K_scaled, proj.i)
                    for which, to, done in ((0, 0, q_done), (1, 2, k_done)):
                        for m in range(KT):
                            for k in range(KT):
                                mm = pe.matmul(bank[to][:, m * T:(m + 1) * T], wT[which][:, k, m * P:(m + 1) * P], xqT[proj.b][:, k, :],
                                               start=(k == 0), stop=(k == KT - 1))
                        mm.then_inc(done, 1)
                if route.yes:
                    pe.wait_ge(x2_done, route.next)
                    turn(bank[1], x2[route.b], ident).then_inc(x2_turned, 1)
                if proj.yes:
                    pe.wait_ge(scale_bc_done, proj.next)
                    for k in range(KT):
                        mm = pe.matmul(bank[3][:, :], xqT[proj.b][:, k, :], wT[2][:, k, :], start=(k == 0), stop=(k == KT - 1))
                    mm.then_inc(v_done, 1)
                if score.yes:
                    pe.wait_ge(QT_done, score.next)
                    pe.wait_ge(KTx_even, score.next * 2)
                    pe.wait_ge(KTx_odd, score.next * 2)
                    after(pe, attn_done, score.i)
                    for j in range(GROUPS):
                        pe.matmul(S[:, j, :], QT[score.b][:, j, :], KTx[score.b][:, j, :, :].rearrange("p j t -> p (j t)"),
                                  start=True, stop=True, skip_group_check=True).then_inc(scores_done, 1)
                if out.yes:
                    pe.wait_ge(aq_done, out.next)
                    if proj.yes:
                        pe.wait_ge(QT_done, proj.next)
                    turn(bank[0].bitcast(BF16), aq, ident_b).then_inc(aq_turned, 1)
                if route.yes:
                    pe.wait_ge(x2T_done, route.next)
                    if proj.yes:
                        pe.wait_ge(V_done, proj.next)
                    after(pe, e_done, route.i)
                    for k in range(KT):
                        mm = pe.matmul(bank[3][:, 0:EXPERTS], x2T[:, k, :], wr[:, k, :], start=(k == 0), stop=(k == KT - 1))
                    mm.then_inc(logits_done, 1)
                if score.yes:
                    pe.wait_ge(neg_lo, score.next)
                    if route.yes:
                        pe.wait_ge(x2T_done, route.next)
                    pe.transpose(bank[1][:, 0:P], negmax[:, :].bitcast(F32), ident[:, :]).then_inc(neg_turned, 1)
                if out.yes:
                    pe.wait_ge(aqT_done, out.next)
                    if proj.yes:
                        pe.wait_ge(K_scaled, proj.next)
                    project(0)
                    project(1)
                if score.yes:
                    pe.wait_ge(neg_t_done, score.next)
                    shift(0)
                    shift(1)
                if out.yes:
                    project(2)
                    project(3).then_inc(projected, 1)
                if score.yes:
                    shift(2)
                    shift(3)
                if score.yes:
                    pe.wait_ge(exp_done, score.i * 2 + 1)
                    turn_probs(0)
                    turn_probs(1)
                    pe.wait_ge(exp_done, score.i * 2 + 2)
                    if out.yes:
                        pe.wait_ge(residual_done, out.next)
                    elif proj.yes:
                        pe.wait_ge(K_scaled, proj.next)
                    turn_probs(2)
                    if proj.yes:
                        pe.wait_ge(V_done, proj.i)
                    heads(0)
                    turn_probs(3)
                    heads(1)
                    heads(2)
                if fit.yes:
                    pe.wait_ge(xq_done, fit.next)
                    if proj.yes:
                        pe.wait_ge(QT_done, proj.next)
                    turn(bank[0].bitcast(BF16), xq[fit.b], ident_b).then_inc(xq_turned, 1)
                    pe.wait_ge(diag_done, fit.next)
                    if proj.yes:
                        pe.wait_ge(V_done, proj.next)
                    if route.yes:
                        pe.wait_ge(e_done, route.next)
                    pe.matmul(bank[3][:, 0:T], ones[:, :], diag[fit.b][:, :], start=True, stop=True).then_inc(spread_done, 1)
                if score.yes:
                    heads(3)

            steps(pe, body)


ROUTED_F = 352
F_TILES = ((0, 128), (128, 128), (256, 96))
UP_COLS = KT * 2 * ROUTED_F
DOWN_COLS = len(F_TILES) * D
PACKED = UP_COLS + DOWN_COLS
PIECES = ((0, UP_COLS // 2), (UP_COLS // 2, UP_COLS), (UP_COLS, PACKED))
BLOCK = 2 * P
TOKENS = SEQS * T
SHARED_BLOCKS = TOKENS // BLOCK
ROUTED_BLOCKS = TOP * TOKENS // BLOCK + EXPERTS - 1
SLOT_TILES = ROUTED_BLOCKS * BLOCK // P


def experts(nc, packed, x2_dram, slot_token, y_dram, out, H, ident, ones, gate_values, gate_experts):
    with ExitStack() as ctx:
        def sb(name, shape, dt=F32):
            return ctx.enter_context(nc.sbuf_tensor(name, shape, dt))

        def ps(name, shape, dt=F32):
            return ctx.enter_context(nc.psum_tensor(name, shape, dt))

        def sem(name):
            return ctx.enter_context(nc.semaphore(name))

        w_stage = sb("w_stage", [P, PACKED])
        w_hi = [sb(f"w_hi{i}", [P, PACKED], F32R) for i in range(2)]
        w_lo = [sb(f"w_lo{i}", [P, PACKED], F32R) for i in range(2)]
        xr = [sb(f"xr{i}", [P, 2, D]) for i in range(2)]
        xT_hi = [sb(f"xT_hi{i}", [P, KT, BLOCK], F32R) for i in range(2)]
        xT_lo = [sb(f"xT_lo{i}", [P, KT, BLOCK], F32R) for i in range(2)]
        act_g = sb("act_g", [P, 3, BLOCK])
        h = sb("h", [P, 3, BLOCK])
        h_hi = [sb(f"h_hi{i}", [P, 3, BLOCK], F32R) for i in range(2)]
        h_lo = [sb(f"h_lo{i}", [P, 3, BLOCK], F32R) for i in range(2)]
        y = sb("y_rows", [P, 2, D])
        comb = [sb(f"comb{i}", [P, TOP, D]) for i in range(2)]
        slot_i = sb("slot_i", [P, TOP * SEQS], I32)
        table_i = sb("table_i", [P, TOP * SEQS], I32)
        token_i = sb("token_i", [P, SEQS], I32)
        slot_tokens = sb("slot_tokens", [P, SLOT_TILES], I32)
        block_expert = sb("block_expert", [P, ROUTED_BLOCKS], I32)

        def early(tile, start, a, b, dt=F32):
            v = tile[:, :] if len(tile.shape) == 2 else tile[:, :, :].rearrange("p a b -> p (a b)")
            v = v[:, start:start + a * b]
            return (v if dt == F32 else v.bitcast(dt)).rearrange("p (a b) -> p a b", a=a)

        E, SE = EXPERTS, EXPERTS * SEQS
        expert_no = early(comb[0], 0, E, SEQS)
        hot = [early(comb[0], SE, E, SEQS), early(comb[0], 2 * SE, E, SEQS)]
        chosen = early(comb[0], 3 * SE, E, SEQS)
        before = early(comb[1], 0, E, SEQS)
        in_seq = early(comb[1], SE, E, SEQS)
        upto = early(comb[1], 2 * SE, E, SEQS)
        zeros = early(comb[1], 3 * SE, E, SEQS)
        block_no = early(y, 0, ROUTED_BLOCKS, E)
        slot_f = early(y, 512, 1, TOP * SEQS)
        tile_f = early(y, 576, 1, TOP * SEQS)
        block_f = early(y, 640, 1, ROUTED_BLOCKS)
        count = early(y, 700, 1, E)
        count_i = early(y, 708, 1, E, I32)
        blocks = early(y, 716, 1, E)
        ends = early(y, 724, 1, E)
        starts = early(y, 732, 1, E)
        tile_i = early(y, 768, 1, TOP * SEQS, I32)
        nothing = early(y, 896, 1, SLOT_TILES, I32)
        below = sb("below", [P, P])

        xT_ps = ps("xT_ps", [P, KT, BLOCK])
        up_ps = [ps(f"up_ps{j}", [P, 512]) for j in range(3)]
        down_ps = [ps(f"down_ps{j}", [P, 512]) for j in range(2)]
        route_ps = ps("route_ps", [P, 512])

        made, masked, plan, counted, blocks_known = sem("made"), sem("masked"), sem("plan"), sem("counted"), sem("blocks_known")
        table_zeroed, scattered, table_in = sem("table_zeroed"), sem("scattered"), sem("table_in")
        stage_in = [sem(f"stage_in{i}") for i in range(3)]
        w_hi_done = [sem(f"w_hi_done{i}") for i in range(3)]
        w_lo_done = [sem(f"w_lo_done{i}") for i in range(3)]
        rows_in = [sem(f"rows_in{i}") for i in range(2)]
        rows_gathered = [sem(f"rows_gathered{i}") for i in range(2)]
        x_turned, xT_hi_done, xT_lo_done = sem("x_turned"), sem("xT_hi_done"), sem("xT_lo_done")
        up_done, silu_done, h_done, h_hi_done, h_lo_done = sem("up_done"), sem("silu_done"), sem("h_done"), sem("h_hi_done"), sem("h_lo_done")
        down_done, y_taken, y_stored = sem("down_done"), sem("y_taken"), sem("y_stored")
        comb_in = [sem(f"comb_in{i}") for i in range(2)]
        combined, out_stored = sem("combined"), sem("out_stored")

        block = ctx.enter_context(nc.Block())

        B_FROM = SHARED_BLOCKS
        C_FROM = B_FROM + ROUTED_BLOCKS
        N = C_FROM + SHARED_BLOCKS
        LAST_W = ROUTED_BLOCKS + 1
        assert (C_FROM - B_FROM) % 2 == 1 and B_FROM % 2 == 0

        def w_of(n, kind):
            return 0 if kind == "A" else LAST_W if kind == "C" else n - (B_FROM - 1)

        def w_buffer(odd, kind):
            return (odd + 1) % 2 if kind == "B" else 0

        def each_block(eng, body):
            body(0, 0, "A", None, "A")
            body(1, 1, "A", "A", "A")
            with eng.Fori(0, (B_FROM - 4) // 2) as m:
                for u in range(2):
                    body(m * 2 + (2 + u), u, "A", "A", "A")
            body(B_FROM - 2, 0, "A", "A", "A")
            body(B_FROM - 1, 1, "A", "A", "B")
            body(B_FROM, 0, "B", "A", "B")
            body(B_FROM + 1, 1, "B", "B", "B")
            with eng.Fori(0, (ROUTED_BLOCKS - 5) // 2) as m:
                for u in range(2):
                    body(m * 2 + (B_FROM + 2 + u), u, "B", "B", "B")
            body(C_FROM - 3, 0, "B", "B", "B")
            body(C_FROM - 2, 1, "B", "B", "B")
            body(C_FROM - 1, 0, "B", "B", "C")
            body(C_FROM, 1, "C", "B", "C")
            with eng.Fori(0, (SHARED_BLOCKS - 2) // 2) as m:
                for u in range(2):
                    body(m * 2 + (C_FROM + 1 + u), u % 2, "C", "C", "C")
            body(N - 1, 0, "C", "C", None)

        @block.sync
        def _(sp):
            def load_weights(w, expert):
                for piece, (a, b) in enumerate(PIECES):
                    after(sp, w_lo_done[piece], w)
                    sp.dma_start(w_stage[:, a:b], packed[bass.ds(expert, 1), :, a:b].rearrange("e p c -> (e p) c")).then_inc(stage_in[piece], 16)

            def load_rows(n, odd, first):
                after(sp, x_turned, n - 1)
                for r in range(2):
                    sp.dma_start(xr[odd][:, r, :], x2_dram[bass.ds((n - first) * BLOCK + r * P, P), :]).then_inc(rows_in[odd], 16)

            def block_weights(r):
                load_weights(r + 1, sp.value_load(block_expert[0:1, bass.ds(r, 1)], min_val=0, max_val=EXPERTS - 1))

            def store_rows(r):
                sp.wait_ge(y_taken, (r + B_FROM + 1) * 2)
                sp.dma_start(y_dram[bass.ds(r * BLOCK, BLOCK), :].rearrange("(a p) d -> p a d", p=P), y[:, :, :]).then_inc(y_stored, 16)

            load_rows(0, 0, 0)
            load_weights(0, EXPERTS)
            load_rows(1, 1, 0)
            sp.wait_ge(made, 5)
            sp.dma_start(slot_token.rearrange("(p c) x -> p (c x)", p=P), nothing[:, 0, :]).then_inc(table_zeroed, 16)
            sp.wait_ge(blocks_known, 1)
            block_weights(0)
            with sp.Fori(0, (SHARED_BLOCKS - 2) // 2) as m:
                for u in range(2):
                    load_rows(m * 2 + (2 + u), u, 0)
            for r in range(1, 3):
                block_weights(r)
            with sp.Fori(0, ROUTED_BLOCKS - 3) as r:
                block_weights(r + 3)
                store_rows(r)
            load_rows(C_FROM, C_FROM % 2, C_FROM)
            load_weights(LAST_W, EXPERTS + 1)
            store_rows(ROUTED_BLOCKS - 3)
            load_rows(C_FROM + 1, 1 - C_FROM % 2, C_FROM)
            store_rows(ROUTED_BLOCKS - 2)
            store_rows(ROUTED_BLOCKS - 1)
            with sp.Fori(0, (SHARED_BLOCKS - 2) // 2) as m:
                for u in range(2):
                    load_rows(m * 2 + (C_FROM + 2 + u), u % 2 ^ (C_FROM % 2), C_FROM)

            def store_out(i):
                sp.wait_ge(combined, (i + 1) * TOP)
                sp.dma_start(out[bass.ds(i, 1), :, :].rearrange("s p d -> (s p) d"), row(H, i)).then_inc(out_stored, 16)

            with sp.Fori(0, SEQS) as i:
                store_out(i)
            sp.wait_ge(out_stored, 16 * SEQS)
            sp.wait_ge(y_stored, 16 * ROUTED_BLOCKS)

        @block.gpsimd
        def _(pool):
            pool.iota(expert_no, pattern=[[1, E], [0, SEQS]], base=0, channel_multiplier=0, allow_small_or_imprecise_dtypes=True).then_inc(made, 1)
            pool.iota(block_no, pattern=[[1, ROUTED_BLOCKS], [0, E]], base=0, channel_multiplier=0, allow_small_or_imprecise_dtypes=True).then_inc(made, 1)
            pool.iota(token_i[:, :], pattern=[[T, SEQS]], base=0, channel_multiplier=1).then_inc(made, 1)
            pool.memset(nothing, 0).then_inc(made, 1)
            pool.memset(zeros, 0.0).then_inc(made, 1)
            pool.memset(below[:, :], 1.0).then_inc(masked, 1)
            pool.wait_ge(masked, 1)
            pool.affine_select(out=below[:, :], in_=below[:, :], compare_op=ALU.is_gt, fill=0.0, base=0, pattern=[[1, P]],
                               channel_multiplier=-1).then_inc(masked, 1)
            pool.wait_ge(table_zeroed, 16)
            pool.wait_ge(plan, 1)
            for t in range(TOP):
                for i in range(SEQS):
                    pool.indirect_dma_start(out=slot_token, out_offset=bass.IndirectOffsetOnAxis(ap=table_i[:, t * SEQS + i:t * SEQS + i + 1], axis=0),
                                            in_=token_i[:, i:i + 1], in_offset=None).then_inc(scattered, 16)
            pool.wait_ge(scattered, 16 * TOP * SEQS)
            pool.dma_start(slot_tokens[:, :], slot_token.rearrange("(p c) x -> p (c x)", p=P)).then_inc(table_in, 16)
            pool.wait_ge(table_in, 16)
            for r in range(ROUTED_BLOCKS):
                n = B_FROM + r
                pool.wait_ge(x_turned, n - 1)
                for a in range(2):
                    pool.indirect_dma_start(out=xr[n % 2][:, a, :], out_offset=None, in_=x2_dram,
                                            in_offset=bass.IndirectOffsetOnAxis(ap=slot_tokens[:, 2 * r + a:2 * r + a + 1], axis=0)).then_inc(rows_gathered[n % 2], 16)
            pool.wait_ge(y_stored, 16 * ROUTED_BLOCKS)
            for i in range(SEQS):
                after(pool, combined, (i - 1) * TOP)
                for t in range(TOP):
                    pool.indirect_dma_start(out=comb[i % 2][:, t, :], out_offset=None, in_=y_dram,
                                            in_offset=bass.IndirectOffsetOnAxis(ap=slot_i[:, t * SEQS + i:t * SEQS + i + 1], axis=0)).then_inc(comb_in[i % 2], 16)

        @block.scalar
        def _(act):
            def turned_hi(n, odd):
                act.wait_ge(x_turned, n + 1)
                after(act, up_done, (n - 1) * 3)
                act.activation(xT_hi[odd][:, :, :], xT_ps[:, :, :], ACT.Copy).then_inc(xT_hi_done, 1)

            def weights_hi(w, piece, buffer):
                a, b = PIECES[piece]
                act.wait_ge(stage_in[piece], (w + 1) * 16)
                act.activation(w_hi[buffer][:, a:b], w_stage[:, a:b], ACT.Copy).then_inc(w_hi_done[piece], 1)

            def take_y(n, kind):
                if kind == "B":
                    act.wait_ge(down_done, n * 2 + 2)
                    after(act, y_stored, (n - B_FROM) * 16)
                    act.activation(y[:, 1, :], down_ps[1][:, :], ACT.Copy).then_inc(y_taken, 1)

            def body(n, odd, kind, kind_before, kind_after):
                if kind_after:
                    turned_hi(n + 1, 1 - odd)
                new = kind_after == "B" or (kind, kind_after) == ("B", "C")
                w = w_of(n + 1, kind_after) if new else None
                buffer = w_buffer(1 - odd, kind_after) if new else None
                if new:
                    act.wait_ge(up_done, n * 3)
                    weights_hi(w, 0, buffer)
                    weights_hi(w, 1, buffer)
                for j, (_, f) in enumerate(F_TILES):
                    act.wait_ge(up_done, n * 3 + j + 1)
                    after(act, h_done, (n - 1) * 3 + j + 1)
                    act.activation(act_g[0:f, j, :], up_ps[j][0:f, 0:BLOCK], ACT.Silu).then_inc(silu_done, 1)
                    act.wait_ge(h_done, n * 3 + j + 1)
                    after(act, down_done, (n - 1) * 2)
                    act.activation(h_hi[odd][0:f, j, :], h[0:f, j, :], ACT.Copy).then_inc(h_hi_done, 1)
                take_y(n - 1, kind_before)
                if new:
                    act.wait_ge(down_done, n * 2)
                    weights_hi(w, 2, buffer)

            turned_hi(0, 0)
            for piece in range(3):
                weights_hi(0, piece, 0)
            each_block(act, body)

        @block.vector
        def _(dve):
            dve.wait_ge(made, 5)
            step = 0

            def did(ins):
                nonlocal step
                step += 1
                ins.then_inc(counted, 1)
                dve.wait_ge(counted, step)

            for t in range(TOP):
                choice = gate_experts[:, :, t].unsqueeze(1).to_broadcast([P, E, SEQS])
                did(dve.tensor_tensor(hot[t], expert_no, choice, ALU.is_equal))
            did(dve.tensor_tensor(chosen, hot[0], hot[1], ALU.add))
            dve.wait_ge(masked, 3)
            sums = route_ps[:, 0:2 * SE].rearrange("p (a e s) -> p a e s", a=2, e=E)
            did(dve.tensor_copy(before, sums[:, 0]))
            did(dve.tensor_copy(in_seq, sums[:, 1]))
            for e in range(E):
                did(dve.tensor_tensor_scan(upto[:, e, :], in_seq[:, e, :], zeros[:, e, :], 0.0, ALU.add, ALU.add))
            did(dve.tensor_scalar(count[:, 0, :], upto[:, :, SEQS - 1], float(BLOCK - 1), None, ALU.add))
            did(dve.tensor_copy(count_i[:, 0, :], count[:, 0, :]))
            did(dve.tensor_scalar(count_i[:, 0, :], count_i[:, 0, :], BLOCK.bit_length() - 1, None, ALU.logical_shift_right))
            did(dve.tensor_copy(blocks[:, 0, :], count_i[:, 0, :]))
            did(dve.tensor_tensor_scan(ends[:, 0, :], blocks[:, 0, :], zeros[:, 0, 0:E], 0.0, ALU.add, ALU.add))
            did(dve.tensor_tensor(block_no, block_no, ends[:, 0, :].unsqueeze(1).to_broadcast([P, ROUTED_BLOCKS, E]), ALU.is_ge))
            did(dve.tensor_reduce(block_f[:, 0, :], block_no, X_AXIS, ALU.add))
            did(dve.tensor_scalar(block_f[:, 0, :], block_f[:, 0, :], float(E - 1), None, ALU.min))
            dve.tensor_copy(block_expert[:, :], block_f[:, 0, :]).then_inc(blocks_known, 1)
            did(dve.tensor_tensor(starts[:, 0, :], ends[:, 0, :], blocks[:, 0, :], ALU.subtract))
            did(dve.tensor_scalar(starts[:, 0, :], starts[:, 0, :], float(BLOCK), None, ALU.mult))
            did(dve.tensor_tensor(upto, upto, in_seq, ALU.subtract))
            did(dve.tensor_tensor(upto, upto, before, ALU.add))
            did(dve.tensor_tensor(upto, upto, starts[:, 0, :].unsqueeze(2).to_broadcast([P, E, SEQS]), ALU.add))
            for t in range(TOP):
                did(dve.tensor_tensor(hot[t], hot[t], upto, ALU.mult))
                did(dve.tensor_reduce(slot_f[:, 0, t * SEQS:(t + 1) * SEQS], hot[t].rearrange("p e s -> p s e"), X_AXIS, ALU.add))
            did(dve.tensor_copy(slot_i[:, :], slot_f[:, 0, :]))
            did(dve.tensor_scalar(tile_i[:, 0, :], slot_i[:, :], P.bit_length() - 1, None, ALU.logical_shift_right))
            did(dve.tensor_copy(tile_f[:, 0, :], tile_i[:, 0, :]))
            did(dve.tensor_scalar(tile_f[:, 0, :], tile_f[:, 0, :], float(1 - P * SLOT_TILES), None, ALU.mult))
            did(dve.scalar_tensor_tensor(out=tile_f[:, 0, :], in0=slot_f[:, 0, :], scalar=float(SLOT_TILES), in1=tile_f[:, 0, :],
                                         op0=ALU.mult, op1=ALU.add))
            dve.tensor_copy(table_i[:, :], tile_f[:, 0, :]).then_inc(plan, 1)

            def turned_lo(n, odd):
                dve.wait_ge(xT_hi_done, n + 1)
                after(dve, up_done, (n - 1) * 3)
                dve.tensor_tensor(xT_lo[odd][:, :, :], xT_ps[:, :, :], xT_hi[odd][:, :, :].bitcast(F32), ALU.subtract).then_inc(xT_lo_done, 1)

            def weights_lo(w, piece, buffer):
                a, b = PIECES[piece]
                dve.wait_ge(w_hi_done[piece], w + 1)
                dve.tensor_tensor(w_lo[buffer][:, a:b], w_stage[:, a:b], w_hi[buffer][:, a:b].bitcast(F32), ALU.subtract).then_inc(w_lo_done[piece], 1)

            def take_y(n, kind):
                if kind == "B":
                    dve.wait_ge(down_done, n * 2 + 1)
                    after(dve, y_stored, (n - B_FROM) * 16)
                    dve.tensor_copy(y[:, 0, :], down_ps[0][:, :]).then_inc(y_taken, 1)
                elif kind:
                    first = 0 if kind == "A" else C_FROM
                    for r in range(2):
                        i = (n - first) * 2 + r
                        dve.wait_ge(down_done, n * 2 + r + 1)
                        dve.tensor_tensor(row(H, i), row(H, i), down_ps[r][:, :], ALU.add).then_inc(y_taken, 1)

            def combine(i, odd):
                dve.wait_ge(comb_in[odd], (i - odd) * TOP * 8 + TOP * 16)
                for t in range(TOP):
                    if t:
                        dve.wait_ge(combined, i * TOP + t)
                    dve.scalar_tensor_tensor(out=row(H, i), in0=comb[odd][:, t, :], scalar=gate_values[:, bass.ds(i, 1), t],
                                             in1=row(H, i), op0=ALU.mult, op1=ALU.add).then_inc(combined, 1)

            def body(n, odd, kind, kind_before, kind_after):
                if kind_after:
                    turned_lo(n + 1, 1 - odd)
                new = kind_after == "B" or (kind, kind_after) == ("B", "C")
                w = w_of(n + 1, kind_after) if new else None
                buffer = w_buffer(1 - odd, kind_after) if new else None
                if new:
                    weights_lo(w, 0, buffer)
                    weights_lo(w, 1, buffer)
                for j, (_, f) in enumerate(F_TILES):
                    dve.wait_ge(silu_done, n * 3 + j + 1)
                    after(dve, h_lo_done, (n - 1) * 3 + j + 1)
                    dve.tensor_tensor(h[0:f, j, :], act_g[0:f, j, :], up_ps[j][0:f, BLOCK:2 * BLOCK], ALU.mult).then_inc(h_done, 1)
                    dve.wait_ge(h_hi_done, n * 3 + j + 1)
                    dve.tensor_tensor(h_lo[odd][0:f, j, :], h[0:f, j, :], h_hi[odd][0:f, j, :].bitcast(F32), ALU.subtract).then_inc(h_lo_done, 1)
                take_y(n - 1, kind_before)
                if new:
                    weights_lo(w, 2, buffer)
                if kind == "C" and kind_before == "C":
                    dve.wait_ge(y_taken, n * 2)
                    if not isinstance(n, int) or n > C_FROM + 1:
                        for r in range(2):
                            combine((n - (C_FROM + 1)) * 2 + r, r)

            turned_lo(0, 0)
            for piece in range(3):
                weights_lo(0, piece, 0)
            each_block(dve, body)
            take_y(N - 1, "C")
            dve.wait_ge(y_taken, 2 * N)
            for i in range(SEQS - 2, SEQS):
                combine(i, i % 2)

        @block.tensor
        def _(pe):
            pe.wait_ge(masked, 2)
            pe.wait_ge(counted, 3)
            flat = chosen.rearrange("p e s -> p (e s)")
            pe.matmul(route_ps[:, 0:SE], below[:, :], flat, start=True, stop=True)
            pe.matmul(route_ps[:, SE:2 * SE], ones[:, :], flat, start=True, stop=True).then_inc(masked, 1)

            def three(out, a_hi, a_lo, b_hi, b_lo, first, last):
                pe.matmul(out, a_hi, b_hi, start=first, stop=False)
                pe.matmul(out, a_hi, b_lo, start=False, stop=False)
                return pe.matmul(out, a_lo, b_hi, start=False, stop=last)

            def up(n, odd, w, buffer):
                pe.wait_ge(xT_lo_done, n + 1)
                pe.wait_ge(w_lo_done[0], w + 1)
                pe.wait_ge(w_lo_done[1], w + 1)
                for j, (start, f) in enumerate(F_TILES):
                    after(pe, h_done, (n - 1) * 3 + j + 1)
                    for half in range(2):
                        for k in range(KT):
                            c = k * 2 * ROUTED_F + half * ROUTED_F + start
                            mm = three(up_ps[j][0:f, half * BLOCK:(half + 1) * BLOCK], w_hi[buffer][:, c:c + f], w_lo[buffer][:, c:c + f],
                                       xT_hi[odd][:, k, :], xT_lo[odd][:, k, :], k == 0, k == KT - 1)
                    mm.then_inc(up_done, 1)

            def down(n, odd, w, buffer):
                pe.wait_ge(h_lo_done, n * 3 + 3)
                pe.wait_ge(w_lo_done[2], w + 1)
                for r in range(2):
                    after(pe, y_taken, n * 2)
                    for j, (_, f) in enumerate(F_TILES):
                        c = UP_COLS + j * D
                        mm = three(down_ps[r][:, :], h_hi[odd][0:f, j, r * P:(r + 1) * P], h_lo[odd][0:f, j, r * P:(r + 1) * P],
                                   w_hi[buffer][0:f, c:c + D], w_lo[buffer][0:f, c:c + D], j == 0, j == 2)
                    mm.then_inc(down_done, 1)

            def body(n, odd, kind, kind_before, kind_after):
                if kind_after:
                    turn(n + 1, 1 - odd, kind_after)
                up(n, odd, w_of(n, kind), w_buffer(odd, kind))
                if kind_before:
                    down(n - 1, 1 - odd, w_of(n - 1, kind_before), w_buffer(1 - odd, kind_before))

            def turn(n, odd, kind):
                if kind == "A":
                    pe.wait_ge(rows_in[odd], (n - odd) * 16 + 32)
                elif kind == "B":
                    pe.wait_ge(rows_gathered[odd], (n - B_FROM - odd) * 16 + 32)
                else:
                    pe.wait_ge(rows_in[odd], (n - C_FROM - (1 - odd)) * 16 + 32 + B_FROM * 16)
                after(pe, xT_lo_done, n)
                for r in range(2):
                    for k in range(KT):
                        mm = pe.transpose(xT_ps[:, k, r * P:(r + 1) * P], xr[odd][:, r, k * P:(k + 1) * P], ident[:, :])
                mm.then_inc(x_turned, 1)

            turn(0, 0, "A")
            each_block(pe, body)
            down(N - 1, 0, LAST_W, 0)


def tower(nc, a, out):
    x2_dram = nc.dram_tensor("x2_rows", [TOKENS, D], F32, kind="Internal").ap()
    y_dram = nc.dram_tensor("slot_rows", [SLOT_TILES * P, D], F32, kind="Internal").ap()
    slot_token = nc.dram_tensor("slot_token", [SLOT_TILES * P, 1], I32, kind="Internal").ap()
    with ExitStack() as ctx:
        def sb(name, shape, dt=F32):
            return ctx.enter_context(nc.sbuf_tensor(name, shape, dt))

        H = sb("H", [P, SEQS, D])
        ident, ones = sb("ident", [P, P]), sb("ones", [P, P])
        gate_values, gate_experts = sb("gate_values", [P, SEQS, TOP]), sb("gate_experts", [P, SEQS, TOP])
        with ExitStack() as attention:
            wT = [attention.enter_context(nc.sbuf_tensor(f"wT_{n}", [P, KT, D], BF16)) for n in "qkvo"]
            w_scale = attention.enter_context(nc.sbuf_tensor("w_scale", [P, 4], F32))
            S_bc = attention.enter_context(nc.sbuf_tensor("S_bc", [P, D], F32))
            embed(nc, a["ids"], a["table"], a["table_t"], a["lora_a"], a["lora_a_t"], a["lora_b_t"], a["magnitude_t"],
                  [a["w_q_t"], a["w_k_t"], a["w_v_t"], a["w_o_t"]], H, wT, w_scale, S_bc, ident, ones)
            attend(nc, a["router_t"], x2_dram, H, wT, w_scale, S_bc, ident, ones, gate_values, gate_experts)
        experts(nc, a["packed"], x2_dram, slot_token, y_dram, out, H, ident, ones, gate_values, gate_experts)


def kernel(x, L0_tok_weight, L0_tok_lora_A, L0_tok_lora_B, L0_tok_magnitude, L0_attn_w_q, L0_attn_w_k, L0_attn_w_v, L0_attn_w_o,
           L0_ffn_Wr, L0_ffn_Wg, L0_ffn_Wu, L0_ffn_Wd, L0_ffn_Wsg, L0_ffn_Wsu, L0_ffn_Wsd):
    import numpy as np
    import concourse.bacc as bacc
    from concourse.bass_utils import run_bass_kernel_spmd

    def turned(w):
        return np.ascontiguousarray(np.asarray(w).T)

    gates = np.concatenate([L0_ffn_Wg, np.asarray(L0_ffn_Wsg).reshape(2, ROUTED_F, D)])
    ups = np.concatenate([L0_ffn_Wu, np.asarray(L0_ffn_Wsu).reshape(2, ROUTED_F, D)])
    downs = np.concatenate([np.asarray(L0_ffn_Wd).transpose(0, 2, 1), turned(L0_ffn_Wsd).reshape(2, ROUTED_F, D)])
    n = len(gates)
    packed = np.zeros((n, P, PACKED), gates.dtype)
    both = packed[:, :, :UP_COLS].reshape(n, P, KT, 2, ROUTED_F)
    both[:, :, :, 0] = gates.reshape(n, ROUTED_F, KT, P).transpose(0, 3, 2, 1)
    both[:, :, :, 1] = ups.reshape(n, ROUTED_F, KT, P).transpose(0, 3, 2, 1)
    packed[:, :, :UP_COLS] = both.reshape(n, P, UP_COLS)
    for j, (start, f) in enumerate(F_TILES):
        packed[:, :f, UP_COLS + j * D:UP_COLS + (j + 1) * D] = downs[:, start:start + f]

    arrays = {
        "ids": turned(x),
        "table": np.ascontiguousarray(L0_tok_weight),
        "table_t": turned(L0_tok_weight),
        "lora_a": np.ascontiguousarray(L0_tok_lora_A),
        "lora_a_t": turned(L0_tok_lora_A),
        "lora_b_t": turned(L0_tok_lora_B),
        "magnitude_t": turned(np.asarray(L0_tok_magnitude).reshape(KT, P)),
        "w_q_t": turned(L0_attn_w_q), "w_k_t": turned(L0_attn_w_k), "w_v_t": turned(L0_attn_w_v), "w_o_t": turned(L0_attn_w_o),
        "router_t": turned(L0_ffn_Wr),
        "packed": packed,
    }
    nc = bacc.Bacc("TRN2", target_bir_lowering=False, num_devices=1)
    inputs = {name: nc.dram_tensor(name, v.shape, mybir.dt.from_np(v.dtype), kind="ExternalInput").ap() for name, v in arrays.items()}
    out = nc.dram_tensor("out", (SEQS, T, D), F32, kind="ExternalOutput").ap()
    tower(nc, inputs, out)
    result = run_bass_kernel_spmd(nc, [arrays], core_ids=[0])
    return result.results[0]["out"]
```

```python
from contextlib import ExitStack

import concourse.bass as bass
from concourse import mybir

F32 = mybir.dt.float32
F32R = mybir.dt.float32r
BF16 = mybir.dt.bfloat16
I32 = mybir.dt.int32
U32 = mybir.dt.uint32
ALU = mybir.AluOpType
ACT = mybir.ActivationFunctionType
X_AXIS = mybir.AxisListType.X

P = 128
SEQS, T = 32, 128
D = 512
KT = D // P
HEADS, DH = 16, 32
GROUPS = P // DH
PER_GROUP = HEADS // GROUPS
VOCAB, RANK = 32000, 16
LORA_SCALE = 2.0
EXPERTS, TOP = 8, 2
LN_EPS = 1e-5
QUANT_MIN = 1e-5
QMAX = 127.0
ROUNDER = 1.5 * 2.0**23

CHUNK = 1000
CHUNKS = VOCAB // CHUNK
HALF = CHUNK // 2
SEQ_GROUP = 4
assert CHUNKS == SEQS


def after(eng, semaphore, value):
    if not isinstance(value, int) or value > 0:
        eng.wait_ge(semaphore, value)


def row(tile, i):
    return tile[:, bass.ds(i, 1), :].rearrange("p a d -> p (a d)")


def embed(nc, ids, table, table_t, lora_a, lora_a_t, lora_b_t, magnitude_t, attn_ws, H, wT, w_scale, S_bc, ident, ones):
    with ExitStack() as ctx:
        def sb(name, shape, dt=F32):
            return ctx.enter_context(nc.sbuf_tensor(name, shape, dt))

        def ps(name, shape):
            return ctx.enter_context(nc.psum_tensor(name, shape, F32))

        def sem(name):
            return ctx.enter_context(nc.semaphore(name))

        ids_i = sb("ids_i", [P, SEQS], I32)
        ids_f = sb("ids_f", [P, SEQS])
        wrap = sb("wrap", [P, SEQS])
        rows_i = sb("rows_i", [P, SEQS], I32)
        a_rows = sb("a_rows", [P, SEQS, DH])
        a_group = sb("a_group", [P, P])
        a_group_t = sb("a_group_t", [P, P])
        b_rep = sb("b_rep", [P, D])
        b_f_place = sb("b_f", [P, D])
        b_f = b_f_place[0:96, :]
        diag = b_f_place[:, :].rearrange("p (k t) -> p k t", k=KT)
        b_split = sb("b_split", [96, D], F32R)
        a_f = sb("a_f", [64, 4, CHUNK])
        a_split = [sb(f"a_split{i}", [96, CHUNK], F32R) for i in range(4)]
        W = sb("W", [P, 4, KT, CHUNK])
        part = sb("part", [P, 2, KT])
        total = sb("total", [P, KT])
        root = sb("root", [P, KT])
        half = sb("half", [P, KT])
        mag = sb("mag", [P, KT])
        col_scale = sb("col_scale", [P, KT])
        w_sum = sb("w_sum", [P, 4])
        w_inv = sb("w_inv", [P, 4])
        minus_rounder = sb("minus_rounder", [P, 1])
        norm_ps = [ps(f"norm_ps{i}", [P, 2, 512]) for i in range(2)]
        lora_ps = [ps(f"lora_ps{i}", [P, 512]) for i in range(2)]
        turn_ps = ps("turn_ps", [P, 512])
        misc_ps = ps("misc_ps", [P, 512])

        ids_in, ids_step = sem("ids_in"), sem("ids_step")
        rows_zeroed, operands_zeroed, const_ready, id_zero = sem("rows_zeroed"), sem("operands_zeroed"), sem("const_ready"), sem("id_zero")
        b_in = sem("b_in")
        gathered = [sem(f"gathered{j}") for j in range(SEQ_GROUP)]
        a_in = [sem(f"a_in{i}") for i in range(4)]
        w_in = [sem(f"w_in{i}") for i in range(4)]
        attn_in = sem("attn_in")
        b_hi, b_lo, a_hi, a_lo = sem("b_hi"), sem("b_lo"), sem("a_hi"), sem("a_lo")
        normed, added, squared, part_added, lora_free = sem("normed"), sem("added"), sem("squared"), sem("part_added"), sem("lora_free")
        grouped, group_turned, group_copied, lora_done = sem("grouped"), sem("group_turned"), sem("group_copied"), sem("lora_done")
        w_abs, w_tot, w_scaled, w_step = sem("w_abs"), sem("w_tot"), sem("w_scaled"), sem("w_step")
        rooted, scaled, diagonal, spread, norm_out = sem("rooted"), sem("scaled"), sem("diagonal"), sem("spread"), sem("norm_out")

        block = ctx.enter_context(nc.Block())
        trips = CHUNKS // 4
        w_f = [H[:, SEQS - (4 - n) * KT:SEQS - (3 - n) * KT, :] for n in range(4)]
        table_t_v = table_t.rearrange("(k p) v -> p k v", p=P)

        @block.sync
        def _(sp):
            sp.dma_start(ids_i[:, :], ids).then_inc(ids_in, 16)
            sp.wait_ge(operands_zeroed, 3)
            for r in range(3):
                sp.dma_start(b_f[32 * r:32 * r + RANK, :], lora_b_t).then_inc(b_in, 16)
            for j in range(GROUPS):
                sp.dma_start(b_rep[DH * j:DH * j + RANK, :], lora_b_t).then_inc(b_in, 16)
            sp.dma_start(mag[:, :], magnitude_t).then_inc(b_in, 16)
            sp.sem_inc(squared, 4 * KT)
            sp.sem_inc(a_lo, 4)
            with sp.Fori(0, trips) as g:
                for q in range(4):
                    c = g * 4 + q
                    sp.wait_ge(a_lo, c + 1)
                    for r in range(2):
                        sp.dma_start(a_f[32 * r:32 * r + RANK, q, :], lora_a[:, bass.ds(c * CHUNK, CHUNK)]).then_inc(a_in[q], 16)
                    sp.wait_ge(squared, (c + 1) * KT)
                    sp.dma_start(W[:, q, :, :], table_t_v[:, :, bass.ds(c * CHUNK, CHUNK)]).then_inc(w_in[q], 16)

        @block.gpsimd
        def _(pool):
            pool.memset(ident[:, :], 0.0).then_inc(id_zero, 1)
            pool.memset(ones[:, :], 1.0).then_inc(const_ready, 1)
            pool.memset(a_rows[:, :, :], 0.0).then_inc(rows_zeroed, 1)
            pool.memset(half[:, :], 0.5).then_inc(const_ready, 1)
            pool.memset(minus_rounder[:, :], -ROUNDER).then_inc(const_ready, 1)
            pool.wait_ge(id_zero, 1)
            pool.affine_select(out=ident[:, :], in_=ident[:, :], compare_op=ALU.not_equal, fill=1.0, base=0,
                               pattern=[[-1, P]], channel_multiplier=1).then_inc(const_ready, 1)

            def gather(i):
                if i == SEQS - 4 * KT:
                    pool.wait_ge(w_step, 8)
                after(pool, gathered[i % SEQ_GROUP], 32 * (i // SEQ_GROUP))
                at = bass.IndirectOffsetOnAxis(ap=rows_i[:, i:i + 1], axis=0)
                pool.indirect_dma_start(out=H[:, i, :], out_offset=None, in_=table, in_offset=at).then_inc(gathered[i % SEQ_GROUP], 16)
                pool.indirect_dma_start(out=a_rows[:, i, 0:RANK], out_offset=None, in_=lora_a_t, in_offset=at).then_inc(gathered[i % SEQ_GROUP], 16)

            def low_part(c):
                pool.wait_ge(a_hi, c + 1)
                pool.wait_ge(a_lo, 4 + c)
                pool.tensor_tensor(a_split[c % 4][64:96, :], a_f[0:32, c % 4, :], a_split[c % 4][0:32, :].bitcast(F32),
                                   ALU.subtract).then_inc(a_lo, 1)

            pool.wait_ge(ids_step, 5)
            pool.wait_ge(rows_zeroed, 1)
            for i in range(SEQ_GROUP):
                gather(i)
            pool.wait_ge(const_ready, 5)
            low_part(0)
            ahead = SEQ_GROUP + 2
            for i in range(SEQ_GROUP, ahead):
                gather(i)
            for c in range(CHUNKS):
                if c + 1 < CHUNKS:
                    low_part(c + 1)
                if c + ahead < SEQS:
                    gather(c + ahead)
            pool.wait_ge(part_added, 2 + CHUNKS)
            pool.tensor_tensor(root[:, :], total[:, :], half[:, :], ALU.pow).then_inc(rooted, 1)

        @block.scalar
        def _(act):
            for n in range(4):
                act.dma_start(w_f[n], attn_ws[n].rearrange("(k p) c -> p k c", p=P)).then_inc(attn_in, 16)
            act.sem_inc(added, 2)
            act.wait_ge(attn_in, 16 * 4)
            for n in range(4):
                act.activation(wT[n][:, :, :], w_f[n], ACT.Abs, accum_out=w_sum[:, n:n + 1]).then_inc(w_abs, 1)
            act.wait_ge(b_in, 16 * 8)
            act.activation(b_split[:, :], b_f[:, :], ACT.Copy, scale=LORA_SCALE).then_inc(b_hi, 1)

            def high_part(c, g, q):
                act.wait_ge(a_in[q], (g + 1) * 32)
                after(act, normed, 2 * KT + (c - 3) * KT)
                act.activation(a_split[q][0:64, :], a_f[:, q, :], ACT.Copy).then_inc(a_hi, 1)

            def squares(c, q, first, last):
                for k in range(first, last):
                    if k == 0:
                        act.wait_ge(part_added, c + 1)
                    act.wait_ge(added, c * KT + k + 3)
                    act.activation(W[:, q, k, :], W[:, q, k, :], ACT.Square, accum_out=part[:, q % 2, k:k + 1]).then_inc(squared, 1)

            def copy_group(g):
                act.wait_ge(group_turned, g + 1)
                act.activation(a_group_t[:, :], turn_ps[:, 0:P], ACT.Copy).then_inc(group_copied, 1)

            def ternary(n):
                act.activation(w_f[n], w_f[n], ACT.Copy, bias=ROUNDER, scale=w_inv[:, n:n + 1]).then_inc(w_step, 1)
                act.wait_ge(w_step, n * 2 + 1)
                act.activation(wT[n][:, :, :], w_f[n], ACT.Sign, bias=minus_rounder[:, :]).then_inc(w_step, 1)

            def trip(g, first, last):
                for q in range(4):
                    c = g * 4 + q
                    squares(c, q, 0, 1)
                    if not (last and q >= 2):
                        high_part(c + 2, g + (q + 2) // 4, (q + 2) % 4)
                    squares(c, q, 1, KT)
                    if first:
                        ternary(q)
                    if q == 1:
                        copy_group(g)

            high_part(0, 0, 0)
            high_part(1, 0, 1)
            act.wait_ge(const_ready, 5)
            act.wait_ge(w_scaled, 2)
            trip(0, True, False)
            with act.Fori(0, trips - 2) as g:
                trip(g + 1, False, False)
            trip(trips - 1, False, True)

        @block.vector
        def _(dve):
            dve.memset(b_f[:, :], 0.0).then_inc(operands_zeroed, 1)
            dve.memset(b_rep[:, :], 0.0).then_inc(operands_zeroed, 1)
            dve.memset(a_f[:, :, :], 0.0).then_inc(operands_zeroed, 1)
            dve.memset(total[:, :], 0.0).then_inc(const_ready, 1)
            dve.sem_inc(part_added, 2)
            dve.wait_ge(ids_in, 16)
            dve.tensor_copy(ids_f[:, :], ids_i[:, :]).then_inc(ids_step, 1)
            dve.wait_ge(ids_step, 1)
            dve.tensor_scalar(wrap[:, :], ids_f[:, :], 0.0, float(VOCAB), ALU.is_lt, ALU.mult).then_inc(ids_step, 1)
            dve.wait_ge(ids_step, 2)
            dve.tensor_tensor(ids_f[:, :], ids_f[:, :], wrap[:, :], ALU.add).then_inc(ids_step, 1)
            dve.wait_ge(ids_step, 3)
            dve.tensor_scalar(ids_f[:, :], ids_f[:, :], 0.0, float(VOCAB - 1), ALU.max, ALU.min).then_inc(ids_step, 1)
            dve.wait_ge(ids_step, 4)
            dve.tensor_copy(rows_i[:, :], ids_f[:, :]).then_inc(ids_step, 1)
            dve.wait_ge(b_hi, 1)
            dve.scalar_tensor_tensor(out=b_split[32:64, :], in0=b_f[32:64, :], scalar=LORA_SCALE, in1=b_split[32:64, :].bitcast(F32),
                                     op0=ALU.mult, op1=ALU.subtract).then_inc(b_lo, 1)

            def add_products(c, g, q, k):
                if k == 0:
                    dve.wait_ge(w_in[q], (g + 1) * 16)
                dve.wait_ge(normed, 2 * KT + c * KT + k + 1)
                w = W[:, q, k, :].rearrange("p (h n) -> p h n", h=2)
                dve.tensor_tensor(w, w, norm_ps[k % 2][:, :, 0:HALF], ALU.add).then_inc(added, 1)

            def add_part(c, q):
                dve.wait_ge(squared, 4 * KT + (c + 1) * KT)
                dve.wait_ge(part_added, c + 2)
                dve.tensor_tensor(total[:, :], total[:, :], part[:, q % 2, :], ALU.add).then_inc(part_added, 1)

            def group_rows(g):
                for rows in gathered:
                    dve.wait_ge(rows, (g + 1) * 32)
                after(dve, group_turned, g)
                dve.tensor_scalar(a_group[:, :].rearrange("p (s r) -> p s r", s=SEQ_GROUP), a_rows[:, bass.ds(g * SEQ_GROUP, SEQ_GROUP), :],
                                  LORA_SCALE, None, ALU.mult).then_inc(grouped, 1)

            def add_lora(i, j):
                dve.wait_ge(lora_done, i + 1)
                dve.tensor_tensor(row(H, i), row(H, i), lora_ps[j % 2][:, :], ALU.add).then_inc(lora_free, 1)

            def trip(g, first):
                for q in range(4):
                    c = g * 4 + q
                    for k in range(KT):
                        add_products(c, g, q, k)
                        if k == 1:
                            j = (q + 1) % 4
                            if j == 0:
                                add_lora(g * 4, 0)
                            elif not first:
                                add_lora(g * 4 + j - 4, j)
                    if q == 1:
                        group_rows(g)
                    if q or not first:
                        add_part(c - 1, (q - 1) % 4)

            dve.wait_ge(const_ready, 5)
            dve.wait_ge(w_tot, 1)
            dve.tensor_scalar(w_scale[:, :], misc_ps[:, 0:4], 1.0 / (D * D), QUANT_MIN, ALU.mult, ALU.max).then_inc(w_scaled, 1)
            dve.wait_ge(w_scaled, 1)
            dve.reciprocal(w_inv[:, :], w_scale[:, :]).then_inc(w_scaled, 1)
            trip(0, True)
            with dve.Fori(0, trips - 1) as g:
                trip(g + 1, False)
            add_part(CHUNKS - 1, 3)
            for j in range(1, 4):
                add_lora(SEQS - 4 + j, j)
            dve.wait_ge(rooted, 1)
            dve.tensor_tensor(col_scale[:, :], root[:, :], mag[:, :], ALU.mult).then_inc(scaled, 1)
            dve.wait_ge(scaled, 1)
            for k in range(KT):
                dve.tensor_scalar(diag[:, k, :], ident[:, :], col_scale[:, k:k + 1], None, ALU.mult).then_inc(diagonal, 1)
            dve.wait_ge(spread, 1)
            dve.tensor_copy(S_bc[:, :], misc_ps[:, :]).then_inc(norm_out, 1)
            dve.wait_ge(norm_out, 1)

        @block.tensor
        def _(pe):
            pe.sem_inc(normed, 2 * KT)
            pe.sem_inc(lora_free, 2)
            pe.wait_ge(const_ready, 5)
            pe.wait_ge(b_lo, 1)

            def products(c, q, lora):
                pe.wait_ge(a_lo, 4 + c + 1)
                for k in range(KT):
                    pe.wait_ge(added, c * KT + k + 1)
                    for h in range(2):
                        mm = pe.matmul(norm_ps[k % 2][:, h, 0:HALF], b_split[:, k * P:(k + 1) * P],
                                       a_split[q][:, h * HALF:(h + 1) * HALF], start=True, stop=True)
                    mm.then_inc(normed, 1)
                    if k % 2 and lora:
                        lora_half(*lora, k // 2)

            def turn_group(g):
                pe.wait_ge(grouped, g + 1)
                pe.transpose(turn_ps[:, 0:P], a_group[:, :], ident[:, :]).then_inc(group_turned, 1)

            def lora_half(i, j, g, half):
                if half == 0:
                    pe.wait_ge(group_copied, g + 1)
                    pe.wait_ge(lora_free, i + 1)
                at = slice(half * D // 2, (half + 1) * D // 2)
                mm = pe.matmul(lora_ps[j % 2][:, at], a_group_t[DH * j:DH * (j + 1), :], b_rep[DH * j:DH * (j + 1), at], start=True, stop=True)
                if half:
                    mm.then_inc(lora_done, 1)

            def trip(g, first):
                for q in range(4):
                    j = (q + 2) % 4
                    lora = (g * 4 + j, j, g) if j < 2 else None if first else (g * 4 + j - 4, j, g - 1)
                    products(g * 4 + q, q, lora)
                    if q == 1:
                        turn_group(g)

            pe.wait_ge(w_abs, 4)
            pe.matmul(misc_ps[:, 0:4], ones[:, :], w_sum[:, :], start=True, stop=True).then_inc(w_tot, 1)
            trip(0, True)
            with pe.Fori(0, trips - 1) as g:
                trip(g + 1, False)
            for j in range(2, 4):
                for half in range(2):
                    lora_half(SEQS - 4 + j, j, trips - 1, half)
            for k in range(KT):
                pe.wait_ge(diagonal, k + 1)
                mm = pe.matmul(misc_ps[:, k * P:(k + 1) * P], ones[:, :], diag[:, k, :], start=(k == 0), stop=(k == KT - 1),
                               skip_group_check=True)
            mm.then_inc(spread, 1)


class Live:

    def __init__(self, step, odd, back):
        self.i = step - back
        self.b = (odd + back) % 2
        self.yes = not isinstance(self.i, int) or 0 <= self.i < SEQS
        self.next = self.i + 1


def attend(nc, packed, w_stage, router_t, x2_dram, x2T_dram, H, wT, w_scale, S_bc, ident, ones, gate_values, gate_experts):
    with ExitStack() as ctx:
        def sb(name, shape, dt=F32):
            return ctx.enter_context(nc.sbuf_tensor(name, shape, dt))

        def pair(name, shape, dt=F32):
            return [sb(f"{name}{i}", shape, dt) for i in range(2)]

        def ps(name, shape, dt=F32):
            return ctx.enter_context(nc.psum_tensor(name, shape, dt))

        def sem(name):
            return ctx.enter_context(nc.semaphore(name))

        wr = sb("wr", [P, KT, EXPERTS])
        ident_b = sb("ident_b", [P, P], BF16)
        head_ones = sb("head_ones", [P, GROUPS, PER_GROUP * T], F32R)
        eps = sb("eps", [P, 1])
        minus_half = sb("minus_half", [P, 1])
        qk_scale = sb("qk_scale", [P, 1])
        carried = sb("carried", [P, 6])
        carried_b = sb("carried_b", [P, 1])
        stats = sb("stats", [P, 6])
        moments = pair("moments", [P, 2])
        rstd = pair("rstd", [P, 2])
        y = pair("y", [P, D])
        absmax = sb("absmax", [P, 1])
        dequant = pair("dequant", [P, 1])
        quant = pair("quant", [P, 1])
        v_scale = pair("v_scale", [P, 1])
        z = pair("z", [P, D])
        xq = pair("xq", [P, D], BF16)
        xqT = pair("xqT", [P, KT, T], BF16)
        diag = pair("diag_t", [P, P])
        scale_bc = sb("scale_bc", [P, T])
        QT = pair("QT", [P, KT, T])
        K_T = sb("K_T", [P, KT, T])
        KTx = pair("KTx", [P, KT, GROUPS, T])
        VX = pair("VX", [P, HEADS, DH + 1])
        rowmax = sb("rowmax", [P, HEADS])
        negmax = sb("negmax", [P, P], F32R)
        negmax_t = sb("negmax_t", [P, P], F32R)
        prob = sb("prob", [P, GROUPS, PER_GROUP * T])
        probT = sb("probT", [P, GROUPS, PER_GROUP * T])
        inv_sum = sb("inv_sum", [P, GROUPS, PER_GROUP])
        attn = sb("attn", [P, D])
        absmax2 = sb("absmax2", [P, 1])
        dequant2 = sb("dequant2", [P, 1])
        quant2 = sb("quant2", [P, 1])
        o_scale = sb("o_scale", [P, 1])
        z2 = sb("z2", [P, D])
        aq = sb("aq", [P, D], BF16)
        aqT = sb("aqT", [P, KT, T], BF16)
        stats2 = sb("stats2", [P, 6])
        moments2 = sb("moments2", [P, 2])
        rstd2 = sb("rstd2", [P, 2])
        x2 = pair("x2", [P, D])
        x2T = pair("x2T", [P, KT, T])
        neg_logit = sb("neg_logit", [P, 1])
        e_logit = sb("e_logit", [P, EXPERTS])
        e_sum = sb("e_sum", [P, 1])
        e_inv = sb("e_inv", [P, 1])
        gate = sb("gate", [P, EXPERTS])
        top_v = sb("top_v", [P, 8])
        top_i = sb("top_i", [P, 8], U32)

        S = ps("S", [P, GROUPS, 512])
        bank = [ps(f"bank{i}", [P, 512]) for i in range(4)]

        stage_in = sem("first_stage_in")
        w_in, pool_const, dve_const = sem("wr_in"), sem("pool_const"), sem("dve_const")
        names = ("rows_scaled stats_done moments_done eps_added rstd_done y_done absmax_done dequant_done quant_done v_scaled z_done xq_done"
                 " diag_done xq_turned xqT_done spread_done scale_bc_done q_done QT_done k_done K_scaled KTx_even KTx_odd v_done V_done"
                 " scores_done max_done neg_hi neg_lo neg_turned neg_t_done shifted exp_done prob_turned probT_done heads_done"
                 " inv_done attn_done absmax2_done dequant2_done quant2_done o_scaled z2_done aq_done aq_turned aqT_done projected residual_done"
                 " stats2_done moments2_done eps2_added rstd2_done x2_done x2_turned x2T_done logits_done neg_logit_done e_done e_inv_done"
                 " gate_done top_v_done top_i_done gates_kept").split()
        s = {n: sem(n) for n in names}
        x2_out = [sem(f"x2_out{i}") for i in range(2)]
        x2T_out = [sem(f"x2T_out{i}") for i in range(2)]
        (rows_scaled, stats_done, moments_done, eps_added, rstd_done, y_done, absmax_done, dequant_done, quant_done, v_scaled, z_done, xq_done,
         diag_done, xq_turned, xqT_done, spread_done, scale_bc_done, q_done, QT_done, k_done, K_scaled, KTx_even, KTx_odd, v_done, V_done,
         scores_done, max_done, neg_hi, neg_lo, neg_turned, neg_t_done, shifted, exp_done, prob_turned, probT_done, heads_done,
         inv_done, attn_done, absmax2_done, dequant2_done, quant2_done, o_scaled, z2_done, aq_done, aq_turned, aqT_done, projected, residual_done,
         stats2_done, moments2_done, eps2_added, rstd2_done, x2_done, x2_turned, x2T_done, logits_done, neg_logit_done, e_done, e_inv_done,
         gate_done, top_v_done, top_i_done, gates_kept) = s.values()

        block = ctx.enter_context(nc.Block())

        FIRST, LAST = -2, SEQS + 2
        LOOP_FROM, LOOP_TO = 6, SEQS - 2

        PROBS_BANK = (1, 0, 2, 1)

        def steps(eng, body):
            def run(k, odd):
                body(Live(k, odd, -2), Live(k, odd, -1), Live(k, odd, 0), Live(k, odd, 1), Live(k, odd, 2), Live(k, odd, 3))
            for k in range(FIRST, LOOP_FROM):
                run(k, k % 2)
            with eng.Fori(0, (LOOP_TO - LOOP_FROM) // 2) as pair_of_steps:
                for u in range(2):
                    run(pair_of_steps * 2 + (LOOP_FROM + u), (LOOP_FROM + u) % 2)
            for k in range(LOOP_TO, LAST + 1):
                run(k, k % 2)

        @block.sync
        def _(sp):
            sp.dma_start(w_stage[:, :], packed[EXPERTS]).then_inc(stage_in, 16)
            sp.dma_start(wr[:, :, :], router_t.rearrange("(k p) e -> p k e", p=P)).then_inc(w_in, 16)

            def body(norm, fit, proj, score, out, route):
                if route.yes:
                    sp.wait_ge(x2_done, route.next)
                    sp.dma_start(x2_dram[bass.ds(route.i * T, T), :], x2[route.b][:, :]).then_inc(x2_out[route.b], 16)
                    sp.wait_ge(x2T_done, route.next)
                    sp.dma_start(x2T_dram[bass.ds(route.i, 1), :, :].rearrange("s p d -> (s p) d"),
                                 x2T[route.b][:, :, :].rearrange("p k t -> p (k t)")).then_inc(x2T_out[route.b], 16)

            steps(sp, body)
            sp.wait_ge(stage_in, 16)
            for b in range(2):
                sp.wait_ge(x2_out[b], 16 * SEQS // 2)
                sp.wait_ge(x2T_out[b], 16 * SEQS // 2)

        @block.gpsimd
        def _(pool):
            pool.memset(eps[:, :], LN_EPS).then_inc(pool_const, 1)
            pool.memset(minus_half[:, :], -0.5).then_inc(pool_const, 1)
            for b in range(2):
                pool.memset(VX[b][:, :, DH:DH + 1], 1.0).then_inc(pool_const, 1)
            pool.tensor_copy(ident_b[:, :], ident[:, :]).then_inc(pool_const, 1)
            pool.wait_ge(pool_const, 5)

            def body(norm, fit, proj, score, out, route):
                if norm.yes:
                    pool.tensor_tensor(row(H, norm.i), row(H, norm.i), S_bc[:, :], ALU.mult).then_inc(rows_scaled, 1)
                    pool.wait_ge(rows_scaled, norm.next)
                if fit.yes:
                    pool.wait_ge(dequant_done, fit.next)
                    after(pool, spread_done, fit.i - 1)
                    pool.tensor_tensor(diag[fit.b][:, :], ident[:, :], dequant[fit.b][:, 0:1].to_broadcast([P, P]), ALU.mult).then_inc(diag_done, 1)
                    pool.wait_ge(diag_done, fit.next)
                if proj.yes:
                    pool.wait_ge(K_scaled, proj.next)
                    after(pool, scores_done, (proj.i - 1) * GROUPS)
                    for n, j in enumerate((1, 3)):
                        at = slice(DH * j, DH * (j + 1))
                        pool.tensor_tensor(KTx[proj.b][at, :, j, :], K_T[at, :, :], ones[at, :].unsqueeze(1).to_broadcast([DH, KT, T]),
                                           ALU.mult).then_inc(KTx_odd, 1)
                        pool.wait_ge(KTx_odd, proj.i * 2 + n + 1)
                if norm.yes:
                    pool.wait_ge(moments_done, norm.next)
                    after(pool, y_done, norm.i)
                    pool.tensor_tensor(rstd[norm.b][:, 0:1], moments[norm.b][:, 1:2], eps[:, :], ALU.add).then_inc(eps_added, 1)
                    pool.wait_ge(eps_added, norm.next)
                    pool.tensor_tensor(rstd[norm.b][:, 1:2], rstd[norm.b][:, 0:1], minus_half[:, :], ALU.pow).then_inc(rstd_done, 1)
                    pool.wait_ge(rstd_done, norm.next)
                if out.yes:
                    pool.wait_ge(moments2_done, out.next)
                    pool.tensor_tensor(rstd2[:, 0:1], moments2[:, 1:2], eps[:, :], ALU.add).then_inc(eps2_added, 1)
                    pool.wait_ge(eps2_added, out.next)
                    after(pool, x2_done, out.i)
                    pool.tensor_tensor(rstd2[:, 1:2], rstd2[:, 0:1], minus_half[:, :], ALU.pow).then_inc(rstd2_done, 1)
                    pool.wait_ge(rstd2_done, out.next)

            steps(pool, body)

        @block.scalar
        def _(act):
            def body(norm, fit, proj, score, out, route):
                if fit.yes:
                    act.wait_ge(quant_done, fit.next)
                    after(act, xq_done, fit.i - 1)
                    act.activation(z[fit.b][:, :], y[fit.b][:, :], ACT.Copy, bias=ROUNDER, scale=quant[fit.b][:, 0:1]).then_inc(z_done, 1)
                if route.yes:
                    act.wait_ge(x2_turned, route.next)
                    after(act, logits_done, route.i)
                    after(act, x2T_out[route.b], (route.i // 2) * 16 if isinstance(route.i, int) else (route.i - route.b) * 8)
                    act.activation(x2T[route.b][:, :, :], bank[1][:, :].rearrange("p (k t) -> p k t", k=KT), ACT.Copy).then_inc(x2T_done, 1)
                if proj.yes:
                    act.wait_ge(v_done, proj.next)
                    act.wait_ge(v_scaled, proj.next)
                    after(act, heads_done, (proj.i - 1) * GROUPS)
                    act.activation(VX[proj.b][:, :, 0:DH], bank[3][:, :].rearrange("p (h d) -> p h d", h=HEADS), ACT.Copy,
                                   scale=v_scale[proj.b][:, 0:1]).then_inc(V_done, 1)
                if out.yes:
                    act.wait_ge(quant2_done, out.next)
                    after(act, aq_done, out.i)
                    act.activation(z2[:, :], attn[:, :], ACT.Copy, bias=ROUNDER, scale=quant2[:, 0:1]).then_inc(z2_done, 1)
                if proj.yes:
                    act.wait_ge(K_scaled, proj.next)
                    after(act, scores_done, (proj.i - 1) * GROUPS)
                    for j in (0, 2):
                        at = slice(DH * j, DH * (j + 1))
                        act.activation(KTx[proj.b][at, :, j, :], K_T[at, :, :], ACT.Copy).then_inc(KTx_even, 1)
                if out.yes:
                    act.wait_ge(aq_turned, out.next)
                    after(act, projected, out.i)
                    act.activation(aqT[:, :, :], bank[0].bitcast(BF16)[:, 0:D].rearrange("p (k t) -> p k t", k=KT), ACT.Copy).then_inc(aqT_done, 1)
                if score.yes:
                    act.wait_ge(neg_turned, score.next)
                    after(act, shifted, score.i * GROUPS)
                    act.activation(negmax_t[:, :], bank[1][:, 0:P], ACT.Copy).then_inc(neg_t_done, 1)
                    for n in range(2):
                        act.wait_ge(shifted, score.i * GROUPS + 2 * n + 2)
                        after(act, prob_turned, score.i * GROUPS)
                        act.activation(prob[:, 2 * n:2 * n + 2, :], S[:, 2 * n:2 * n + 2, :], ACT.Exp).then_inc(exp_done, 1)
                if route.yes:
                    act.wait_ge(neg_logit_done, route.next)
                    after(act, gate_done, route.i)
                    act.activation(e_logit[:, :], bank[3][:, 0:EXPERTS], ACT.Exp, bias=neg_logit[:, 0:1], accum_out=e_sum[:, 0:1]).then_inc(e_done, 1)
                if score.yes:
                    for j in range(GROUPS):
                        act.wait_ge(prob_turned, score.i * GROUPS + j + 1)
                        after(act, heads_done, score.i * GROUPS)
                        act.activation(probT[:, j, :], bank[PROBS_BANK[j]][:, :], ACT.Copy).then_inc(probT_done, 1)
                if fit.yes:
                    act.wait_ge(xq_turned, fit.next)
                    after(act, v_done, fit.i - 1)
                    act.activation(xqT[fit.b][:, :, :], bank[0].bitcast(BF16)[:, 0:D].rearrange("p (k t) -> p k t", k=KT), ACT.Copy).then_inc(xqT_done, 1)
                    act.wait_ge(spread_done, fit.next)
                    after(act, K_scaled, fit.i)
                    act.activation(scale_bc[:, :], bank[3][:, 0:T], ACT.Copy).then_inc(scale_bc_done, 1)

            steps(act, body)

        @block.vector
        def _(dve):
            dve.tensor_scalar(qk_scale[:, :], w_scale[:, 0:1], w_scale[:, 1:2], DH**-0.5, ALU.mult, ALU.mult).then_inc(dve_const, 1)
            dve.memset(carried_b[:, :], 0.0).then_inc(dve_const, 1)
            dve.memset(negmax[:, 2 * HEADS:P].bitcast(F32), 0.0).then_inc(dve_const, 1)
            for b in range(2):
                dve.memset(KTx[b][:, :, :, :], 0.0).then_inc(dve_const, 1)
            dve.tensor_tensor(head_ones[:, :, :].rearrange("r j (m t) -> r (j m) t", m=PER_GROUP), ident[:, 0:HEADS].unsqueeze(2).to_broadcast([P, HEADS, T]),
                              ident[:, HEADS:2 * HEADS].unsqueeze(2).to_broadcast([P, HEADS, T]), ALU.add).then_inc(dve_const, 1)
            dve.wait_ge(dve_const, 6)
            dve.wait_ge(pool_const, 5)

            carriers = (residual_done, stats2_done, rows_scaled, stats_done, gate_done, top_v_done)

            def carry(semaphore, value):
                c = carriers.index(semaphore)
                dve.wait_ge(semaphore, value)
                dve.tensor_copy(carried[:, c:c + 1], carried_b[:, :])

            def body(norm, fit, proj, score, out, route):
                def row_maxima(j):
                    dve.wait_ge(scores_done, score.i * GROUPS + j + 1)
                    dve.tensor_reduce(rowmax[:, j * PER_GROUP:(j + 1) * PER_GROUP], S[:, j, :].rearrange("p (m t) -> p m t", m=PER_GROUP),
                                      X_AXIS, ALU.max).then_inc(max_done, 1)

                if out.yes:
                    dve.wait_ge(heads_done, out.next * GROUPS)
                    dve.reciprocal(inv_sum[:, :, :], S[:, :, 0:PER_GROUP * (DH + 1)].rearrange("p j (m d) -> p j m d", m=PER_GROUP)[:, :, :, DH]).then_inc(inv_done, 1)
                    dve.wait_ge(inv_done, out.next)
                    after(dve, z2_done, out.i)
                    heads = attn[:, :].rearrange("p (j m d) -> p j m d", j=GROUPS, m=PER_GROUP)
                    found = S[:, :, 0:PER_GROUP * (DH + 1)].rearrange("p j (m d) -> p j m d", m=PER_GROUP)[:, :, :, 0:DH]
                    dve.tensor_tensor(heads, found, inv_sum[:, :, :].unsqueeze(3).to_broadcast([P, GROUPS, PER_GROUP, DH]), ALU.mult).then_inc(attn_done, 1)
                bc = scale_bc[:, :].unsqueeze(1).to_broadcast([P, KT, T])
                if proj.yes:
                    dve.wait_ge(scale_bc_done, proj.next)
                    dve.wait_ge(q_done, proj.next)
                    dve.scalar_tensor_tensor(out=QT[proj.b][:, :, :], in0=bank[0][:, :].rearrange("p (k t) -> p k t", k=KT), scalar=qk_scale[:, 0:1],
                                             in1=bc, op0=ALU.mult, op1=ALU.mult).then_inc(QT_done, 1)
                if out.yes:
                    dve.wait_ge(attn_done, out.next)
                    dve.tensor_reduce(absmax2[:, :], attn[:, :], X_AXIS, ALU.max, apply_absolute_value=True).then_inc(absmax2_done, 1)
                if out.yes:
                    dve.wait_ge(absmax2_done, out.next)
                    dve.tensor_scalar(dequant2[:, :], absmax2[:, :], QUANT_MIN, 1.0 / QMAX, ALU.max, ALU.mult).then_inc(dequant2_done, 1)
                if out.yes:
                    dve.wait_ge(dequant2_done, out.next)
                    dve.reciprocal(quant2[:, :], dequant2[:, :]).then_inc(quant2_done, 1)
                    after(dve, residual_done, out.i)
                    dve.tensor_scalar(o_scale[:, :], dequant2[:, :], w_scale[:, 3:4], None, ALU.mult).then_inc(o_scaled, 1)
                if proj.yes:
                    after(dve, KTx_even, proj.i * 2)
                    after(dve, KTx_odd, proj.i * 2)
                    dve.wait_ge(k_done, proj.next)
                    dve.tensor_tensor(K_T[:, :, :], bank[2][:, :].rearrange("p (k t) -> p k t", k=KT), bc, ALU.mult).then_inc(K_scaled, 1)
                if score.yes:
                    row_maxima(0)
                if score.yes:
                    row_maxima(1)
                if out.yes:
                    dve.wait_ge(z2_done, out.next)
                    dve.tensor_scalar(aq[:, :], z2[:, :], -ROUNDER, None, ALU.add).then_inc(aq_done, 1)
                if score.yes:
                    row_maxima(2)
                    row_maxima(3)
                    dve.wait_ge(max_done, score.next * GROUPS)
                    dve.tensor_scalar(negmax[:, 0:HEADS], rowmax[:, :], -1.0, None, ALU.mult).then_inc(neg_hi, 1)
                    dve.wait_ge(neg_hi, score.next)
                    dve.scalar_tensor_tensor(out=negmax[:, HEADS:2 * HEADS], in0=rowmax[:, :], scalar=-1.0, in1=negmax[:, 0:HEADS].bitcast(F32),
                                             op0=ALU.mult, op1=ALU.subtract).then_inc(neg_lo, 1)
                if norm.yes:
                    carry(rows_scaled, norm.next)
                    dve.bn_stats(stats[:, :], row(H, norm.i)).then_inc(stats_done, 1)
                if route.yes:
                    dve.wait_ge(logits_done, route.next)
                    dve.tensor_reduce(neg_logit[:, :], bank[3][:, 0:EXPERTS], X_AXIS, ALU.max, negate=True).then_inc(neg_logit_done, 1)
                if norm.yes:
                    carry(stats_done, norm.next)
                    dve.bn_aggr(moments[norm.b][:, :], stats[:, :]).then_inc(moments_done, 1)
                if fit.yes:
                    dve.wait_ge(z_done, fit.next)
                    after(dve, xq_turned, fit.i - 1)
                    dve.tensor_scalar(xq[fit.b][:, :], z[fit.b][:, :], -ROUNDER, None, ALU.add).then_inc(xq_done, 1)
                    dve.wait_ge(dequant_done, fit.next)
                    after(dve, V_done, fit.i - 1)
                    dve.tensor_scalar(v_scale[fit.b][:, :], dequant[fit.b][:, :], w_scale[:, 2:3], None, ALU.mult).then_inc(v_scaled, 1)
                if out.yes:
                    dve.wait_ge(projected, out.next)
                    dve.scalar_tensor_tensor(out=row(H, out.i), in0=bank[2][:, :], scalar=o_scale[:, 0:1], in1=row(H, out.i),
                                             op0=ALU.mult, op1=ALU.add).then_inc(residual_done, 1)
                if out.yes:
                    carry(residual_done, out.next)
                    dve.bn_stats(stats2[:, :], row(H, out.i)).then_inc(stats2_done, 1)
                if norm.yes:
                    dve.wait_ge(rstd_done, norm.next)
                    after(dve, z_done, norm.i - 1)
                    dve.tensor_scalar(y[norm.b][:, :], row(H, norm.i), moments[norm.b][:, 0:1], rstd[norm.b][:, 1:2], ALU.subtract, ALU.mult).then_inc(y_done, 1)
                if out.yes:
                    carry(stats2_done, out.next)
                    dve.bn_aggr(moments2[:, :], stats2[:, :]).then_inc(moments2_done, 1)
                if norm.yes:
                    dve.wait_ge(y_done, norm.next)
                    dve.tensor_reduce(absmax[:, :], y[norm.b][:, :], X_AXIS, ALU.max, apply_absolute_value=True).then_inc(absmax_done, 1)
                    dve.wait_ge(absmax_done, norm.next)
                    after(dve, diag_done, norm.i - 1)
                    dve.tensor_scalar(dequant[norm.b][:, :], absmax[:, :], QUANT_MIN, 1.0 / QMAX, ALU.max, ALU.mult).then_inc(dequant_done, 1)
                    dve.wait_ge(dequant_done, norm.next)
                    dve.reciprocal(quant[norm.b][:, :], dequant[norm.b][:, :]).then_inc(quant_done, 1)
                if out.yes:
                    dve.wait_ge(rstd2_done, out.next)
                    after(dve, x2_out[out.b], (out.i // 2) * 16 if isinstance(out.i, int) else (out.i - out.b) * 8)
                    dve.tensor_scalar(x2[out.b][:, :], row(H, out.i), moments2[:, 0:1], rstd2[:, 1:2], ALU.subtract, ALU.mult).then_inc(x2_done, 1)
                if route.yes:
                    dve.wait_ge(e_done, route.next)
                    dve.reciprocal(e_inv[:, :], e_sum[:, :]).then_inc(e_inv_done, 1)
                    dve.wait_ge(e_inv_done, route.next)
                    dve.tensor_scalar(gate[:, :], e_logit[:, :], e_inv[:, 0:1], None, ALU.mult).then_inc(gate_done, 1)
                    carry(gate_done, route.next)
                    dve.max(top_v[:, :], gate[:, :]).then_inc(top_v_done, 1)
                    carry(top_v_done, route.next)
                    dve.max_index(top_i[:, :], top_v[:, :], gate[:, :]).then_inc(top_i_done, 1)
                    dve.tensor_scalar(row(gate_values, route.i), top_v[:, 0:TOP], 1.0, None, ALU.mult).then_inc(gates_kept, 1)
                    dve.wait_ge(top_i_done, route.next)
                    dve.tensor_scalar(row(gate_experts, route.i), top_i[:, 0:TOP], 1.0, None, ALU.mult).then_inc(gates_kept, 1)

            steps(dve, body)
            dve.wait_ge(gates_kept, 2 * SEQS)

        @block.tensor
        def _(pe):
            pe.wait_ge(pool_const, 5)
            pe.wait_ge(dve_const, 6)
            pe.wait_ge(w_in, 16)
            T1, X2T_BANK, Q_BANK, V_BANK = 0, 1, 2, 3

            def turn(to, tile, identity):
                for k in range(KT):
                    mm = pe.transpose(to[:, k * T:(k + 1) * T], tile[:, k * P:(k + 1) * P], identity[:, :])
                return mm

            def body(norm, fit, proj, score, out, route):
                def project(k):
                    return pe.matmul(bank[2][:, :], aqT[:, k, :], wT[3][:, k, :], start=(k == 0), stop=(k == KT - 1))

                def shift(j):
                    pe.matmul(S[:, j, :], negmax_t[:, :], head_ones[:, j, :], start=False, stop=True, skip_group_check=True).then_inc(shifted, 1)

                def turn_probs(j):
                    for m in range(PER_GROUP):
                        mm = pe.transpose(bank[PROBS_BANK[j]][:, m * T:(m + 1) * T], prob[:, j, m * T:(m + 1) * T], ident[:, :])
                    mm.then_inc(prob_turned, 1)

                def heads(j):
                    pe.wait_ge(probT_done, score.i * GROUPS + j + 1)
                    for m in range(PER_GROUP):
                        mm = pe.matmul(S[:, j, m * (DH + 1):(m + 1) * (DH + 1)], probT[:, j, m * T:(m + 1) * T],
                                       VX[score.b][:, j * PER_GROUP + m, :], start=True, stop=True)
                    mm.then_inc(heads_done, 1)

                if proj.yes:
                    pe.wait_ge(xqT_done, proj.next)
                    after(pe, probT_done, score.i * GROUPS)
                    after(pe, K_scaled, proj.i)
                    for which, to, done in ((0, 0, q_done), (1, 2, k_done)):
                        for m in range(KT):
                            for k in range(KT):
                                mm = pe.matmul(bank[to][:, m * T:(m + 1) * T], wT[which][:, k, m * P:(m + 1) * P], xqT[proj.b][:, k, :],
                                               start=(k == 0), stop=(k == KT - 1))
                        mm.then_inc(done, 1)
                if route.yes:
                    pe.wait_ge(x2_done, route.next)
                    turn(bank[1], x2[route.b], ident).then_inc(x2_turned, 1)
                if proj.yes:
                    pe.wait_ge(scale_bc_done, proj.next)
                    for k in range(KT):
                        mm = pe.matmul(bank[3][:, :], xqT[proj.b][:, k, :], wT[2][:, k, :], start=(k == 0), stop=(k == KT - 1))
                    mm.then_inc(v_done, 1)
                if score.yes:
                    pe.wait_ge(QT_done, score.next)
                    pe.wait_ge(KTx_even, score.next * 2)
                    pe.wait_ge(KTx_odd, score.next * 2)
                    after(pe, attn_done, score.i)
                    for j in range(GROUPS):
                        pe.matmul(S[:, j, :], QT[score.b][:, j, :], KTx[score.b][:, j, :, :].rearrange("p j t -> p (j t)"),
                                  start=True, stop=True, skip_group_check=True).then_inc(scores_done, 1)
                if out.yes:
                    pe.wait_ge(aq_done, out.next)
                    if proj.yes:
                        pe.wait_ge(QT_done, proj.next)
                    turn(bank[0].bitcast(BF16), aq, ident_b).then_inc(aq_turned, 1)
                if route.yes:
                    pe.wait_ge(x2T_done, route.next)
                    if proj.yes:
                        pe.wait_ge(V_done, proj.next)
                    after(pe, e_done, route.i)
                    for k in range(KT):
                        mm = pe.matmul(bank[3][:, 0:EXPERTS], x2T[route.b][:, k, :], wr[:, k, :], start=(k == 0), stop=(k == KT - 1))
                    mm.then_inc(logits_done, 1)
                if score.yes:
                    pe.wait_ge(neg_lo, score.next)
                    if route.yes:
                        pe.wait_ge(x2T_done, route.next)
                    pe.transpose(bank[1][:, 0:P], negmax[:, :].bitcast(F32), ident[:, :]).then_inc(neg_turned, 1)
                if out.yes:
                    pe.wait_ge(aqT_done, out.next)
                    if proj.yes:
                        pe.wait_ge(K_scaled, proj.next)
                    project(0)
                    project(1)
                if score.yes:
                    pe.wait_ge(neg_t_done, score.next)
                    shift(0)
                    shift(1)
                if out.yes:
                    project(2)
                    project(3).then_inc(projected, 1)
                if score.yes:
                    shift(2)
                    shift(3)
                if score.yes:
                    pe.wait_ge(exp_done, score.i * 2 + 1)
                    turn_probs(0)
                    turn_probs(1)
                    pe.wait_ge(exp_done, score.i * 2 + 2)
                    if out.yes:
                        pe.wait_ge(residual_done, out.next)
                    elif proj.yes:
                        pe.wait_ge(K_scaled, proj.next)
                    turn_probs(2)
                    if proj.yes:
                        pe.wait_ge(V_done, proj.i)
                    heads(0)
                    turn_probs(3)
                    heads(1)
                    heads(2)
                if fit.yes:
                    pe.wait_ge(xq_done, fit.next)
                    if proj.yes:
                        pe.wait_ge(QT_done, proj.next)
                    turn(bank[0].bitcast(BF16), xq[fit.b], ident_b).then_inc(xq_turned, 1)
                    pe.wait_ge(diag_done, fit.next)
                    if proj.yes:
                        pe.wait_ge(V_done, proj.next)
                    if route.yes:
                        pe.wait_ge(e_done, route.next)
                    pe.matmul(bank[3][:, 0:T], ones[:, :], diag[fit.b][:, :], start=True, stop=True).then_inc(spread_done, 1)
                if score.yes:
                    heads(3)

            steps(pe, body)


ROUTED_F = 352
F_TILES = ((0, 128), (128, 128), (256, 96))
UP_COLS = KT * 2 * ROUTED_F
DOWN_COLS = len(F_TILES) * D
PACKED = UP_COLS + DOWN_COLS
PIECES = ((0, UP_COLS // 2), (UP_COLS // 2, UP_COLS), (UP_COLS, PACKED))
BLOCK = 2 * P
TOKENS = SEQS * T
SHARED_BLOCKS = TOKENS // BLOCK
ROUTED_BLOCKS = TOP * TOKENS // BLOCK + EXPERTS - 1
SLOT_TILES = ROUTED_BLOCKS * BLOCK // P


def experts(nc, packed, w_stage, x2_dram, x2T_dram, slot_token, y_dram, out, H, ident, ones, gate_values, gate_experts):
    with ExitStack() as ctx:
        def sb(name, shape, dt=F32):
            return ctx.enter_context(nc.sbuf_tensor(name, shape, dt))

        def ps(name, shape, dt=F32):
            return ctx.enter_context(nc.psum_tensor(name, shape, dt))

        def sem(name):
            return ctx.enter_context(nc.semaphore(name))

        w_hi = [sb(f"w_hi{i}", [P, PACKED], F32R) for i in range(2)]
        w_lo = [sb(f"w_lo{i}", [P, PACKED], F32R) for i in range(2)]
        xr = [sb(f"xr{i}", [P, 2, D]) for i in range(2)]
        xT_hi = [sb(f"xT_hi{i}", [P, KT, BLOCK], F32R) for i in range(2)]
        xT_lo = [sb(f"xT_lo{i}", [P, KT, BLOCK], F32R) for i in range(2)]
        act_g = sb("act_g", [P, 3, BLOCK])
        h = sb("h", [P, 3, BLOCK])
        h_hi = [sb(f"h_hi{i}", [P, 3, BLOCK], F32R) for i in range(2)]
        h_lo = [sb(f"h_lo{i}", [P, 3, BLOCK], F32R) for i in range(2)]
        y = sb("y_rows", [P, 2, D])
        comb = [sb(f"comb{i}", [P, TOP, D]) for i in range(2)]
        slot_i = sb("slot_i", [P, TOP * SEQS], I32)
        table_i = sb("table_i", [P, TOP * SEQS], I32)
        token_i = sb("token_i", [P, SEQS], I32)
        slot_tokens = sb("slot_tokens", [P, SLOT_TILES], I32)
        block_expert = sb("block_expert", [P, ROUTED_BLOCKS], I32)

        def early(tile, start, a, b, dt=F32):
            v = tile[:, :] if len(tile.shape) == 2 else tile[:, :, :].rearrange("p a b -> p (a b)")
            v = v[:, start:start + a * b]
            return (v if dt == F32 else v.bitcast(dt)).rearrange("p (a b) -> p a b", a=a)

        E, SE = EXPERTS, EXPERTS * SEQS
        expert_no = early(comb[0], 0, E, SEQS)
        hot = [early(comb[0], SE, E, SEQS), early(comb[0], 2 * SE, E, SEQS)]
        chosen = early(comb[0], 3 * SE, E, SEQS)
        before = early(comb[1], 0, E, SEQS)
        in_seq = early(comb[1], SE, E, SEQS)
        upto = early(comb[1], 2 * SE, E, SEQS)
        zeros = early(comb[1], 3 * SE, E, SEQS)
        block_no = early(y, 0, ROUTED_BLOCKS, E)
        slot_f = early(y, 512, 1, TOP * SEQS)
        tile_f = early(y, 576, 1, TOP * SEQS)
        block_f = early(y, 640, 1, ROUTED_BLOCKS)
        count = early(y, 700, 1, E)
        count_i = early(y, 708, 1, E, I32)
        blocks = early(y, 716, 1, E)
        ends = early(y, 724, 1, E)
        starts = early(y, 732, 1, E)
        tile_i = early(y, 768, 1, TOP * SEQS, I32)
        nothing = early(y, 896, 1, SLOT_TILES, I32)
        below = sb("below", [P, P])

        xT_ps = ps("xT_ps", [P, KT, BLOCK])
        up_ps = [ps(f"up_ps{j}", [P, 512]) for j in range(3)]
        down_ps = [ps(f"down_ps{j}", [P, 512]) for j in range(2)]
        route_ps = ps("route_ps", [P, 512])

        made, masked, plan, counted, blocks_known = sem("made"), sem("masked"), sem("plan"), sem("counted"), sem("blocks_known")
        table_zeroed, scattered, table_in = sem("table_zeroed"), sem("scattered"), sem("table_in")
        stage_in = [sem(f"stage_in{i}") for i in range(3)]
        w_hi_done = [sem(f"w_hi_done{i}") for i in range(3)]
        w_lo_done = [sem(f"w_lo_done{i}") for i in range(3)]
        rows_in = [sem(f"rows_in{i}") for i in range(2)]
        rows_gathered = [sem(f"rows_gathered{i}") for i in range(2)]
        x_turned, xT_hi_done, xT_lo_done = sem("x_turned"), sem("xT_hi_done"), sem("xT_lo_done")
        up_done, silu_done, h_done, h_hi_done, h_lo_done = sem("up_done"), sem("silu_done"), sem("h_done"), sem("h_hi_done"), sem("h_lo_done")
        down_done, y_taken, y_stored = sem("down_done"), sem("y_taken"), sem("y_stored")
        comb_in = [sem(f"comb_in{i}") for i in range(2)]
        combined, out_stored = sem("combined"), sem("out_stored")

        block = ctx.enter_context(nc.Block())

        B_FROM = SHARED_BLOCKS
        C_FROM = B_FROM + ROUTED_BLOCKS
        N = C_FROM + SHARED_BLOCKS
        LAST_W = ROUTED_BLOCKS + 1
        assert (C_FROM - B_FROM) % 2 == 1 and B_FROM % 2 == 0

        def w_of(n, kind):
            return 0 if kind == "A" else LAST_W if kind == "C" else n - (B_FROM - 1)

        def split(tile):
            return tile[:, :, :].rearrange("p k (r t) -> p k r t", r=2)

        def turned(odd, kind):
            return split(xT_ps) if kind == "B" else xr[odd][:, :, :].rearrange("p r (k t) -> p k r t", k=KT)

        def w_buffer(odd, kind):
            return (odd + 1) % 2 if kind == "B" else 0

        def each_block(eng, body, after_first=None, after_second=None):
            body(0, 0, "A", None, "A")
            if after_first:
                after_first()
            body(1, 1, "A", "A", "A")
            if after_second:
                after_second()
            with eng.Fori(0, (B_FROM - 4) // 2) as m:
                for u in range(2):
                    body(m * 2 + (2 + u), u, "A", "A", "A")
            body(B_FROM - 2, 0, "A", "A", "A")
            body(B_FROM - 1, 1, "A", "A", "B")
            body(B_FROM, 0, "B", "A", "B")
            body(B_FROM + 1, 1, "B", "B", "B")
            with eng.Fori(0, (ROUTED_BLOCKS - 5) // 2) as m:
                for u in range(2):
                    body(m * 2 + (B_FROM + 2 + u), u, "B", "B", "B")
            body(C_FROM - 3, 0, "B", "B", "B")
            body(C_FROM - 2, 1, "B", "B", "B")
            body(C_FROM - 1, 0, "B", "B", "C")
            body(C_FROM, 1, "C", "B", "C")
            with eng.Fori(0, (SHARED_BLOCKS - 2) // 2) as m:
                for u in range(2):
                    body(m * 2 + (C_FROM + 1 + u), u % 2, "C", "C", "C")
            body(N - 1, 0, "C", "C", None)

        @block.sync
        def _(sp):
            def load_weights(w, expert):
                for piece, (a, b) in enumerate(PIECES):
                    after(sp, w_lo_done[piece], w)
                    sp.dma_start(w_stage[:, a:b], packed[bass.ds(expert, 1), :, a:b].rearrange("e p c -> (e p) c")).then_inc(stage_in[piece], 16)

            def load_rows(n, odd, first):
                after(sp, xT_lo_done, n - 1)
                sp.dma_start(xr[odd][:, :, :], x2T_dram[bass.ds((n - first) * 2, 2), :, :].rearrange("s p d -> p s d")).then_inc(rows_in[odd], 16)

            def block_weights(r):
                load_weights(r + 1, sp.value_load(block_expert[0:1, bass.ds(r, 1)], min_val=0, max_val=EXPERTS - 1))

            def store_rows(r):
                sp.wait_ge(y_taken, (r + B_FROM + 1) * 2)
                sp.dma_start(y_dram[bass.ds(r * BLOCK, BLOCK), :].rearrange("(a p) d -> p a d", p=P), y[:, :, :]).then_inc(y_stored, 16)

            load_rows(0, 0, 0)
            load_rows(1, 1, 0)
            sp.wait_ge(made, 5)
            sp.dma_start(slot_token.rearrange("(p c) x -> p (c x)", p=P), nothing[:, 0, :]).then_inc(table_zeroed, 16)
            load_rows(2, 0, 0)
            load_rows(3, 1, 0)
            sp.wait_ge(blocks_known, 1)
            block_weights(0)
            with sp.Fori(0, (SHARED_BLOCKS - 4) // 2) as m:
                for u in range(2):
                    load_rows(m * 2 + (4 + u), u, 0)
            for r in range(1, 3):
                block_weights(r)
            with sp.Fori(0, ROUTED_BLOCKS - 3) as r:
                block_weights(r + 3)
                store_rows(r)
            load_rows(C_FROM, C_FROM % 2, C_FROM)
            load_weights(LAST_W, EXPERTS + 1)
            store_rows(ROUTED_BLOCKS - 3)
            load_rows(C_FROM + 1, 1 - C_FROM % 2, C_FROM)
            store_rows(ROUTED_BLOCKS - 2)
            store_rows(ROUTED_BLOCKS - 1)
            with sp.Fori(0, (SHARED_BLOCKS - 2) // 2) as m:
                for u in range(2):
                    load_rows(m * 2 + (C_FROM + 2 + u), u % 2 ^ (C_FROM % 2), C_FROM)

            def store_out(i):
                sp.wait_ge(combined, (i + 1) * TOP)
                sp.dma_start(out[bass.ds(i, 1), :, :].rearrange("s p d -> (s p) d"), row(H, i)).then_inc(out_stored, 16)

            with sp.Fori(0, SEQS) as i:
                store_out(i)
            sp.wait_ge(out_stored, 16 * SEQS)
            sp.wait_ge(y_stored, 16 * ROUTED_BLOCKS)

        @block.gpsimd
        def _(pool):
            pool.iota(expert_no, pattern=[[1, E], [0, SEQS]], base=0, channel_multiplier=0, allow_small_or_imprecise_dtypes=True).then_inc(made, 1)
            pool.iota(block_no, pattern=[[1, ROUTED_BLOCKS], [0, E]], base=0, channel_multiplier=0, allow_small_or_imprecise_dtypes=True).then_inc(made, 1)
            pool.iota(token_i[:, :], pattern=[[T, SEQS]], base=0, channel_multiplier=1).then_inc(made, 1)
            pool.memset(nothing, 0).then_inc(made, 1)
            pool.memset(zeros, 0.0).then_inc(made, 1)
            pool.memset(below[:, :], 1.0).then_inc(masked, 1)
            pool.wait_ge(masked, 1)
            pool.affine_select(out=below[:, :], in_=below[:, :], compare_op=ALU.is_gt, fill=0.0, base=0, pattern=[[1, P]],
                               channel_multiplier=-1).then_inc(masked, 1)
            pool.wait_ge(table_zeroed, 16)
            pool.wait_ge(plan, 1)
            for t in range(TOP):
                for i in range(SEQS):
                    pool.indirect_dma_start(out=slot_token, out_offset=bass.IndirectOffsetOnAxis(ap=table_i[:, t * SEQS + i:t * SEQS + i + 1], axis=0),
                                            in_=token_i[:, i:i + 1], in_offset=None).then_inc(scattered, 16)
            pool.wait_ge(scattered, 16 * TOP * SEQS)
            pool.dma_start(slot_tokens[:, :], slot_token.rearrange("(p c) x -> p (c x)", p=P)).then_inc(table_in, 16)
            pool.wait_ge(table_in, 16)
            for r in range(ROUTED_BLOCKS):
                n = B_FROM + r
                if r < 2:
                    pool.wait_ge(xT_lo_done, n - 1)
                else:
                    pool.wait_ge(x_turned, r - 1)
                for a in range(2):
                    pool.indirect_dma_start(out=xr[n % 2][:, a, :], out_offset=None, in_=x2_dram,
                                            in_offset=bass.IndirectOffsetOnAxis(ap=slot_tokens[:, 2 * r + a:2 * r + a + 1], axis=0)).then_inc(rows_gathered[n % 2], 16)
            pool.wait_ge(y_stored, 16 * ROUTED_BLOCKS)
            for i in range(SEQS):
                after(pool, combined, (i - 1) * TOP)
                for t in range(TOP):
                    pool.indirect_dma_start(out=comb[i % 2][:, t, :], out_offset=None, in_=y_dram,
                                            in_offset=bass.IndirectOffsetOnAxis(ap=slot_i[:, t * SEQS + i:t * SEQS + i + 1], axis=0)).then_inc(comb_in[i % 2], 16)

        @block.scalar
        def _(act):
            def turned_hi(n, odd, kind):
                if kind == "B":
                    act.wait_ge(x_turned, n - B_FROM + 1)
                elif kind == "A":
                    act.wait_ge(rows_in[odd], (n - odd) * 8 + 16)
                else:
                    act.wait_ge(rows_in[odd], (n - C_FROM - (1 - odd)) * 8 + 16 + B_FROM * 8)
                after(act, up_done, (n - 1) * 3)
                act.activation(split(xT_hi[odd]), turned(odd, kind), ACT.Copy).then_inc(xT_hi_done, 1)

            def weights_hi(w, piece, buffer):
                a, b = PIECES[piece]
                after(act, stage_in[piece], w * 16)
                act.activation(w_hi[buffer][:, a:b], w_stage[:, a:b], ACT.Copy).then_inc(w_hi_done[piece], 1)

            def take_y(n, kind):
                if kind == "B":
                    act.wait_ge(down_done, n * 2 + 2)
                    after(act, y_stored, (n - B_FROM) * 16)
                    act.activation(y[:, 1, :], down_ps[1][:, :], ACT.Copy).then_inc(y_taken, 1)

            def body(n, odd, kind, kind_before, kind_after):
                if kind_after:
                    turned_hi(n + 1, 1 - odd, kind_after)
                new = kind_after == "B" or (kind, kind_after) == ("B", "C")
                w = w_of(n + 1, kind_after) if new else None
                buffer = w_buffer(1 - odd, kind_after) if new else None
                if new:
                    act.wait_ge(up_done, n * 3)
                    weights_hi(w, 0, buffer)
                    weights_hi(w, 1, buffer)
                for j, (_, f) in enumerate(F_TILES):
                    act.wait_ge(up_done, n * 3 + j + 1)
                    after(act, h_done, (n - 1) * 3 + j + 1)
                    act.activation(act_g[0:f, j, :], up_ps[j][0:f, 0:BLOCK], ACT.Silu).then_inc(silu_done, 1)
                    act.wait_ge(h_done, n * 3 + j + 1)
                    after(act, down_done, (n - 1) * 2)
                    act.activation(h_hi[odd][0:f, j, :], h[0:f, j, :], ACT.Copy).then_inc(h_hi_done, 1)
                take_y(n - 1, kind_before)
                if new:
                    act.wait_ge(down_done, n * 2)
                    weights_hi(w, 2, buffer)

            weights_hi(0, 0, 0)
            weights_hi(0, 1, 0)
            turned_hi(0, 0, "A")
            weights_hi(0, 2, 0)
            each_block(act, body)

        @block.vector
        def _(dve):
            def turned_lo(n, odd, kind):
                dve.wait_ge(xT_hi_done, n + 1)
                after(dve, up_done, (n - 1) * 3)
                dve.tensor_tensor(split(xT_lo[odd]), turned(odd, kind), split(xT_hi[odd]).bitcast(F32), ALU.subtract).then_inc(xT_lo_done, 1)

            def weights_lo(w, piece, buffer):
                a, b = PIECES[piece]
                dve.wait_ge(w_hi_done[piece], w + 1)
                dve.tensor_tensor(w_lo[buffer][:, a:b], w_stage[:, a:b], w_hi[buffer][:, a:b].bitcast(F32), ALU.subtract).then_inc(w_lo_done[piece], 1)

            step = 0

            def did(ins):
                nonlocal step
                step += 1
                ins.then_inc(counted, 1)
                dve.wait_ge(counted, step)

            def plan_choices():
                dve.wait_ge(made, 5)
                for t in range(TOP):
                    choice = gate_experts[:, :, t].unsqueeze(1).to_broadcast([P, E, SEQS])
                    did(dve.tensor_tensor(hot[t], expert_no, choice, ALU.is_equal))
                did(dve.tensor_tensor(chosen, hot[0], hot[1], ALU.add))

            def plan_blocks():
                dve.wait_ge(masked, 3)
                sums = route_ps[:, 0:2 * SE].rearrange("p (a e s) -> p a e s", a=2, e=E)
                did(dve.tensor_copy(before, sums[:, 0]))
                did(dve.tensor_copy(in_seq, sums[:, 1]))
                for e in range(E):
                    did(dve.tensor_tensor_scan(upto[:, e, :], in_seq[:, e, :], zeros[:, e, :], 0.0, ALU.add, ALU.add))
                did(dve.tensor_scalar(count[:, 0, :], upto[:, :, SEQS - 1], float(BLOCK - 1), None, ALU.add))
                did(dve.tensor_copy(count_i[:, 0, :], count[:, 0, :]))
                did(dve.tensor_scalar(count_i[:, 0, :], count_i[:, 0, :], BLOCK.bit_length() - 1, None, ALU.logical_shift_right))
                did(dve.tensor_copy(blocks[:, 0, :], count_i[:, 0, :]))
                did(dve.tensor_tensor_scan(ends[:, 0, :], blocks[:, 0, :], zeros[:, 0, 0:E], 0.0, ALU.add, ALU.add))
                did(dve.tensor_tensor(block_no, block_no, ends[:, 0, :].unsqueeze(1).to_broadcast([P, ROUTED_BLOCKS, E]), ALU.is_ge))
                did(dve.tensor_reduce(block_f[:, 0, :], block_no, X_AXIS, ALU.add))
                did(dve.tensor_scalar(block_f[:, 0, :], block_f[:, 0, :], float(E - 1), None, ALU.min))
                dve.tensor_copy(block_expert[:, :], block_f[:, 0, :]).then_inc(blocks_known, 1)

            def plan_slots():
                did(dve.tensor_tensor(starts[:, 0, :], ends[:, 0, :], blocks[:, 0, :], ALU.subtract))
                did(dve.tensor_scalar(starts[:, 0, :], starts[:, 0, :], float(BLOCK), None, ALU.mult))
                did(dve.tensor_tensor(upto, upto, in_seq, ALU.subtract))
                did(dve.tensor_tensor(upto, upto, before, ALU.add))
                did(dve.tensor_tensor(upto, upto, starts[:, 0, :].unsqueeze(2).to_broadcast([P, E, SEQS]), ALU.add))
                for t in range(TOP):
                    did(dve.tensor_tensor(hot[t], hot[t], upto, ALU.mult))
                    did(dve.tensor_reduce(slot_f[:, 0, t * SEQS:(t + 1) * SEQS], hot[t].rearrange("p e s -> p s e"), X_AXIS, ALU.add))
                did(dve.tensor_copy(slot_i[:, :], slot_f[:, 0, :]))
                did(dve.tensor_scalar(tile_i[:, 0, :], slot_i[:, :], P.bit_length() - 1, None, ALU.logical_shift_right))
                did(dve.tensor_copy(tile_f[:, 0, :], tile_i[:, 0, :]))
                did(dve.tensor_scalar(tile_f[:, 0, :], tile_f[:, 0, :], float(1 - P * SLOT_TILES), None, ALU.mult))
                did(dve.scalar_tensor_tensor(out=tile_f[:, 0, :], in0=slot_f[:, 0, :], scalar=float(SLOT_TILES), in1=tile_f[:, 0, :],
                                             op0=ALU.mult, op1=ALU.add))
                dve.tensor_copy(table_i[:, :], tile_f[:, 0, :]).then_inc(plan, 1)

            def take_y(n, kind):
                if kind == "B":
                    dve.wait_ge(down_done, n * 2 + 1)
                    after(dve, y_stored, (n - B_FROM) * 16)
                    dve.tensor_copy(y[:, 0, :], down_ps[0][:, :]).then_inc(y_taken, 1)
                elif kind:
                    first = 0 if kind == "A" else C_FROM
                    for r in range(2):
                        i = (n - first) * 2 + r
                        dve.wait_ge(down_done, n * 2 + r + 1)
                        dve.tensor_tensor(row(H, i), row(H, i), down_ps[r][:, :], ALU.add).then_inc(y_taken, 1)

            def combine(i, odd):
                dve.wait_ge(comb_in[odd], (i - odd) * TOP * 8 + TOP * 16)
                for t in range(TOP):
                    if t:
                        dve.wait_ge(combined, i * TOP + t)
                    dve.scalar_tensor_tensor(out=row(H, i), in0=comb[odd][:, t, :], scalar=gate_values[:, bass.ds(i, 1), t],
                                             in1=row(H, i), op0=ALU.mult, op1=ALU.add).then_inc(combined, 1)

            def body(n, odd, kind, kind_before, kind_after):
                if kind_after:
                    turned_lo(n + 1, 1 - odd, kind_after)
                new = kind_after == "B" or (kind, kind_after) == ("B", "C")
                w = w_of(n + 1, kind_after) if new else None
                buffer = w_buffer(1 - odd, kind_after) if new else None
                if new:
                    weights_lo(w, 0, buffer)
                    weights_lo(w, 1, buffer)
                for j, (_, f) in enumerate(F_TILES):
                    dve.wait_ge(silu_done, n * 3 + j + 1)
                    after(dve, h_lo_done, (n - 1) * 3 + j + 1)
                    dve.tensor_tensor(h[0:f, j, :], act_g[0:f, j, :], up_ps[j][0:f, BLOCK:2 * BLOCK], ALU.mult).then_inc(h_done, 1)
                    dve.wait_ge(h_hi_done, n * 3 + j + 1)
                    dve.tensor_tensor(h_lo[odd][0:f, j, :], h[0:f, j, :], h_hi[odd][0:f, j, :].bitcast(F32), ALU.subtract).then_inc(h_lo_done, 1)
                take_y(n - 1, kind_before)
                if new:
                    weights_lo(w, 2, buffer)
                if kind == "C" and kind_before == "C":
                    dve.wait_ge(y_taken, n * 2)
                    if not isinstance(n, int) or n > C_FROM + 1:
                        for r in range(2):
                            combine((n - (C_FROM + 1)) * 2 + r, r)

            weights_lo(0, 0, 0)
            weights_lo(0, 1, 0)
            turned_lo(0, 0, "A")
            weights_lo(0, 2, 0)
            plan_choices()
            each_block(dve, body, plan_blocks, plan_slots)
            take_y(N - 1, "C")
            dve.wait_ge(y_taken, 2 * N)
            for i in range(SEQS - 2, SEQS):
                combine(i, i % 2)

        @block.tensor
        def _(pe):
            def count_choices():
                pe.wait_ge(masked, 2)
                pe.wait_ge(counted, 3)
                flat = chosen.rearrange("p e s -> p (e s)")
                pe.matmul(route_ps[:, 0:SE], below[:, :], flat, start=True, stop=True)
                pe.matmul(route_ps[:, SE:2 * SE], ones[:, :], flat, start=True, stop=True).then_inc(masked, 1)

            def three(out, a_hi, a_lo, b_hi, b_lo, first, last):
                pe.matmul(out, a_hi, b_hi, start=first, stop=False)
                pe.matmul(out, a_hi, b_lo, start=False, stop=False)
                return pe.matmul(out, a_lo, b_hi, start=False, stop=last)

            def up(n, odd, w, buffer):
                pe.wait_ge(xT_lo_done, n + 1)
                pe.wait_ge(w_lo_done[0], w + 1)
                pe.wait_ge(w_lo_done[1], w + 1)
                for j, (start, f) in enumerate(F_TILES):
                    after(pe, h_done, (n - 1) * 3 + j + 1)
                    for half in range(2):
                        for k in range(KT):
                            c = k * 2 * ROUTED_F + half * ROUTED_F + start
                            mm = three(up_ps[j][0:f, half * BLOCK:(half + 1) * BLOCK], w_hi[buffer][:, c:c + f], w_lo[buffer][:, c:c + f],
                                       xT_hi[odd][:, k, :], xT_lo[odd][:, k, :], k == 0, k == KT - 1)
                    mm.then_inc(up_done, 1)

            def down(n, odd, w, buffer):
                pe.wait_ge(h_lo_done, n * 3 + 3)
                pe.wait_ge(w_lo_done[2], w + 1)
                for r in range(2):
                    after(pe, y_taken, n * 2)
                    for j, (_, f) in enumerate(F_TILES):
                        c = UP_COLS + j * D
                        mm = three(down_ps[r][:, :], h_hi[odd][0:f, j, r * P:(r + 1) * P], h_lo[odd][0:f, j, r * P:(r + 1) * P],
                                   w_hi[buffer][0:f, c:c + D], w_lo[buffer][0:f, c:c + D], j == 0, j == 2)
                    mm.then_inc(down_done, 1)

            def body(n, odd, kind, kind_before, kind_after):
                if kind_after == "B":
                    turn(n + 1, 1 - odd)
                up(n, odd, w_of(n, kind), w_buffer(odd, kind))
                if kind_before:
                    down(n - 1, 1 - odd, w_of(n - 1, kind_before), w_buffer(1 - odd, kind_before))

            def turn(n, odd):
                pe.wait_ge(rows_gathered[odd], (n - B_FROM - odd) * 16 + 32)
                after(pe, xT_lo_done, n)
                for r in range(2):
                    for k in range(KT):
                        mm = pe.transpose(xT_ps[:, k, r * P:(r + 1) * P], xr[odd][:, r, k * P:(k + 1) * P], ident[:, :])
                mm.then_inc(x_turned, 1)

            each_block(pe, body, count_choices)
            down(N - 1, 0, LAST_W, 0)


def tower(nc, a, out):
    x2_dram = nc.dram_tensor("x2_rows", [TOKENS, D], F32, kind="Internal").ap()
    x2T_dram = nc.dram_tensor("x2_turned", [SEQS, P, D], F32, kind="Internal").ap()
    y_dram = nc.dram_tensor("slot_rows", [SLOT_TILES * P, D], F32, kind="Internal").ap()
    slot_token = nc.dram_tensor("slot_token", [SLOT_TILES * P, 1], I32, kind="Internal").ap()
    with ExitStack() as ctx:
        def sb(name, shape, dt=F32):
            return ctx.enter_context(nc.sbuf_tensor(name, shape, dt))

        H = sb("H", [P, SEQS, D])
        ident, ones = sb("ident", [P, P]), sb("ones", [P, P])
        gate_values, gate_experts = sb("gate_values", [P, SEQS, TOP]), sb("gate_experts", [P, SEQS, TOP])
        w_stage = sb("w_stage", [P, PACKED])
        with ExitStack() as attention:
            wT = [attention.enter_context(nc.sbuf_tensor(f"wT_{n}", [P, KT, D], BF16)) for n in "qkvo"]
            w_scale = attention.enter_context(nc.sbuf_tensor("w_scale", [P, 4], F32))
            S_bc = attention.enter_context(nc.sbuf_tensor("S_bc", [P, D], F32))
            embed(nc, a["ids"], a["table"], a["table_t"], a["lora_a"], a["lora_a_t"], a["lora_b_t"], a["magnitude_t"],
                  [a["w_q_t"], a["w_k_t"], a["w_v_t"], a["w_o_t"]], H, wT, w_scale, S_bc, ident, ones)
            attend(nc, a["packed"], w_stage, a["router_t"], x2_dram, x2T_dram, H, wT, w_scale, S_bc, ident, ones, gate_values, gate_experts)
        experts(nc, a["packed"], w_stage, x2_dram, x2T_dram, slot_token, y_dram, out, H, ident, ones, gate_values, gate_experts)


def kernel(x, L0_tok_weight, L0_tok_lora_A, L0_tok_lora_B, L0_tok_magnitude, L0_attn_w_q, L0_attn_w_k, L0_attn_w_v, L0_attn_w_o,
           L0_ffn_Wr, L0_ffn_Wg, L0_ffn_Wu, L0_ffn_Wd, L0_ffn_Wsg, L0_ffn_Wsu, L0_ffn_Wsd):
    import numpy as np
    import concourse.bacc as bacc
    from concourse.bass_utils import run_bass_kernel_spmd

    def turned(w):
        return np.ascontiguousarray(np.asarray(w).T)

    gates = np.concatenate([L0_ffn_Wg, np.asarray(L0_ffn_Wsg).reshape(2, ROUTED_F, D)])
    ups = np.concatenate([L0_ffn_Wu, np.asarray(L0_ffn_Wsu).reshape(2, ROUTED_F, D)])
    downs = np.concatenate([np.asarray(L0_ffn_Wd).transpose(0, 2, 1), turned(L0_ffn_Wsd).reshape(2, ROUTED_F, D)])
    n = len(gates)
    packed = np.zeros((n, P, PACKED), gates.dtype)
    both = packed[:, :, :UP_COLS].reshape(n, P, KT, 2, ROUTED_F)
    both[:, :, :, 0] = gates.reshape(n, ROUTED_F, KT, P).transpose(0, 3, 2, 1)
    both[:, :, :, 1] = ups.reshape(n, ROUTED_F, KT, P).transpose(0, 3, 2, 1)
    packed[:, :, :UP_COLS] = both.reshape(n, P, UP_COLS)
    for j, (start, f) in enumerate(F_TILES):
        packed[:, :f, UP_COLS + j * D:UP_COLS + (j + 1) * D] = downs[:, start:start + f]

    arrays = {
        "ids": turned(x),
        "table": np.ascontiguousarray(L0_tok_weight),
        "table_t": turned(L0_tok_weight),
        "lora_a": np.ascontiguousarray(L0_tok_lora_A),
        "lora_a_t": turned(L0_tok_lora_A),
        "lora_b_t": turned(L0_tok_lora_B),
        "magnitude_t": turned(np.asarray(L0_tok_magnitude).reshape(KT, P)),
        "w_q_t": turned(L0_attn_w_q), "w_k_t": turned(L0_attn_w_k), "w_v_t": turned(L0_attn_w_v), "w_o_t": turned(L0_attn_w_o),
        "router_t": turned(L0_ffn_Wr),
        "packed": packed,
    }
    nc = bacc.Bacc("TRN2", target_bir_lowering=False, num_devices=1)
    inputs = {name: nc.dram_tensor(name, v.shape, mybir.dt.from_np(v.dtype), kind="ExternalInput").ap() for name, v in arrays.items()}
    out = nc.dram_tensor("out", (SEQS, T, D), F32, kind="ExternalOutput").ap()
    tower(nc, inputs, out)
    result = run_bass_kernel_spmd(nc, [arrays], core_ids=[0])
    return result.results[0]["out"]
```
